# Optimizing a Trainium2 kernel written in Bass

```python
import numpy as np
import jax
import jax.numpy as jnp

def _softmax(x, axis=-1):
    return jax.nn.softmax(x, axis=axis)

def _gelu(x):
    return jax.nn.gelu(x, approximate=True)

def _silu(x):
    return jax.nn.silu(x)

def _sigmoid(x):
    return jax.nn.sigmoid(x)

def _layernorm(x, axis=-1, eps=1e-05):
    m = jnp.mean(x, axis=axis, keepdims=True)
    v = jnp.var(x, axis=axis, keepdims=True)
    return (x - m) / jnp.sqrt(v + eps)

def _scatter_add(tgt, idx, src, axis=0):
    return tgt.at[idx].add(src)

def _segment_sum(src, seg, n):
    return jax.ops.segment_sum(src, seg, n)
kernel_name = 'mk_xattn_ffn_d4_seqx_r8_3eec24'

def setup_inputs(seed: int=0):
    np.random.seed(seed)
    _w = jnp.asarray

    def _rec_inputs():
        import jax
        import jax.numpy as jnp
        _rk = jax.random.key(seed)
        x = -0.000125 + 0.9999 * jax.random.normal(jax.random.fold_in(_rk, 1), (4, 256, 256), jnp.float32)
        _lenS = 256 - jax.random.randint(jax.random.fold_in(_rk, 7), (4,), 0, max(1, 256 // 4) + 1, jnp.int32)
        _lenS2 = 1601 - jax.random.randint(jax.random.fold_in(_rk, 8), (4,), 0, max(1, 1601 // 4) + 1, jnp.int32)
        _ctx_2048P = jax.random.normal(jax.random.fold_in(_rk, 11), (4, 16, 256), jnp.float32)
        _ctx_2048c = jax.random.dirichlet(jax.random.fold_in(_rk, 511), 0.3 * jnp.ones((16,), jnp.float32), (4, 1601))
        _ctx_2048t = jnp.einsum('bsk,bkd->bsd', _ctx_2048c, _ctx_2048P)
        _ctx_2048t = _ctx_2048t * jax.lax.rsqrt(jnp.mean(jnp.square(_ctx_2048t)) + 1e-12) * 0.953939
        ctx_2048 = -0.000514642 + 1.00011 * (_ctx_2048t + 0.3 * jax.random.normal(jax.random.fold_in(_rk, 611), (4, 1601, 256), jnp.float32))
        _validS = jnp.arange(256)[None, :] < _lenS[:, None]
        _validS2 = jnp.arange(1601)[None, :] < _lenS2[:, None]
        _causal = jnp.tril(jnp.ones((256, 256), dtype=bool))
        mask_BxS2_bk0 = jnp.logical_not(jnp.broadcast_to(_validS2[:, :], (4, 1601)))
        return (x, ctx_2048, mask_BxS2_bk0)
    x, ctx_2048, mask_BxS2_bk0 = _rec_inputs()

    def _L0_xattn_setup():
        import jax, jax.numpy as jnp
        import numpy as np
        key = jax.random.key(seed)
        k1, k2, k3 = jax.random.split(key, 3)
        B, S, D, M = (8, 256, 256, 128)
        hidden_states = jax.random.normal(k1, (B, S, D), dtype=jnp.float32)
        memory_tokens = jax.random.normal(k2, (B, M, D), dtype=jnp.float32)
        memory_mask = jax.random.randint(k3, (B, M), 0, 2).astype(jnp.bool_)
        return {'hidden_states': hidden_states, 'memory_tokens': memory_tokens, 'memory_mask': memory_mask}
    _L0_xattn_all = _L0_xattn_setup()
    _L0_xattn_in = {k: v for k, v in _L0_xattn_all.items() if k in ()}
    del _L0_xattn_all

    def _L0_ffn_setup():
        import jax, jax.numpy as jnp
        import numpy as np
        TOP_K = 8

        def _masked_routing(router_logits):
            T, E = router_logits.shape
            sel_w, sel_e = jax.lax.top_k(router_logits, TOP_K)
            sel_w = jax.nn.softmax(sel_w.astype(jnp.float32), axis=1)
            rows = jnp.arange(T)[:, None]
            masked = jnp.zeros((T, E), dtype=jnp.float32).at[rows, sel_e].set(sel_w)
            count = jnp.zeros((E,), dtype=jnp.int32).at[sel_e.reshape(-1)].add(1)
            return (masked, count)
        key = jax.random.key(seed)
        k1, k2, k3, k4, k5 = jax.random.split(key, 5)
        B, S, H, E, I = (1, 256, 256, 32, 96)
        return {'hidden_states': jax.random.normal(k1, (B, S, H), dtype=jnp.float32), 'gate_w': jax.random.normal(k2, (E, H), dtype=jnp.float32) * H ** (-0.5), 'w_gate_proj': jax.random.normal(k3, (E, I, H), dtype=jnp.float32) * H ** (-0.5), 'w_up_proj': jax.random.normal(k4, (E, I, H), dtype=jnp.float32) * H ** (-0.5), 'w_down_proj': jax.random.normal(k5, (E, H, I), dtype=jnp.float32) * I ** (-0.5)}
    _L0_ffn_all = _L0_ffn_setup()
    _L0_ffn_in = {k: v for k, v in _L0_ffn_all.items() if k in ('gate_w', 'w_gate_proj', 'w_up_proj', 'w_down_proj')}
    del _L0_ffn_all

    def _L1_xattn_setup():
        import jax, jax.numpy as jnp
        import numpy as np
        from jax import lax
        LN_EPS = 1e-05
        key = jax.random.key(seed)
        ks = jax.random.split(key, 8)
        B, S, T, D = (4, 128, 256, 256)
        scale = 0.02
        return {'Z': jax.random.normal(ks[0], (B, S, D), dtype=jnp.float32), 'kv': jax.random.normal(ks[1], (B, T, D), dtype=jnp.float32), 'decay': jnp.float32(0.9), 'W_in': jax.random.normal(ks[2], (D, D), dtype=jnp.float32) * scale, 'b_in': jnp.zeros((D,), dtype=jnp.float32), 'W_out': jax.random.normal(ks[3], (D, D), dtype=jnp.float32) * scale, 'b_out': jnp.zeros((D,), dtype=jnp.float32), 'gamma': jnp.ones((D,), dtype=jnp.float32), 'beta': jnp.zeros((D,), dtype=jnp.float32)}
    _L1_xattn_all = _L1_xattn_setup()
    _L1_xattn_in = {k: v for k, v in _L1_xattn_all.items() if k in ('decay', 'W_in', 'b_in', 'W_out', 'b_out', 'gamma', 'beta')}
    del _L1_xattn_all

    def _L1_ffn_setup():
        import jax, jax.numpy as jnp
        import numpy as np
        E = 8
        K = 2
        DIM = 256
        INTER = 176
        N_SHARED = 2
        STD = 0.02
        key = jax.random.key(seed)
        ks = jax.random.split(key, 9)
        B, S = (2, 256)
        return {'x': jax.random.normal(ks[0], (B, S, DIM), dtype=jnp.float32), 'gate_w': jax.random.normal(ks[1], (E, DIM), dtype=jnp.float32) * STD, 'router_bias': jnp.zeros((E,), dtype=jnp.float32), 'W1': jax.random.normal(ks[2], (E, DIM, INTER), dtype=jnp.float32) * STD, 'W3': jax.random.normal(ks[3], (E, DIM, INTER), dtype=jnp.float32) * STD, 'W2': jax.random.normal(ks[4], (E, INTER, DIM), dtype=jnp.float32) * STD, 'sw1': jax.random.normal(ks[5], (N_SHARED * INTER, DIM), dtype=jnp.float32) * STD, 'sw3': jax.random.normal(ks[6], (N_SHARED * INTER, DIM), dtype=jnp.float32) * STD, 'sw2': jax.random.normal(ks[7], (DIM, N_SHARED * INTER), dtype=jnp.float32) * STD}
    _L1_ffn_all = _L1_ffn_setup()
    _L1_ffn_in = {k: v for k, v in _L1_ffn_all.items() if k in ('gate_w', 'router_bias', 'W1', 'W3', 'W2', 'sw1', 'sw3', 'sw2')}
    del _L1_ffn_all

    def _L2_xattn_setup():
        import jax, jax.numpy as jnp
        import numpy as np
        HIDDEN = 256
        NUM_HEADS = 16
        NUM_KV_HEADS = 4
        HEAD_DIM = 128
        ROPE_THETA = 10000.0
        EPS = 1e-06

        def rms_norm(x, w, eps=EPS):
            var = jnp.mean(jnp.square(x), axis=-1, keepdims=True)
            return x * jax.lax.rsqrt(var + eps) * w

        def rope_cache(L, head_dim, theta, dtype):
            inv_freq = 1.0 / theta ** (jnp.arange(0, head_dim, 2, dtype=jnp.float32) / head_dim)
            t = jnp.arange(L, dtype=jnp.float32)
            freqs = jnp.outer(t, inv_freq)
            emb = jnp.concatenate([freqs, freqs], -1)
            cos = jnp.cos(emb).astype(dtype)[None, :, None, :]
            sin = jnp.sin(emb).astype(dtype)[None, :, None, :]
            return (cos, sin)

        def rotate_half(x):
            x1, x2 = jnp.split(x, 2, axis=-1)
            return jnp.concatenate([-x2, x1], axis=-1)
        key = jax.random.key(seed)
        ks = jax.random.split(key, 10)
        B, L, T = (2, 256, 64)
        q_out = NUM_HEADS * HEAD_DIM
        kv_out = NUM_KV_HEADS * HEAD_DIM
        s = lambda fan_in: 1.0 / np.sqrt(fan_in)
        return {'x': jax.random.normal(ks[0], (B, L, HIDDEN), jnp.float32), 'h_ctx_kv': jax.random.normal(ks[1], (B, T, HIDDEN), jnp.float32), 'wq': jax.random.normal(ks[2], (HIDDEN, q_out), jnp.float32) * s(HIDDEN), 'wk': jax.random.normal(ks[3], (HIDDEN, kv_out), jnp.float32) * s(HIDDEN), 'wv': jax.random.normal(ks[4], (HIDDEN, kv_out), jnp.float32) * s(HIDDEN), 'wo': jax.random.normal(ks[5], (q_out, HIDDEN), jnp.float32) * s(q_out), 'wk_ctx': jax.random.normal(ks[6], (HIDDEN, kv_out), jnp.float32) * s(HIDDEN), 'wv_ctx': jax.random.normal(ks[7], (HIDDEN, kv_out), jnp.float32) * s(HIDDEN), 'q_norm_w': jnp.ones((HEAD_DIM,), jnp.float32), 'k_norm_w': jnp.ones((HEAD_DIM,), jnp.float32)}
    _L2_xattn_all = _L2_xattn_setup()
    _L2_xattn_in = {k: v for k, v in _L2_xattn_all.items() if k in ('wq', 'wk', 'wv', 'wo', 'wk_ctx', 'wv_ctx', 'q_norm_w', 'k_norm_w')}
    del _L2_xattn_all

    def _L2_ffn_setup():
        import jax, jax.numpy as jnp
        import numpy as np
        D_MODEL = 256
        D_FF = 1024
        N_EXPERTS = 4
        B, S = (2, 256)
        key = jax.random.key(seed)
        ks = jax.random.split(key, 6)
        scale = 0.02
        return {'hidden_states': jax.random.normal(ks[0], (B, S, D_MODEL), dtype=jnp.float32), 'Wr': jax.random.normal(ks[1], (D_MODEL, N_EXPERTS), dtype=jnp.float32) * scale, 'br': jnp.zeros((N_EXPERTS,), dtype=jnp.float32), 'Wg': jax.random.normal(ks[2], (N_EXPERTS, D_MODEL, D_FF), dtype=jnp.float32) * scale, 'Wu': jax.random.normal(ks[3], (N_EXPERTS, D_MODEL, D_FF), dtype=jnp.float32) * scale, 'Wd': jax.random.normal(ks[4], (N_EXPERTS, D_FF, D_MODEL), dtype=jnp.float32) * scale}
    _L2_ffn_all = _L2_ffn_setup()
    _L2_ffn_in = {k: v for k, v in _L2_ffn_all.items() if k in ('Wr', 'br', 'Wg', 'Wu', 'Wd')}
    del _L2_ffn_all

    def _L3_xattn_setup():
        import jax, jax.numpy as jnp
        import numpy as np
        DIM = 256
        NHEADS = 32
        HEAD_DIM = DIM // NHEADS
        EPS = 1e-06

        def _rmsnorm(t):
            return t * jax.lax.rsqrt(jnp.mean(t * t, axis=-1, keepdims=True) + EPS)
        key = jax.random.key(seed)
        kx, kc, kq, kk, kv = jax.random.split(key, 5)
        x = jax.random.normal(kx, (2, 512, DIM), dtype=jnp.float32)
        context = jax.random.normal(kc, (2, 64, DIM), dtype=jnp.float32)
        std = 0.02
        Wq = jax.random.normal(kq, (DIM, DIM), dtype=jnp.float32) * std
        Wk = jax.random.normal(kk, (DIM, DIM), dtype=jnp.float32) * std
        Wv = jax.random.normal(kv, (DIM, DIM), dtype=jnp.float32) * std
        return {'x': x, 'context': context, 'Wq': Wq, 'Wk': Wk, 'Wv': Wv}
    _L3_xattn_all = _L3_xattn_setup()
    _L3_xattn_in = {k: v for k, v in _L3_xattn_all.items() if k in ('Wq', 'Wk', 'Wv')}
    del _L3_xattn_all

    def _L3_ffn_setup():
        import jax, jax.numpy as jnp
        import numpy as np
        EPS = 1e-05

        def _quant_weight(w):
            scale = jnp.mean(jnp.abs(w)) + EPS
            wq = jnp.clip(jnp.round(w / scale), -1.0, 1.0)
            return (wq, scale)

        def _quant_act(x):
            s = jnp.max(jnp.abs(x), axis=-1, keepdims=True) / 127.0 + EPS
            xq = jnp.clip(jnp.round(x / s), -128.0, 127.0)
            return (xq, s)

        def _qlinear(x, w):
            wq, ws = _quant_weight(w)
            xq, xs = _quant_act(x)
            y = jnp.einsum('bsi,oi->bso', xq, wq)
            return y * xs * ws
        key = jax.random.key(seed)
        k1, k2, k3, k4 = jax.random.split(key, 4)
        H, I = (256, 1024)
        x = jax.random.normal(k1, (4, 512, H), dtype=jnp.float32)
        w_gate = jax.random.normal(k2, (I, H), dtype=jnp.float32) * (1.0 / np.sqrt(H))
        w_up = jax.random.normal(k3, (I, H), dtype=jnp.float32) * (1.0 / np.sqrt(H))
        w_down = jax.random.normal(k4, (H, I), dtype=jnp.float32) * (1.0 / np.sqrt(I))
        return {'x': x, 'w_gate': w_gate, 'w_up': w_up, 'w_down': w_down}
    _L3_ffn_all = _L3_ffn_setup()
    _L3_ffn_in = {k: v for k, v in _L3_ffn_all.items() if k in ('w_gate', 'w_up', 'w_down')}
    del _L3_ffn_all
    return {'x': x, 'ctx_2048': ctx_2048, 'mask_BxS2_bk0': mask_BxS2_bk0, 'L0_ffn_gate_w': _L0_ffn_in['gate_w'], 'L0_ffn_w_gate_proj': _L0_ffn_in['w_gate_proj'], 'L0_ffn_w_up_proj': _L0_ffn_in['w_up_proj'], 'L0_ffn_w_down_proj': _L0_ffn_in['w_down_proj'], 'L1_xattn_decay': _L1_xattn_in['decay'], 'L1_xattn_W_in': _L1_xattn_in['W_in'], 'L1_xattn_b_in': _L1_xattn_in['b_in'], 'L1_xattn_W_out': _L1_xattn_in['W_out'], 'L1_xattn_b_out': _L1_xattn_in['b_out'], 'L1_xattn_gamma': _L1_xattn_in['gamma'], 'L1_xattn_beta': _L1_xattn_in['beta'], 'L1_ffn_gate_w': _L1_ffn_in['gate_w'], 'L1_ffn_router_bias': _L1_ffn_in['router_bias'], 'L1_ffn_W1': _L1_ffn_in['W1'], 'L1_ffn_W3': _L1_ffn_in['W3'], 'L1_ffn_W2': _L1_ffn_in['W2'], 'L1_ffn_sw1': _L1_ffn_in['sw1'], 'L1_ffn_sw3': _L1_ffn_in['sw3'], 'L1_ffn_sw2': _L1_ffn_in['sw2'], 'L2_xattn_wq': _L2_xattn_in['wq'], 'L2_xattn_wk': _L2_xattn_in['wk'], 'L2_xattn_wv': _L2_xattn_in['wv'], 'L2_xattn_wo': _L2_xattn_in['wo'], 'L2_xattn_wk_ctx': _L2_xattn_in['wk_ctx'], 'L2_xattn_wv_ctx': _L2_xattn_in['wv_ctx'], 'L2_xattn_q_norm_w': _L2_xattn_in['q_norm_w'], 'L2_xattn_k_norm_w': _L2_xattn_in['k_norm_w'], 'L2_ffn_Wr': _L2_ffn_in['Wr'], 'L2_ffn_br': _L2_ffn_in['br'], 'L2_ffn_Wg': _L2_ffn_in['Wg'], 'L2_ffn_Wu': _L2_ffn_in['Wu'], 'L2_ffn_Wd': _L2_ffn_in['Wd'], 'L3_xattn_Wq': _L3_xattn_in['Wq'], 'L3_xattn_Wk': _L3_xattn_in['Wk'], 'L3_xattn_Wv': _L3_xattn_in['Wv'], 'L3_ffn_w_gate': _L3_ffn_in['w_gate'], 'L3_ffn_w_up': _L3_ffn_in['w_up'], 'L3_ffn_w_down': _L3_ffn_in['w_down']}

def reference(x, ctx_2048, mask_BxS2_bk0, L0_ffn_gate_w, L0_ffn_w_gate_proj, L0_ffn_w_up_proj, L0_ffn_w_down_proj, L1_xattn_decay, L1_xattn_W_in, L1_xattn_b_in, L1_xattn_W_out, L1_xattn_b_out, L1_xattn_gamma, L1_xattn_beta, L1_ffn_gate_w, L1_ffn_router_bias, L1_ffn_W1, L1_ffn_W3, L1_ffn_W2, L1_ffn_sw1, L1_ffn_sw3, L1_ffn_sw2, L2_xattn_wq, L2_xattn_wk, L2_xattn_wv, L2_xattn_wo, L2_xattn_wk_ctx, L2_xattn_wv_ctx, L2_xattn_q_norm_w, L2_xattn_k_norm_w, L2_ffn_Wr, L2_ffn_br, L2_ffn_Wg, L2_ffn_Wu, L2_ffn_Wd, L3_xattn_Wq, L3_xattn_Wk, L3_xattn_Wv, L3_ffn_w_gate, L3_ffn_w_up, L3_ffn_w_down):
    import jax
    import jax.numpy as jnp

    def _L0_xattn_ref(hidden_states, memory_tokens, memory_mask):
        import jax, jax.numpy as jnp
        import numpy as np
        B, S, D = hidden_states.shape
        scale = 1.0 / jnp.sqrt(jnp.asarray(D, hidden_states.dtype))
        scores = jnp.einsum('bsd,bmd->bsm', hidden_states, memory_tokens) * scale
        neg_inf = jnp.asarray(-1e+30, scores.dtype)
        scores = jnp.where(memory_mask[:, None, :], scores, neg_inf)
        attn = jax.nn.softmax(scores, axis=-1)
        readout = jnp.einsum('bsm,bmd->bsd', attn, memory_tokens)
        valid_b = jnp.any(memory_mask, axis=-1)
        out = jnp.where(valid_b[:, None, None], readout, jnp.zeros_like(readout))
        return out

    def _L0_ffn_ref(hidden_states, gate_w, w_gate_proj, w_up_proj, w_down_proj):
        import jax, jax.numpy as jnp
        import numpy as np
        TOP_K = 8

        def _masked_routing(router_logits):
            T, E = router_logits.shape
            sel_w, sel_e = jax.lax.top_k(router_logits, TOP_K)
            sel_w = jax.nn.softmax(sel_w.astype(jnp.float32), axis=1)
            rows = jnp.arange(T)[:, None]
            masked = jnp.zeros((T, E), dtype=jnp.float32).at[rows, sel_e].set(sel_w)
            count = jnp.zeros((E,), dtype=jnp.int32).at[sel_e.reshape(-1)].add(1)
            return (masked, count)
        B, S, H = hidden_states.shape
        x = hidden_states.reshape(-1, H)
        router_logits = x @ gate_w.T
        masked_w, _count = _masked_routing(router_logits)
        g = jnp.einsum('th,eih->tei', x, w_gate_proj)
        u = jnp.einsum('th,eih->tei', x, w_up_proj)
        h = jax.nn.silu(g) * u
        h = h * masked_w[:, :, None]
        out = jnp.einsum('tei,ehi->th', h, w_down_proj)
        return out.reshape(B, S, H)

    def _L1_xattn_ref(Z, kv, decay, W_in, b_in, W_out, b_out, gamma, beta):
        import jax, jax.numpy as jnp
        import numpy as np
        from jax import lax
        LN_EPS = 1e-05
        B, T, D = kv.shape
        K = jax.nn.sigmoid(decay)
        x = jnp.einsum('btd,ed->bte', kv, W_in) + b_in

        def scan_fn(s, xt):
            s = K * s + xt
            return (s, s)
        s0 = jnp.zeros((B, D), dtype=kv.dtype)
        _, states = lax.scan(scan_fn, s0, jnp.swapaxes(x, 0, 1))
        states = jnp.swapaxes(states, 0, 1)
        proj = jnp.einsum('btd,ed->bte', states, W_out) + b_out
        summary = jnp.mean(proj, axis=1, keepdims=True)
        y = Z + summary
        mu = jnp.mean(y, axis=-1, keepdims=True)
        var = jnp.mean((y - mu) ** 2, axis=-1, keepdims=True)
        return (y - mu) / jnp.sqrt(var + LN_EPS) * gamma + beta

    def _L1_ffn_ref(x, gate_w, router_bias, W1, W3, W2, sw1, sw3, sw2):
        import jax, jax.numpy as jnp
        import numpy as np
        E = 8
        K = 2
        DIM = 256
        INTER = 176
        N_SHARED = 2
        STD = 0.02
        B, S, D = x.shape
        X = x.reshape(-1, D)
        T = X.shape[0]
        logits = jnp.einsum('td,ed->te', X, gate_w)
        scores = jax.nn.sigmoid(logits)
        sel = scores + router_bias[None, :]
        _, idx = jax.lax.top_k(sel, K)
        w = jnp.take_along_axis(scores, idx, axis=1)
        w = w / jnp.clip(jnp.sum(w, axis=-1, keepdims=True), 1e-12)
        gate_full = jnp.zeros((T, E), dtype=w.dtype).at[jnp.arange(T)[:, None], idx].set(w)
        h1 = jnp.einsum('td,edh->eth', X, W1)
        h3 = jnp.einsum('td,edh->eth', X, W3)
        y = jnp.einsum('eth,ehd->etd', jax.nn.silu(h1) * h3, W2)
        out = jnp.einsum('etd,te->td', y, gate_full)
        shared = jnp.einsum('th,dh->td', jax.nn.silu(jnp.einsum('td,hd->th', X, sw1)) * jnp.einsum('td,hd->th', X, sw3), sw2)
        out = out + shared
        return out.reshape(B, S, D)

    def _L2_xattn_ref(x, h_ctx_kv, wq, wk, wv, wo, wk_ctx, wv_ctx, q_norm_w, k_norm_w):
        import jax, jax.numpy as jnp
        import numpy as np
        HIDDEN = 256
        NUM_HEADS = 16
        NUM_KV_HEADS = 4
        HEAD_DIM = 128
        ROPE_THETA = 10000.0
        EPS = 1e-06

        def rms_norm(x, w, eps=EPS):
            var = jnp.mean(jnp.square(x), axis=-1, keepdims=True)
            return x * jax.lax.rsqrt(var + eps) * w

        def rope_cache(L, head_dim, theta, dtype):
            inv_freq = 1.0 / theta ** (jnp.arange(0, head_dim, 2, dtype=jnp.float32) / head_dim)
            t = jnp.arange(L, dtype=jnp.float32)
            freqs = jnp.outer(t, inv_freq)
            emb = jnp.concatenate([freqs, freqs], -1)
            cos = jnp.cos(emb).astype(dtype)[None, :, None, :]
            sin = jnp.sin(emb).astype(dtype)[None, :, None, :]
            return (cos, sin)

        def rotate_half(x):
            x1, x2 = jnp.split(x, 2, axis=-1)
            return jnp.concatenate([-x2, x1], axis=-1)
        B, L, _ = x.shape
        T = h_ctx_kv.shape[1]
        rep = NUM_HEADS // NUM_KV_HEADS
        q = (x @ wq).reshape(B, L, NUM_HEADS, HEAD_DIM)
        k = (x @ wk).reshape(B, L, NUM_KV_HEADS, HEAD_DIM)
        v = (x @ wv).reshape(B, L, NUM_KV_HEADS, HEAD_DIM)
        q = rms_norm(q, q_norm_w)
        k = rms_norm(k, k_norm_w)
        k_ctx = (h_ctx_kv @ wk_ctx).reshape(B, T, NUM_KV_HEADS, HEAD_DIM)
        v_ctx = (h_ctx_kv @ wv_ctx).reshape(B, T, NUM_KV_HEADS, HEAD_DIM)
        k_ctx = rms_norm(k_ctx, k_norm_w)
        cos, sin = rope_cache(L, HEAD_DIM, ROPE_THETA, x.dtype)
        q = q * cos + rotate_half(q) * sin
        k = k * cos + rotate_half(k) * sin
        k_full = jnp.concatenate([k_ctx, k], axis=1)
        v_full = jnp.concatenate([v_ctx, v], axis=1)
        k_full = jnp.repeat(k_full, rep, axis=2)
        v_full = jnpp_repeat = jnp.repeat(v_full, rep, axis=2)
        i = jnp.arange(L)[:, None]
        j = jnp.arange(L)[None, :]
        causal = jnp.where(j > i, -jnp.inf, 0.0).astype(x.dtype)
        mask = jnp.concatenate([jnp.zeros((L, T), x.dtype), causal], axis=1)
        scale = 1.0 / np.sqrt(HEAD_DIM)
        scores = jnp.einsum('blhd,bmhd->bhlm', q, k_full) * scale + mask
        probs = jax.nn.softmax(scores, axis=-1)
        out = jnp.einsum('bhlm,bmhd->blhd', probs, v_full)
        out = out.reshape(B, L, NUM_HEADS * HEAD_DIM)
        return out @ wo

    def _L2_ffn_ref(hidden_states, Wr, br, Wg, Wu, Wd):
        import jax, jax.numpy as jnp
        import numpy as np
        D_MODEL = 256
        D_FF = 1024
        N_EXPERTS = 4
        B, S = (2, 256)
        b, s, d = hidden_states.shape
        x = hidden_states.reshape(-1, d)
        logits = x @ Wr + br
        probs = jax.nn.softmax(logits, axis=-1)
        top_w, top_idx = jax.lax.top_k(probs, 1)
        g = jnp.einsum('td,edf->tef', x, Wg)
        u = jnp.einsum('td,edf->tef', x, Wu)
        h = jax.nn.silu(g) * u
        y = jnp.einsum('tef,efd->ted', h, Wd)
        sel = jnp.take_along_axis(y, top_idx[:, :, None], axis=1)[:, 0]
        out = sel * top_w
        return out.reshape(b, s, d)

    def _L3_xattn_ref(x, context, Wq, Wk, Wv):
        import jax, jax.numpy as jnp
        import numpy as np
        DIM = 256
        NHEADS = 32
        HEAD_DIM = DIM // NHEADS
        EPS = 1e-06

        def _rmsnorm(t):
            return t * jax.lax.rsqrt(jnp.mean(t * t, axis=-1, keepdims=True) + EPS)
        b, n, _ = x.shape
        m = context.shape[1]
        q = x @ Wq.T
        k_raw = context @ Wk.T
        v_raw = context @ Wv.T
        q = q.reshape(b, n, NHEADS, HEAD_DIM).transpose(0, 2, 1, 3)
        kv = jnp.concatenate([k_raw, v_raw], axis=-1)
        kv = kv.reshape(b, m, NHEADS, HEAD_DIM, 2)
        k = kv[..., 0].transpose(0, 2, 1, 3)
        v = kv[..., 1].transpose(0, 2, 1, 3)
        q = _rmsnorm(q)
        k = _rmsnorm(k)
        scale = HEAD_DIM ** (-0.5)
        scores = jnp.einsum('bhnd,bhmd->bhnm', q, k) * scale
        attn = jax.nn.softmax(scores, axis=-1)
        out = jnp.einsum('bhnm,bhmd->bhnd', attn, v)
        return out.transpose(0, 2, 1, 3).reshape(b, n, NHEADS * HEAD_DIM)

    def _L3_ffn_ref(x, w_gate, w_up, w_down):
        import jax, jax.numpy as jnp
        import numpy as np
        EPS = 1e-05

        def _quant_weight(w):
            scale = jnp.mean(jnp.abs(w)) + EPS
            wq = jnp.clip(jnp.round(w / scale), -1.0, 1.0)
            return (wq, scale)

        def _quant_act(x):
            s = jnp.max(jnp.abs(x), axis=-1, keepdims=True) / 127.0 + EPS
            xq = jnp.clip(jnp.round(x / s), -128.0, 127.0)
            return (xq, s)

        def _qlinear(x, w):
            wq, ws = _quant_weight(w)
            xq, xs = _quant_act(x)
            y = jnp.einsum('bsi,oi->bso', xq, wq)
            return y * xs * ws
        gate = jax.nn.silu(_qlinear(x, w_gate))
        up = _qlinear(x, w_up)
        return _qlinear(gate * up, w_down)
    x = x + _L0_xattn_ref(_layernorm(x, axis=-1), ctx_2048, mask_BxS2_bk0)
    x = x + _L0_ffn_ref(_layernorm(x, axis=-1), L0_ffn_gate_w, L0_ffn_w_gate_proj, L0_ffn_w_up_proj, L0_ffn_w_down_proj)
    x = x + _L1_xattn_ref(_layernorm(x, axis=-1), ctx_2048, L1_xattn_decay, L1_xattn_W_in, L1_xattn_b_in, L1_xattn_W_out, L1_xattn_b_out, L1_xattn_gamma, L1_xattn_beta)
    x = x + _L1_ffn_ref(_layernorm(x, axis=-1), L1_ffn_gate_w, L1_ffn_router_bias, L1_ffn_W1, L1_ffn_W3, L1_ffn_W2, L1_ffn_sw1, L1_ffn_sw3, L1_ffn_sw2)
    x = x + _L2_xattn_ref(_layernorm(x, axis=-1), ctx_2048, L2_xattn_wq, L2_xattn_wk, L2_xattn_wv, L2_xattn_wo, L2_xattn_wk_ctx, L2_xattn_wv_ctx, L2_xattn_q_norm_w, L2_xattn_k_norm_w)
    x = x + _L2_ffn_ref(_layernorm(x, axis=-1), L2_ffn_Wr, L2_ffn_br, L2_ffn_Wg, L2_ffn_Wu, L2_ffn_Wd)
    x = x + _L3_xattn_ref(_layernorm(x, axis=-1), ctx_2048, L3_xattn_Wq, L3_xattn_Wk, L3_xattn_Wv)
    x = x + _L3_ffn_ref(_layernorm(x, axis=-1), L3_ffn_w_gate, L3_ffn_w_up, L3_ffn_w_down)
    return x

_drawn_inputs = setup_inputs


def setup_inputs(seed=0):
    import zlib

    import numpy as np

    out = dict(_drawn_inputs(seed))
    spreads = {'L1_xattn_b_in': (0.0, 0.1),
     'L1_xattn_b_out': (0.0, 0.1),
     'L1_xattn_gamma': (1.0, 0.2),
     'L1_xattn_beta': (0.0, 0.1),
     'L1_ffn_router_bias': (0.0, 0.8),
     'L2_xattn_q_norm_w': (1.0, 0.6),
     'L2_xattn_k_norm_w': (1.0, 0.6),
     'L2_ffn_br': (0.0, 0.8)}
    factors = {'L1_ffn_gate_w': 8.0,
     'L1_ffn_W1': 8.0,
     'L1_ffn_W3': 8.0,
     'L1_ffn_W2': 8.0,
     'L1_ffn_sw1': 6.344,
     'L1_ffn_sw3': 6.248,
     'L1_ffn_sw2': 6.292,
     'L2_xattn_wk': 4.967,
     'L2_ffn_Wr': 8.0,
     'L2_ffn_Wg': 8.0,
     'L2_ffn_Wu': 8.0,
     'L2_ffn_Wd': 8.0,
     'L3_xattn_Wq': 8.0,
     'L3_xattn_Wk': 8.0,
     'L3_xattn_Wv': 8.0,
     'L3_ffn_w_gate': 7.336,
     'L3_ffn_w_up': 7.071,
     'L3_ffn_w_down': 7.089}
    for name, (base, spread) in spreads.items():
        noise = np.random.default_rng([zlib.crc32(name.encode()), seed]).standard_normal(out[name].shape)
        drawn = base * np.exp(spread * noise) if base else spread * noise
        out[name] = jnp.asarray(drawn.astype(out[name].dtype))
    for name, factor in factors.items():
        out[name] = (out[name] * factor).astype(out[name].dtype)
    return out
```

```python
from contextlib import ExitStack

import numpy as np

import concourse.bass as bass
from concourse import mybir

F32 = mybir.dt.float32
F32R = mybir.dt.float32r
BF16 = mybir.dt.bfloat16
F16 = mybir.dt.float16
U8 = mybir.dt.uint8
ACT = mybir.ActivationFunctionType
ALU = mybir.AluOpType
AX = mybir.AxisListType

P = 128
B, S, D = 4, 256, 256
DC = D // P
TB = S // P
NT = B * TB
NTOK = B * S
M = 1601
MC = -(-M // P)
ML = M - (MC - 1) * P
BANK = 512
HALF = NTOK // 2
LN_EPS = 1e-5
RMS_EPS = 1e-6
BIG = 1e30
LOWEST = -3.0e38

MOE = {"L0": (32, 96, 0), "L1": (8, 176, 352), "L2": (4, 1024, 0)}

QH, KH, HD = 16, 4, 128
REP = QH // KH
H3, D3 = 32, 8
HG = 4
NG = H3 // HG
FF3 = 1024


def chunk_rows(j):
    return P if j < MC - 1 else ML


def moe_chunks(name):
    experts, hidden, shared = MOE[name]
    n = -(-(experts * hidden + shared) // P)
    return n + n % 2


class Steps:

    def __init__(self, sem):
        self.sem, self.base, self.done, self.i, self.per = sem, 0, 0, None, 0

    def then(self, engine, instruction):
        instruction.then_inc(self.sem, 1)
        self.done += 1
        value = self.base + self.done
        engine.wait_ge(self.sem, value if self.i is None else self.i * self.per + value)

    def enter(self, i, per):
        self.base, self.done, self.i, self.per = self.base + self.done, 0, i, per

    def leave(self, turns):
        assert self.done == self.per, (self.done, self.per)
        self.base, self.done, self.i = self.base + turns * self.per, 0, None



def program(nc, t, out):
    with ExitStack() as stack:

        def sem(name):
            return stack.enter_context(nc.semaphore(name))

        def sems(name, n):
            return [sem(f"{name}{i}") for i in range(n)]

        def sb(name, shape, dt=F32, scope=stack):
            return scope.enter_context(nc.sbuf_tensor(name, shape, dt))

        psum = stack.enter_context(nc.psum_tensor("psum", [P, 8 * BANK], F32))

        def bank(n, width=BANK, at=0):
            return psum[:, n * BANK + at:n * BANK + at + width]

        x = sb("x", [P, NT, D])
        xn = sb("xn", [P, NT, D])
        xT = sb("xT", [P, DC, NTOK])
        ident = sb("ident", [P, P])
        identb = sb("identb", [P, P], BF16)
        identh = sb("identh", [P, P], F16)
        half_power = sb("half_power", [P, 2 * HD])
        zerob = sb("zerob", [1, BANK], BF16)
        ones = sb("ones", [P, P])
        stats = sb("stats", [P, NT, 6])
        mv = sb("mv", [P, NT, 2])
        veps = sb("veps", [P, NT])
        rstd = sb("rstd", [P, NT])

        decay_raw = sb("decay_raw", [P, 1])
        decay_k = sb("decay_k", [P, 1])
        decay_sum = sb("decay_sum", [P, DC, B])
        decay_total = sb("decay_total", [P, 1])

        r_earlier = sb("r_earlier", [P, 8, 8])
        l1_in, l1_out = sb("l1_in", [P, DC, D]), sb("l1_out", [P, DC, D])
        l1_bin, l1_bout = sb("l1_bin", [P, DC]), sb("l1_bout", [P, DC])
        l1_gamma, l1_beta = sb("l1_gamma", [P, D]), sb("l1_beta", [P, D])
        causal = sb("causal", [P, P], BF16)
        x_land = sem("x_land")
        consts = sem("consts")
        x_upd = sem("x_upd")
        ln_stats, ln_mv, ln_veps, ln_rstd = sem("ln_stats"), sem("ln_mv"), sem("ln_veps"), sem("ln_rstd")
        xn_done = sem("xn_done")
        xT_ps = sem("xT_ps")
        xT_cp = sem("xT_cp")
        xT_lo = sem("xT_lo")
        dve_steps = Steps(sem("dve_steps"))
        pool_steps = Steps(sem("pool_steps"))
        out_done = sem("out_done")
        NCONST = 6

        UPDATES = [NT, NT, NT, NT, B * KH * TB, NT, B * NG, NT]
        X_AT = [sum(UPDATES[:k]) for k in range(len(UPDATES) + 1)]

        norm_count = {"k": 0, "ps": 0, "cp": 0, "lo": 0}

        def norm_plan(transposed, split):
            at = dict(norm_count, transposed=transposed, split=split)
            norm_count["k"] += 1
            if transposed:
                norm_count["ps"] += 2
                norm_count["cp"] += 4
                if split:
                    norm_count["lo"] += 4
            at["cp_end"], at["lo_end"] = norm_count["cp"], norm_count["lo"]
            return at

        def norm_vector(v, at, src):
            k = at["k"]
            for n in range(NT):
                v.bn_stats(stats[:, n, :], src[:, n, :]).then_inc(ln_stats, 1)
            v.wait_ge(ln_stats, NT * (k + 1))
            for n in range(NT):
                v.bn_aggr(mv[:, n, :], stats[:, n, :]).then_inc(ln_mv, 1)
            v.wait_ge(ln_mv, NT * (k + 1))
            v.tensor_scalar(veps[:, :], mv[:, :, 1], LN_EPS, None, ALU.add).then_inc(ln_veps, 1)
            v.wait_ge(ln_rstd, k + 1)
            for n in range(NT):
                v.tensor_scalar(xn[:, n, :], src[:, n, :], mv[:, n, 0:1], rstd[:, n:n + 1],
                                ALU.subtract, ALU.mult).then_inc(xn_done, 1)
            if at["split"]:
                for q in range(4):
                    hf, c = q // 2, q % 2
                    v.wait_ge(xT_cp, at["cp"] + q + 1)
                    cols = slice(hf * HALF, (hf + 1) * HALF)
                    v.tensor_tensor(xlo[:, c, cols], bank(2 * c + hf), xhi[:, c, cols].bitcast(F32),
                                    ALU.subtract).then_inc(xT_lo, 1)

        def norm_pool(g, at):
            g.wait_ge(ln_veps, at["k"] + 1)
            g.tensor_tensor(rstd[:, :], veps[:, :], half_power[:, 0:NT], ALU.pow).then_inc(ln_rstd, 1)

        def norm_tensor(pe, at):
            for n in range(NT):
                pe.wait_ge(xn_done, NT * at["k"] + n + 1)
                for c in range(DC):
                    last_t = pe.transpose(bank(2 * c + n // 4, P, (n % 4) * P),
                                          xn[:, n, c * P:(c + 1) * P], ident[:, :])
                if n % 4 == 3:
                    last_t.then_inc(xT_ps, 1)

        def norm_scalar(act, at):
            dst = xhi if at["split"] else xT
            for q in range(4):
                hf, c = q // 2, q % 2
                act.wait_ge(xT_ps, at["ps"] + hf + 1)
                act.activation(dst[:, c, hf * HALF:(hf + 1) * HALF], bank(2 * c + hf),
                               ACT.Copy).then_inc(xT_cp, 1)

        ln_l0x = norm_plan(True, False)
        l0 = ExitStack()
        c_T = [sb(f"c_T{s}", [P, DC, M], F32, l0) for s in range(2)]
        c_N = [sb(f"c_N{s}", [P, MC, D], F32, l0) for s in range(2)]
        c_mask = [sb(f"c_mask{s}", [P, M], U8, l0) for s in range(2)]
        c_bias = [sb(f"c_bias{s}", [P, M], F32, l0) for s in range(2)]
        c_any = [sb(f"c_any{s}", [P, 1], F32, l0) for s in range(2)]
        l0_xb = [sb(f"l0_xb{s}", [P, DC, S], F32, l0) for s in range(2)]
        l0_sm = [sb(f"l0_sm{n}", [P, M], F32, l0) for n in range(TB)]
        l0_p = [sb(f"l0_p{n}", [P, M], F32, l0) for n in range(TB)]
        l0_pt = [sb(f"l0_pt{n}", [P, MC, P], F32, l0) for n in range(TB)]
        l0_mx = sb("l0_mx", [P, TB], F32, l0)
        l0_nmx = sb("l0_nmx", [P, TB], F32, l0)
        l0_sum = sb("l0_sum", [P, TB], F32, l0)
        l0_rec = sb("l0_rec", [P, TB], F32, l0)
        l0_top = sb("l0_top", [P, 1], F32, l0)
        l0_gate = sb("l0_gate", [P, TB], F32, l0)
        decay_geo = sb("decay_geo", [P, M], F32, l0)
        decay_junk = sb("decay_junk", [P, M], F32, l0)
        decay_tmp = [sb(f"decay_tmp{s}", [P, DC], F32, l0) for s in range(2)]
        l0.close()
        c_land = sems("c_land", 2)
        decay_land, decay_sig = sem("decay_land"), sem("decay_sig")
        l0_xbd, l0_s, l0_masked, l0_shift = sem("l0_xbd"), sem("l0_s"), sem("l0_masked"), sem("l0_shift")
        l0_exp, l0_T, l0_ptd = sem("l0_exp"), sem("l0_T"), sem("l0_ptd")
        l0_pv = sems("l0_pv", 2)
        l0_decayed = sems("l0_decayed", 2)
        TG = -(-MC // 4)

        def l0x_sync(sp):
            with sp.Fori(0, B // 2) as i:
                for s in range(2):
                    n = i * 2 + s
                    sp.wait_ge(l0_pv[s], i * TB)
                    sp.wait_ge(l0_decayed[s], i)
                    one = bass.ds(n, 1)
                    sp.dma_start(c_T[s][:, :, :], t["ctx_T"][one].rearrange("o p c m -> p (o c) m"))\
                        .then_inc(c_land[s], 16)
                    sp.dma_start(c_mask[s][:, :], t["mask"][one, :].to_broadcast([P, M]))\
                        .then_inc(c_land[s], 16)
                    sp.dma_start(c_N[s][:, 0:MC - 1, :],
                                 t["ctx"][one, 0:(MC - 1) * P, :].rearrange("o (j p) d -> p (o j) d", p=P))\
                        .then_inc(c_land[s], 16)
                    sp.dma_start(c_N[s][0:ML, MC - 1, :],
                                 t["ctx"][one, (MC - 1) * P:M, :].rearrange("o p d -> p (o d)"))\
                        .then_inc(c_land[s], 16)

        def l0x_scalar(act):
            act.wait_ge(decay_land, 16)
            act.activation(decay_k[:, :], decay_raw[:, :], ACT.Sigmoid).then_inc(decay_sig, 1)
            act.preload_act_table(ACT.Exp)
            act.wait_ge(xT_cp, ln_l0x["cp_end"])
            with act.Fori(0, B // 2) as i:
                for s in range(2):
                    n = i * 2 + s
                    act.activation(l0_xb[s][:, :, :], xT[:, :, bass.ds(n * S, S)], ACT.Copy)\
                        .then_inc(l0_xbd, 1)
                    for k in range(TB):
                        act.wait_ge(l0_shift, i * 4 + 2 * s + k + 1)
                        act.activation(l0_p[k][:, :], l0_sm[k][:, :], ACT.Exp, bias=l0_nmx[:, k:k + 1],
                                       accum_out=l0_sum[:, k:k + 1]).then_inc(l0_exp, 1)
                    for k in range(TB):
                        for q in range(TG):
                            act.wait_ge(l0_T, (i * 4 + 2 * s + k) * TG + q + 1)
                            if q < TG - 1:
                                ins = act.activation(l0_pt[k][:, 4 * q:4 * q + 4, :], bank(4 + q % 2), ACT.Copy)
                            else:
                                ins = act.activation(l0_pt[k][0:ML, MC - 1, :], bank(4 + q % 2, P)[0:ML, :], ACT.Copy)
                            ins.then_inc(l0_ptd, 1)

        def l0x_vector(v):
            v.wait_ge(decay_sig, 1)
            v.wait_ge(consts, NCONST)
            dve_steps.then(v, v.tensor_tensor_scan(decay_geo[:, :], decay_k[:, 0:1].to_broadcast([P, M]),
                                                   ones[:, 0:1].to_broadcast([P, M]), 0.0, ALU.mult, ALU.add))
            dve_steps.then(v, v.tensor_reduce(decay_total[:, :], decay_geo[:, :], AX.X, ALU.add))
            with v.Fori(0, B // 2) as i:
                dve_steps.enter(i, 2 * (5 + 2 * TB))
                for s in range(2):
                    n = i * 2 + s
                    v.wait_ge(c_land[s], 64 * (i + 1))
                    dve_steps.then(v, v.tensor_scalar(c_bias[s][:, :], c_mask[s][:, :], 16 * BIG, -16 * BIG,
                                                      ALU.mult, ALU.add))
                    dve_steps.then(v, v.tensor_reduce(l0_top[:, :], c_bias[s][:, :], AX.X, ALU.max))
                    dve_steps.then(v, v.tensor_scalar(c_any[s][:, :], l0_top[:, :], -1.0, None, ALU.is_ge))
                    for k in range(TB):
                        v.wait_ge(l0_s, i * 4 + 2 * s + k + 1)
                        v.memset(l0_gate[:, k:k + 1], 0.0)
                        v.tensor_tensor_reduce(l0_sm[k][:, :], psum[:, 0:M], c_bias[s][:, :], 1.0 / 16, LOWEST,
                                               ALU.add, ALU.max, l0_mx[:, k:k + 1]).then_inc(l0_masked, 1)
                        v.wait_ge(l0_masked, i * 4 + 2 * s + k + 1)
                        v.tensor_scalar(l0_nmx[:, k:k + 1], l0_mx[:, k:k + 1], -1.0, None, ALU.mult)\
                            .then_inc(l0_shift, 1)
                    for c in range(DC):
                        ins = v.tensor_tensor_reduce(decay_junk[:, :], c_T[s][:, c, :], decay_geo[:, ::-1], 1.0, 0.0,
                                                     ALU.mult, ALU.add, decay_tmp[s][:, c:c + 1])
                        dve_steps.then(v, ins)
                    v.tensor_copy(decay_sum[:, :, bass.ds(n, 1)], decay_tmp[s][:, :].rearrange("p (c o) -> p c o", o=1))\
                        .then_inc(l0_decayed[s], 1)
                    for k in range(TB):
                        v.wait_ge(l0_exp, i * 4 + 2 * s + k + 1)
                        dve_steps.then(v, v.reciprocal(l0_rec[:, k:k + 1], l0_sum[:, k:k + 1]))
                        dve_steps.then(v, v.tensor_tensor(l0_rec[:, k:k + 1], l0_rec[:, k:k + 1], c_any[s][:, :], ALU.mult))
                        v.wait_ge(l0_pv[s], i * TB + k + 1)
                        row = x[:, bass.ds(n * TB + k, 1), :].rearrange("p o d -> p (o d)")
                        v.scalar_tensor_tensor(row, bank(6 + k, D), l0_rec[:, k:k + 1], row,
                                               ALU.mult, ALU.add).then_inc(x_upd, 1)
            dve_steps.leave(B // 2)

        def l0x_tensor(pe):
            with pe.Fori(0, B // 2) as i:
                for s in range(2):
                    pe.wait_ge(c_land[s], 64 * (i + 1))
                    pe.wait_ge(l0_xbd, i * 2 + s + 1)
                    for k in range(TB):
                        pe.wait_ge(l0_masked, i * 4 + 2 * s + k)
                        for a in range(0, M, BANK):
                            z = min(a + BANK, M)
                            for c in range(DC):
                                mm = pe.matmul(psum[:, a:z], l0_xb[s][:, c, k * P:(k + 1) * P], c_T[s][:, c, a:z],
                                               start=(c == 0), stop=(c == DC - 1))
                        mm.then_inc(l0_s, 1)
                    for k in range(TB):
                        tile = i * 4 + 2 * s + k
                        pe.wait_ge(l0_exp, tile + 1)
                        for q in range(TG):
                            if q >= 2:
                                pe.wait_ge(l0_ptd, tile * TG + q - 1)
                            for j in range(4 * q, min(4 * q + 4, MC)):
                                r = chunk_rows(j)
                                mm = pe.transpose(bank(4 + q % 2, P, (j % 4) * P)[0:r, :],
                                                  l0_p[k][:, j * P:j * P + r], ident[:, :])
                            mm.then_inc(l0_T, 1)
                        for j in range(MC):
                            if j % 4 == 0:
                                pe.wait_ge(l0_ptd, tile * TG + j // 4 + 1)
                            r = chunk_rows(j)
                            mm = pe.matmul(bank(6 + k, D), l0_pt[k][0:r, j, :], c_N[s][0:r, j, :],
                                           start=(j == 0), stop=(j == MC - 1))
                        mm.then_inc(l0_pv[s], 1)

        def constants_pool(g):
            for tile in (ident, identb, identh):
                pool_steps.then(g, g.memset(tile[:, :], 0.0))
                g.affine_select(out=tile[:, :], in_=tile[:, :], compare_op=ALU.not_equal, fill=1.0,
                                base=0, pattern=[[-1, P]], channel_multiplier=1).then_inc(consts, 1)
            pool_steps.then(g, g.memset(half_power[:, :], -0.5))
            g.memset(ones[:, :], 1.0).then_inc(consts, 1)
            g.memset(zerob[:, :], 0.0).then_inc(consts, 1)
            pool_steps.then(g, g.memset(causal[:, :], 0.0))
            g.affine_select(out=causal[:, :], in_=causal[:, :], compare_op=ALU.is_ge, fill=-BIG,
                            base=0, pattern=[[-1, P]], channel_multiplier=1).then_inc(consts, 1)
            pool_steps.then(g, g.memset(r_earlier[:, :, :], 1.0))
            g.affine_select(out=r_earlier[:, :, :], in_=r_earlier[:, :, :], compare_op=ALU.is_gt, fill=0.0,
                            base=0, pattern=[[1, 8], [-1, 8]], channel_multiplier=0).then_inc(early_done, 1)

        def parameters_scalar(act):
            act.dma_start(decay_raw[:, :], t["decay"].to_broadcast([P, 1])).then_inc(decay_land, 16)
            for dst, name in ((l1_in, "L1_in"), (l1_out, "L1_out"), (l1_bin, "L1_bin"), (l1_bout, "L1_bout")):
                act.dma_start(dst[...], t[name]).then_inc(l1_land, 16)
            for dst, name in ((l1_gamma, "L1_gamma"), (l1_beta, "L1_beta")):
                act.dma_start(dst[:, :], t[name].to_broadcast([P, D])).then_inc(l1_land, 16)

        EMAX = 32
        moe = ExitStack()
        xhi = sb("xhi", [P, DC, NTOK], F32R, moe)
        xlo = sb("xlo", [P, DC, NTOK], F32R, moe)
        w_stage = [sb(f"w_stage{s}", [P, 3 * D], F32, moe) for s in range(2)]
        w_hi_gu = [sb(f"w_hi_gu{s}", [P, 2 * D], F32R, moe) for s in range(2)]
        w_lo_gu = [sb(f"w_lo_gu{s}", [P, 2 * D], F32R, moe) for s in range(2)]
        w_hi_d = [sb(f"w_hi_d{s}", [P, D], F32R, moe) for s in range(2)]
        w_lo_d = [sb(f"w_lo_d{s}", [P, D], F32R, moe) for s in range(2)]
        e_silu = [sb(f"e_silu{s}", [P, HALF], F32, moe) for s in range(2)]
        e_h = [sb(f"e_h{s}", [P, HALF], F32, moe) for s in range(2)]
        e_hhi = [sb(f"e_hhi{s}", [P, HALF], F32R, moe) for s in range(2)]
        e_hlo = [sb(f"e_hlo{s}", [P, HALF], F32R, moe) for s in range(2)]
        e_out = sb("e_out", [P, DC, HALF], F32, moe)
        e_rows = sb("e_rows", [3 * EMAX, max(moe_chunks(n) for n in MOE) * P], BF16, moe)
        r_w = sb("r_w", [P, DC, EMAX], F32, moe)
        r_whi = sb("r_whi", [P, DC, EMAX], F32R, moe)
        r_wlo = sb("r_wlo", [P, DC, EMAX], F32R, moe)
        r_bias = {"L1": sb("r_bias1", [P, 8], F32, moe), "L2": sb("r_bias2", [P, 4], F32, moe)}
        r_log = sb("r_log", [P, NT, EMAX], F32, moe)
        r_a = sb("r_a", [P, NT, EMAX], F32, moe)
        r_b = sb("r_b", [P, NT, EMAX], F32, moe)
        r_top = sb("r_top", [P, NT, 8], F32, moe)
        r_sum = sb("r_sum", [P, NT], F32, moe)
        r_pair = sb("r_pair", [P, NT, 8, 8], F32, moe)
        r_tie = sb("r_tie", [P, NT, 8, 8], F32, moe)
        r_route = sb("r_route", [P, NT, EMAX], F32, moe)
        r_parts = sb("r_parts", [P, NT, 3 * EMAX], BF16, moe)
        r_T = sb("r_T", [3 * EMAX, NTOK], BF16, moe)
        moe.close()

        rows_land, rw_land, rw_split = sem("rows_land"), sem("rw_land"), sem("rw_split")
        rbias_land, early_done = sem("rbias_land"), sem("early_done")
        r_logits, r_in, r_acted, r_done, r_Tps, r_Tcp = (sem(n) for n in (
            "r_logits", "r_in", "r_acted", "r_done", "r_Tps", "r_Tcp"))
        w_land, w_gu, w_d = sems("w_land", 2), sems("w_gu", 2), sems("w_d", 2)
        e_gu, e_act, e_hd, e_down = sems("e_gu", 2), sems("e_act", 2), sems("e_hd", 2), sems("e_down", 2)
        e_acc, e_outd, e_T = sem("e_acc"), sem("e_outd"), sem("e_T")
        G_BANK, U_BANK, R_BANK = (2, 3), (4, 5), (6, 7)

        def three(pe, dst, lhs, rhs, start, stop):
            pe.matmul(dst, lhs[0], rhs[0], start=start, stop=False)
            pe.matmul(dst, lhs[0], rhs[1], start=False, stop=False)
            return pe.matmul(dst, lhs[1], rhs[0], start=False, stop=stop)

        moe_plan = {}

        def moe_prepare(name, index, layer):
            experts, hidden, shared = MOE[name]
            plan = {"ln": norm_plan(True, True), "index": index, "n": moe_chunks(name), "experts": experts,
                    "slots": experts + (shared > 0), "x_at": X_AT[layer],
                    "pairs": sum(moe_chunks(m) for m in list(MOE)[:index])}
            moe_plan[name] = plan

        def moe_sync(sp, name):
            p = moe_plan[name]
            pairs = p["n"] // 2
            sp.wait_ge(x_upd, p["x_at"])
            n3, E = 3 * p["slots"], p["experts"]
            sp.dma_start(e_rows[0:n3, 0:p["n"] * P], t[f"{name}_rows"]).then_inc(rows_land, 16)
            sp.dma_start(r_w[:, :, 0:E], t[f"{name}_router"]).then_inc(rw_land, 16)
            if name in r_bias:
                sp.dma_start(r_bias[name][:, :], t[f"{name}_rbias"].to_broadcast([P, E])).then_inc(rbias_land, 16)
            for hf in range(2):
                m0 = p["pairs"] + hf * pairs
                with sp.Fori(0, pairs) as i:
                    for s in range(2):
                        sp.wait_ge(w_d[s], i + m0)
                        sp.dma_start(w_stage[s][:, :], t[f"{name}_w"][bass.ds(i * 2 + s, 1)]
                                     .rearrange("o p n -> p (o n)")).then_inc(w_land[s], 16)

        def moe_pool(g, name):
            p = moe_plan[name]
            pairs = p["n"] // 2
            for hf in range(2):
                m0 = p["pairs"] + hf * pairs
                with g.Fori(0, pairs) as i:
                    pool_steps.enter(i, 4)
                    for s in range(2):
                        g.wait_ge(w_land[s], i * 16 + 16 * (m0 + 1))
                        g.wait_ge(e_gu[s], i + m0)
                        gu = w_stage[s][:, 0:2 * D]
                        pool_steps.then(g, g.tensor_tensor(w_hi_gu[s][:, :], gu, ones[:, 0:1].to_broadcast([P, 2 * D]), ALU.mult))
                        g.tensor_tensor(w_lo_gu[s][:, :], gu, w_hi_gu[s][:, :].bitcast(F32), ALU.subtract)\
                            .then_inc(w_gu[s], 1)
                        g.wait_ge(e_down[s], i + m0)
                        d = w_stage[s][:, 2 * D:3 * D]
                        pool_steps.then(g, g.tensor_tensor(w_hi_d[s][:, :], d, ones[:, 0:1].to_broadcast([P, D]), ALU.mult))
                        g.tensor_tensor(w_lo_d[s][:, :], d, w_hi_d[s][:, :].bitcast(F32), ALU.subtract)\
                            .then_inc(w_d[s], 1)
                pool_steps.leave(pairs)

        def moe_scalar(act, name):
            p = moe_plan[name]
            norm_scalar(act, p["ln"])
            k, E = p["index"], p["experts"]
            act.wait_ge(r_in, k + 1)
            if name == "L0":
                act.activation(r_a[:, :, 0:E], r_a[:, :, 0:E], ACT.Exp)
                act.activation(r_b[:, :, 0:E], r_b[:, :, 0:E], ACT.Exp).then_inc(r_acted, 1)
            else:
                act.activation(r_a[:, :, 0:E], r_log[:, :, 0:E], ACT.Sigmoid if name == "L1" else ACT.Exp)\
                    .then_inc(r_acted, 1)
            pairs = p["n"] // 2
            act.preload_act_table(ACT.Silu)
            for hf in range(2):
                m0 = p["pairs"] + hf * pairs
                with act.Fori(0, pairs) as i:
                    for s in range(2):
                        act.wait_ge(e_gu[s], i + (m0 + 1))
                        act.activation(e_silu[s][:, :], bank(G_BANK[s]), ACT.Silu).then_inc(e_act[s], 1)
                act.wait_ge(e_acc, 2 * k + hf + 1)
                for c in range(DC):
                    act.activation(e_out[:, c, :], bank(c), ACT.Copy).then_inc(e_outd, 1)

        def route_topk(v, E, k, scores):
            def by(ap, axis):
                return ap.unsqueeze(axis).to_broadcast([P, NT, E, E])
            pair, tie = r_pair[:, :, 0:E, 0:E], r_tie[:, :, 0:E, 0:E]
            other, own = by(scores, 2), by(scores, 3)
            dve_steps.then(v, v.tensor_tensor(tie, other, own, ALU.is_equal))
            dve_steps.then(v, v.tensor_tensor(tie, tie, r_earlier[:, 0:E, 0:E].unsqueeze(1).to_broadcast([P, NT, E, E]), ALU.mult))
            dve_steps.then(v, v.tensor_tensor(pair, other, own, ALU.is_gt))
            dve_steps.then(v, v.tensor_tensor(pair, pair, tie, ALU.add))
            dve_steps.then(v, v.tensor_reduce(r_b[:, :, 0:E], pair, AX.X, ALU.add))
            dve_steps.then(v, v.tensor_scalar(r_b[:, :, 0:E], r_b[:, :, 0:E], k - 0.5, None, ALU.is_lt))

        def moe_vector(v, name):
            p = moe_plan[name]
            k, E, n_slots = p["index"], p["experts"], p["slots"]
            v.wait_ge(x_upd, p["x_at"])
            norm_vector(v, p["ln"], x)
            v.wait_ge(rw_land, 16 * (k + 1))
            dve_steps.then(v, v.tensor_copy(r_whi[:, :, 0:E], r_w[:, :, 0:E]))
            v.tensor_tensor(r_wlo[:, :, 0:E], r_w[:, :, 0:E], r_whi[:, :, 0:E].bitcast(F32), ALU.subtract)\
                .then_inc(rw_split, 1)
            v.wait_ge(r_logits, k + 1)
            lg = bank(6, NT * E).rearrange("p (k e) -> p k e", k=NT)
            a, b, log, route = (r[:, :, 0:E] for r in (r_a, r_b, r_log, r_route))

            def wide(col):
                return col.unsqueeze(2).to_broadcast([P, NT, E])

            if name == "L0":
                dve_steps.then(v, v.tensor_copy(log, lg))
                for n in range(NT):
                    ins = v.max(r_top[:, n, :], log[:, n, :])
                dve_steps.then(v, ins)
                for n in range(NT):
                    ins = v.match_replace(b[:, n, :], r_top[:, n, :], log[:, n, :], -BIG)
                dve_steps.then(v, ins)
                dve_steps.then(v, v.tensor_tensor(a, log, wide(r_top[:, :, 0]), ALU.subtract))
                v.tensor_tensor(b, b, wide(r_top[:, :, 0]), ALU.subtract).then_inc(r_in, 1)
                v.wait_ge(r_acted, k + 1)
                dve_steps.then(v, v.tensor_tensor(route, a, b, ALU.subtract))
                dve_steps.then(v, v.tensor_reduce(r_sum[:, :], route, AX.X, ALU.add))
                dve_steps.then(v, v.reciprocal(r_sum[:, :], r_sum[:, :]))
                dve_steps.then(v, v.tensor_tensor(route, route, wide(r_sum[:, :]), ALU.mult))
            elif name == "L1":
                v.tensor_copy(log, lg).then_inc(r_in, 1)
                v.wait_ge(rbias_land, 16)
                v.wait_ge(early_done, 1)
                v.wait_ge(r_acted, k + 1)
                dve_steps.then(v, v.tensor_tensor(log, a, r_bias[name][:, :].unsqueeze(1).to_broadcast([P, NT, E]), ALU.add))
                route_topk(v, E, 2, log)
                dve_steps.then(v, v.tensor_tensor(route, a, b, ALU.mult))
                dve_steps.then(v, v.tensor_reduce(r_sum[:, :], route, AX.X, ALU.add))
                dve_steps.then(v, v.tensor_scalar(r_sum[:, :], r_sum[:, :], 1e-12, None, ALU.max))
                dve_steps.then(v, v.reciprocal(r_sum[:, :], r_sum[:, :]))
                dve_steps.then(v, v.tensor_tensor(route, route, wide(r_sum[:, :]), ALU.mult))
                dve_steps.then(v, v.memset(r_route[:, :, E:E + 1], 1.0))
            else:
                v.wait_ge(rbias_land, 32)
                dve_steps.then(v, v.tensor_tensor(log, lg, r_bias[name][:, :].unsqueeze(1).to_broadcast([P, NT, E]), ALU.add))
                dve_steps.then(v, v.tensor_reduce(r_sum[:, :], log, AX.X, ALU.max))
                v.tensor_tensor(log, log, wide(r_sum[:, :]), ALU.subtract).then_inc(r_in, 1)
                v.wait_ge(r_acted, k + 1)
                dve_steps.then(v, v.tensor_reduce(r_sum[:, :], a, AX.X, ALU.add))
                dve_steps.then(v, v.reciprocal(r_sum[:, :], r_sum[:, :]))
                dve_steps.then(v, v.tensor_tensor(a, a, wide(r_sum[:, :]), ALU.mult))
                route_topk(v, E, 1, a)
                dve_steps.then(v, v.tensor_tensor(route, a, b, ALU.mult))
            route = r_route[:, :, 0:n_slots]
            rest = r_a[:, :, 0:n_slots]
            parts = [r_parts[:, :, i * n_slots:(i + 1) * n_slots] for i in range(3)]
            dve_steps.then(v, v.tensor_copy(parts[0], route))
            dve_steps.then(v, v.tensor_tensor(rest, route, parts[0], ALU.subtract))
            dve_steps.then(v, v.tensor_copy(parts[1], rest))
            v.tensor_tensor(parts[2], rest, parts[1], ALU.subtract)\
                .then_inc(r_done, 1)
            v.wait_ge(r_Tps, k + 1)
            v.tensor_copy(r_T[0:3 * n_slots, :], bank(7).bitcast(BF16)[0:3 * n_slots, :]).then_inc(r_Tcp, 1)
            pairs = p["n"] // 2
            for hf in range(2):
                m0 = p["pairs"] + hf * pairs
                with v.Fori(0, pairs) as i:
                    dve_steps.enter(i, 6)
                    for s in range(2):
                        v.wait_ge(e_act[s], i + (m0 + 1))
                        dve_steps.then(v, v.tensor_tensor(e_silu[s][:, :], bank(U_BANK[s]), e_silu[s][:, :], ALU.mult))
                        dve_steps.then(v, v.tensor_tensor(e_h[s][:, :], bank(R_BANK[s]), e_silu[s][:, :], ALU.mult))
                        v.wait_ge(e_down[s], i + m0)
                        dve_steps.then(v, v.tensor_copy(e_hhi[s][:, :], e_h[s][:, :]))
                        v.tensor_tensor(e_hlo[s][:, :], e_h[s][:, :], e_hhi[s][:, :].bitcast(F32), ALU.subtract)\
                            .then_inc(e_hd[s], 1)
                dve_steps.leave(pairs)
                for n in range(NT // 2):
                    if n % 2 == 0:
                        v.wait_ge(e_T, 2 * k + hf + 1)
                    tile = x[:, hf * (NT // 2) + n, :]
                    v.tensor_tensor(tile, bank((3, 5)[n // 2], D, (n % 2) * D), tile, ALU.add).then_inc(x_upd, 1)

        def moe_tensor(pe, name):
            p = moe_plan[name]
            k, E, n3 = p["index"], p["experts"], 3 * p["slots"]
            norm_tensor(pe, p["ln"])
            pe.wait_ge(rw_split, k + 1)
            pe.wait_ge(xT_lo, p["ln"]["lo_end"])
            for n in range(NT):
                tok = slice(n * P, (n + 1) * P)
                for c in range(DC):
                    mm = three(pe, bank(6, E, n * E), (xhi[:, c, tok], xlo[:, c, tok]),
                               (r_whi[:, c, 0:E], r_wlo[:, c, 0:E]), c == 0, c == DC - 1)
            mm.then_inc(r_logits, 1)
            pe.wait_ge(r_done, k + 1)
            for n in range(NT):
                mm = pe.transpose(bank(7).bitcast(BF16)[0:n3, n * P:(n + 1) * P],
                                  r_parts[:, n, 0:n3], identb[:, :])
            mm.then_inc(r_Tps, 1)
            pe.wait_ge(r_Tcp, k + 1)
            pe.wait_ge(rows_land, 16 * (k + 1))
            pairs = p["n"] // 2
            for hf in range(2):
                m0 = p["pairs"] + hf * pairs
                cols = slice(hf * HALF, (hf + 1) * HALF)

                def gate_up(s, pair, chunk):
                    pe.wait_ge(w_gu[s], pair + 1)
                    pe.wait_ge(e_hd[s], pair)
                    for at, dst in ((0, G_BANK), (D, U_BANK)):
                        for c in range(DC):
                            w = slice(at + c * P, at + (c + 1) * P)
                            three(pe, bank(dst[s]), (w_hi_gu[s][:, w], w_lo_gu[s][:, w]),
                                  (xhi[:, c, cols], xlo[:, c, cols]), c == 0, c == DC - 1)
                    pe.matmul(bank(R_BANK[s]), e_rows[0:n3, chunk], r_T[0:n3, cols],
                              start=True, stop=True).then_inc(e_gu[s], 1)

                def down(s, pair):
                    pe.wait_ge(w_d[s], pair + 1)
                    pe.wait_ge(e_hd[s], pair + 1)
                    for c in range(DC):
                        w = slice(c * P, (c + 1) * P)
                        mm = pe.matmul(bank(c), w_hi_d[s][:, w], e_hhi[s][:, :], start=False, stop=False, skip_group_check=True)
                        mm = pe.matmul(bank(c), w_hi_d[s][:, w], e_hlo[s][:, :], start=False, stop=False, skip_group_check=True)
                        mm = pe.matmul(bank(c), w_lo_d[s][:, w], e_hhi[s][:, :], start=False, stop=False, skip_group_check=True)
                    mm.then_inc(e_down[s], 1)

                if hf == 1:
                    pe.wait_ge(x_upd, p["x_at"] + NT // 2)
                for c in range(DC):
                    pe.matmul(bank(c), zerob[:, 0:P], zerob[:, :], start=True, stop=False, skip_group_check=True)
                gate_up(0, m0, slice(0, P))
                with pe.Fori(0, pairs - 1) as i:
                    gate_up(1, i + m0, bass.ds(i * 2 * P + P, P))
                    down(0, i + m0)
                    gate_up(0, i + (m0 + 1), bass.ds(i * 2 * P + 2 * P, P))
                    down(1, i + m0)
                gate_up(1, m0 + pairs - 1, slice((p["n"] - 1) * P, p["n"] * P))
                down(0, m0 + pairs - 1)
                down(1, m0 + pairs - 1)
                for c in range(DC):
                    mm = pe.matmul(bank(c), zerob[:, 0:P], zerob[:, :], start=False, stop=True, skip_group_check=True)
                mm.then_inc(e_acc, 1)
                for n in range(NT // 2):
                    for c in range(DC):
                        if n == 0:
                            pe.wait_ge(e_outd, 4 * k + 2 * hf + c + 1)
                        mm = pe.transpose(bank((3, 5)[n // 2], P, (n % 2) * D + c * P),
                                          e_out[:, c, n * P:(n + 1) * P], ident[:, :])
                mm.then_inc(e_T, 1)

        moe_prepare("L0", 0, 1)

        ln_l1z = norm_plan(False, False)
        ln_l1y = norm_plan(False, False)
        l1 = ExitStack()
        l1_bsum = sb("l1_bsum", [P, DC], F32, l1)
        l1_mean = sb("l1_mean", [P, DC, B], F32, l1)
        l1_summ = sb("l1_summ", [P, DC, B], F32, l1)
        l1_wide = sb("l1_wide", [P, DC, B, P], F32, l1)
        l1_y = sb("l1_y", [P, NT, D], F32, l1)
        l1.close()
        l1_land, l1_h, l1_meand, l1_s, l1_wided, l1_b = (sem(n) for n in (
            "l1_land", "l1_h", "l1_meand", "l1_s", "l1_wided", "l1_b"))

        def l1x_scalar(act):
            pass

        def l1x_vector(v):
            v.wait_ge(x_upd, X_AT[2])
            norm_vector(v, ln_l1z, x)
            v.wait_ge(l1_land, 16 * 6)
            dve_steps.then(v, v.tensor_scalar(l1_bsum[:, :], l1_bin[:, :], decay_total[:, 0:1], None, ALU.mult))
            v.wait_ge(l1_h, 1)
            for c in range(DC):
                v.tensor_scalar(l1_mean[:, c, :], bank(0, B, c * B), l1_bsum[:, c:c + 1], 1.0 / M,
                                ALU.add, ALU.mult).then_inc(l1_meand, 1)
            v.wait_ge(l1_s, 1)
            for c in range(DC):
                ins = v.tensor_scalar(l1_summ[:, c, :], bank(1, B, c * B), l1_bout[:, c:c + 1], None, ALU.add)
            dve_steps.then(v, ins)
            v.tensor_copy(l1_wide[:, :, :, :].rearrange("p c b n -> p (c b) n"),
                          l1_summ[:, :, :].rearrange("p c b -> p (c b)").unsqueeze(2).to_broadcast([P, DC * B, P]))\
                .then_inc(l1_wided, 1)
            v.wait_ge(l1_b, 1)
            v.wait_ge(xn_done, NT * (ln_l1z["k"] + 1))
            for n in range(NT):
                b = n // TB
                ins = v.tensor_tensor(l1_y[:, n, :], xn[:, n, :], bank(2 + b // 2, D, (b % 2) * D), ALU.add)
            dve_steps.then(v, ins)
            norm_vector(v, ln_l1y, l1_y)
            v.wait_ge(xn_done, NT * (ln_l1y["k"] + 1))
            gamma = l1_gamma[:, :].unsqueeze(1).to_broadcast([P, NT, D])
            beta = l1_beta[:, :].unsqueeze(1).to_broadcast([P, NT, D])
            dve_steps.then(v, v.tensor_tensor(xn[:, :, :], xn[:, :, :], gamma, ALU.mult))
            dve_steps.then(v, v.tensor_tensor(xn[:, :, :], xn[:, :, :], beta, ALU.add))
            for n in range(NT):
                v.tensor_tensor(x[:, n, :], x[:, n, :], xn[:, n, :], ALU.add).then_inc(x_upd, 1)

        def l1x_tensor(pe):
            pe.wait_ge(l1_land, 16 * 6)
            pe.wait_ge(x_upd, X_AT[2])
            for e in range(DC):
                for c in range(DC):
                    mm = pe.matmul(bank(0, B, e * B), l1_in[:, c, e * P:(e + 1) * P], decay_sum[:, c, :],
                                   start=(c == 0), stop=(c == DC - 1))
            mm.then_inc(l1_h, 1)
            pe.wait_ge(l1_meand, DC)
            for e in range(DC):
                for c in range(DC):
                    mm = pe.matmul(bank(1, B, e * B), l1_out[:, c, e * P:(e + 1) * P], l1_mean[:, c, :],
                                   start=(c == 0), stop=(c == DC - 1))
            mm.then_inc(l1_s, 1)
            pe.wait_ge(l1_wided, 1)
            for b in range(B):
                for c in range(DC):
                    mm = pe.matmul(bank(2 + b // 2, P, (b % 2) * D + c * P), l1_wide[:, c, b, :], ident[:, :],
                                   start=True, stop=True)
            mm.then_inc(l1_b, 1)

        moe_prepare("L1", 1, 3)

        ln_l2x = norm_plan(True, False)
        l2 = ExitStack()
        KC = MC + TB
        MX = M + S
        U = REP * TB
        l2_ctx = sb("l2_ctx", [P, DC, M], F32, l2)
        l2_w = sb("l2_w", [P, DC, 4 * HD + REP * HD], F32, l2)
        l2_wo = sb("l2_wo", [P, REP, D], F32, l2)
        l2_xb = sb("l2_xb", [P, DC, S], F32, l2)
        l2_kraw = sb("l2_kraw", [P, KC, HD], F32, l2)
        l2_kn = sb("l2_kn", [P, KC, HD], F32, l2)
        l2_ra = sb("l2_ra", [P, TB, HD], F32, l2)
        l2_rb = sb("l2_rb", [P, TB, HD], F32, l2)
        l2_vhi = sb("l2_vhi", [P, KC, HD], F32R, l2)
        l2_vlo = sb("l2_vlo", [P, KC, HD], F32R, l2)
        l2_kThi = sb("l2_kThi", [P, MX], F32R, l2)
        l2_kTlo = sb("l2_kTlo", [P, MX], F32R, l2)
        l2_q = sb("l2_q", [P, TB, REP, HD], F32, l2)
        l2_qa = sb("l2_qa", [P, TB, REP, HD], F32, l2)
        l2_qb = sb("l2_qb", [P, TB, REP, HD], F32, l2)
        l2_qThi = sb("l2_qThi", [P, TB, REP * P], F32R, l2)
        l2_qTlo = sb("l2_qTlo", [P, TB, REP * P], F32R, l2)
        l2_p = [sb(f"l2_p{n}", [P, MX], F32, l2) for n in range(2)]
        l2_pThi = sb("l2_pThi", [P, KC, 2 * P], F32R, l2)
        l2_pTlo = sb("l2_pTlo", [P, KC, 2 * P], F32R, l2)
        l2_oT = sb("l2_oT", [P, REP, P], F32, l2)
        l2_cos, l2_sin = sb("l2_cos", [P, TB, HD // 2], F32, l2), sb("l2_sin", [P, TB, HD // 2], F32, l2)
        l2_qw, l2_kw = sb("l2_qw", [P, HD], F32, l2), sb("l2_kw", [P, HD], F32, l2)
        l2_kwc = sb("l2_kwc", [P, 1], F32, l2)
        rope_q = [sb(f"rope_q{n}", [P, TB, HD], F32, l2) for n in range(2)]
        rope_k = [sb(f"rope_k{n}", [P, TB, HD], F32, l2) for n in range(2)]
        l2_kms, l2_krs = sb("l2_kms", [P, KC], F32, l2), sb("l2_krs", [P, KC], F32, l2)
        l2_qms, l2_qrs = sb("l2_qms", [P, U], F32, l2), sb("l2_qrs", [P, U], F32, l2)
        l2_scale = sb("l2_scale", [P, U], F32, l2)
        l2_mx4, l2_mx = sb("l2_mx4", [P, U, 4], F32, l2), sb("l2_mx", [P, U], F32, l2)
        l2_nb = sb("l2_nb", [P, U], F32, l2)
        l2_sum, l2_rec = sb("l2_sum", [P, U], F32, l2), sb("l2_rec", [P, U], F32, l2)
        l2.close()
        (l2_cland, l2_wland, l2_oland, l2_pland, l2_xbd, l2_kv, l2_qp, l2_kva, l2_vd, l2_ksqd, l2_qsqd, l2_kmsd,
         l2_krsd, l2_qmsd, l2_qrsd, l2_knd, l2_qnd, l2_kT, l2_kTh, l2_kTl, l2_qT, l2_qTh, l2_qTl, l2_s, l2_sc, l2_nbd,
         l2_exp, l2_pn, l2_T, l2_Th, l2_Tl, l2_pv, l2_o, l2_y) = (sem(n) for n in (
             "l2_cland l2_wland l2_oland l2_pland l2_xbd l2_kv l2_qp l2_kva l2_vd l2_ksqd l2_qsqd l2_kmsd "
             "l2_krsd l2_qmsd l2_qrsd l2_knd l2_qnd l2_kT l2_kTh l2_kTl l2_qT l2_qTh l2_qTl l2_s l2_sc l2_nbd "
             "l2_exp l2_pn l2_T l2_Th l2_Tl l2_pv l2_o l2_y").split())
        KG = -(-KC // 4)

        def l2_keys(k):
            return M + (k + 1) * P

        def l2_blocks(k, q):
            cols = [(j, j * P, chunk_rows(j)) if j < MC else (j, M + (j - MC) * P, P) for j in range(MC + k + 1)]
            return cols[4 * q:4 * q + 4]

        def l2_pieces(k):
            return [(a, min(a + BANK, l2_keys(k))) for a in range(0, l2_keys(k), BANK)]

        PIECES = len(l2_pieces(0))
        assert PIECES == len(l2_pieces(1)) == KG == 4

        def l2x_sync(sp):
            sp.wait_ge(x_upd, X_AT[4])
            for dst, name in ((l2_cos, "rope_cos"), (l2_sin, "rope_sin"), (l2_kwc, "L2_kwc")):
                sp.dma_start(dst[...], t[name]).then_inc(l2_pland, 16)
            for dst, name in ((l2_qw, "L2_qw"), (l2_kw, "L2_kw")):
                sp.dma_start(dst[:, :], t[name].to_broadcast([P, HD])).then_inc(l2_pland, 16)
            with sp.Fori(0, B) as b:
                sp.wait_ge(l2_qp, b * (KH * TB))
                sp.dma_start(l2_ctx[:, :, :], t["ctx_T"][bass.ds(b, 1)].rearrange("o p c m -> p (o c) m"))\
                    .then_inc(l2_cland, 16)
                with sp.Fori(0, KH) as h:
                    g = b * KH + h
                    sp.wait_ge(l2_qp, g * TB)
                    sp.dma_start(l2_w[:, :, :], t["L2_w_qkv"][bass.ds(h, 1)].rearrange("o p c n -> p (o c) n"))\
                        .then_inc(l2_wland, 16)
                    sp.wait_ge(l2_y, g * TB)
                    sp.dma_start(l2_wo[:, :, :], t["L2_wo"][bass.ds(h, 1)].rearrange("o p r n -> p (o r) n"))\
                        .then_inc(l2_oland, 16)

        def l2x_pool(g_):
            with g_.Fori(0, B * KH) as g:
                g_.wait_ge(l2_kmsd, g + 1)
                g_.tensor_tensor(l2_krs[:, :], l2_kms[:, :], half_power[:, 0:KC], ALU.pow).then_inc(l2_krsd, 1)
                g_.wait_ge(l2_qmsd, g + 1)
                g_.tensor_tensor(l2_qrs[:, :], l2_qms[:, :], half_power[:, 0:U], ALU.pow).then_inc(l2_qrsd, 1)

        def l2x_scalar(act):
            norm_scalar(act, ln_l2x)
            act.preload_act_table(ACT.Exp)
            act.wait_ge(xT_cp, ln_l2x["cp_end"])
            act.wait_ge(l2_pland, 16 * 5)
            with act.Fori(0, B) as b, act.Fori(0, KH) as h:
                g = b * KH + h
                act.wait_ge(l2_qp, g * TB)
                act.activation(l2_xb[:, :, :], xT[:, :, bass.ds(b * S, S)], ACT.Copy).then_inc(l2_xbd, 1)
                for j in range(KC):
                    r = chunk_rows(j) if j < MC else P
                    act.wait_ge(l2_kv, g * KC + (j + 1))
                    kv = bank(j % 3, 2 * HD)
                    act.activation(l2_kraw[0:r, j, :], kv[0:r, 0:HD], ACT.Copy).then_inc(l2_kva, 1)
                    act.activation(l2_vhi[0:r, j, :], kv[0:r, HD:2 * HD], ACT.Copy).then_inc(l2_kva, 1)
                for k in range(TB):
                    act.wait_ge(l2_qp, g * TB + (k + 1))
                    act.activation(l2_q[:, k, :, :], bank(3 + k), ACT.Copy)
                    act.activation(l2_qa[:, k, :, :], bank(3 + k), ACT.Square).then_inc(l2_qsqd, 1)
                act.wait_ge(l2_kva, (g + 1) * (2 * KC))
                act.activation(l2_kn[:, :, :], l2_kraw[:, :, :], ACT.Square).then_inc(l2_ksqd, 1)
                for k in range(TB):
                    act.wait_ge(l2_qT, g * TB + (k + 1))
                    act.activation(l2_qThi[:, k, :], bank(3 + k), ACT.Copy).then_inc(l2_qTh, 1)
                for q in range(KG):
                    act.wait_ge(l2_kT, g * KG + (q + 1))
                    a, z = q * BANK, min(q * BANK + BANK, M)
                    ins = act.activation(l2_kThi[:, a:z], bank(3 + q % 2, z - a), ACT.Copy, scale=l2_kwc[:, 0:1])
                    if q == KG - 1:
                        ins = act.activation(l2_kThi[:, M:MX], bank(3 + q % 2, S, M - a), ACT.Copy)
                    ins.then_inc(l2_kTh, 1)

                def exp(u):
                    n = l2_keys(u // REP)
                    act.wait_ge(l2_nbd, g * U + (u + 1))
                    act.activation(l2_p[u % 2][:, 0:n], l2_p[u % 2][:, 0:n], ACT.Exp, bias=l2_nb[:, u:u + 1],
                                   scale=l2_scale[:, u:u + 1], accum_out=l2_sum[:, u:u + 1]).then_inc(l2_exp, 1)

                def turned(u):
                    for q in range(KG):
                        nb = len(l2_blocks(u // REP, q))
                        act.wait_ge(l2_T, (g * U + u) * KG + (q + 1))
                        act.activation(l2_pThi[:, 4 * q:4 * q + nb, (u % 2) * P:(u % 2 + 1) * P],
                                       bank(3 + q % 2, nb * P).rearrange("p (j n) -> p j n", n=P), ACT.Copy)\
                            .then_inc(l2_Th, 1)

                def out_rows(w):
                    act.wait_ge(l2_pv, g * (U // 2) + (w + 1))
                    act.activation(l2_oT[:, 2 * (w % 2):2 * (w % 2) + 2, :].rearrange("p r n -> p (r n)"),
                                   bank(5, 2 * P, (w % 2) * 2 * P), ACT.Copy).then_inc(l2_o, 1)

                exp(0)
                for u in range(U):
                    if u + 1 < U:
                        exp(u + 1)
                    if u % 2 == 0 and u >= 2:
                        out_rows(u // 2 - 1)
                    turned(u)
                out_rows(U // 2 - 1)

        def l2x_vector(v):
            v.wait_ge(x_upd, X_AT[4])
            dve_steps.then(v, v.memset(l2_kraw[:, :, :], 0.0))
            v.wait_ge(l2_pland, 16 * 5)
            hh = HD // 2
            for (own, other), w in ((rope_q, l2_qw), (rope_k, l2_kw)):
                for k in range(TB):
                    v.tensor_tensor(own[:, k, 0:hh], l2_cos[:, k, :], w[:, 0:hh], ALU.mult)
                    v.tensor_tensor(own[:, k, hh:HD], l2_cos[:, k, :], w[:, hh:HD], ALU.mult)
                    v.scalar_tensor_tensor(other[:, k, 0:hh], l2_sin[:, k, :], -1.0, w[:, hh:HD], ALU.mult, ALU.mult)
                    ins = v.tensor_tensor(other[:, k, hh:HD], l2_sin[:, k, :], w[:, 0:hh], ALU.mult)
            dve_steps.then(v, ins)
            norm_vector(v, ln_l2x, x)
            with v.Fori(0, B) as b, v.Fori(0, KH) as h:
                g = b * KH + h
                dve_steps.enter(g, L2_DVE_STEPS)
                for j in range(KC):
                    r = chunk_rows(j) if j < MC else P
                    v.wait_ge(l2_kva, g * (2 * KC) + 2 * (j + 1))
                    kv = bank(j % 3, 2 * HD)
                    v.tensor_tensor(l2_vlo[0:r, j, :], kv[0:r, HD:2 * HD], l2_vhi[0:r, j, :].bitcast(F32),
                                    ALU.subtract).then_inc(l2_vd, 1)
                v.wait_ge(l2_qsqd, (g + 1) * TB)
                dve_steps.then(v, v.tensor_reduce(l2_qms[:, :], l2_qa[:, :, :, :].rearrange("p k r n -> p (k r) n"), AX.X, ALU.add))
                v.tensor_scalar(l2_qms[:, :], l2_qms[:, :], 1.0 / HD, RMS_EPS, ALU.mult, ALU.add).then_inc(l2_qmsd, 1)
                v.wait_ge(l2_ksqd, g + 1)
                dve_steps.then(v, v.tensor_reduce(l2_kms[:, :], l2_kn[:, :, :], AX.X, ALU.add))
                v.tensor_scalar(l2_kms[:, :], l2_kms[:, :], 1.0 / HD, RMS_EPS, ALU.mult, ALU.add).then_inc(l2_kmsd, 1)
                own, other = (r[:, :, :].unsqueeze(2).to_broadcast([P, TB, REP, HD]) for r in rope_q)
                dve_steps.then(v, v.tensor_tensor(l2_qa[:, :, :, :], l2_q[:, :, :, :], own, ALU.mult))
                v.tensor_tensor(l2_qb[:, :, :, 0:hh], l2_q[:, :, :, hh:HD], other[:, :, :, 0:hh], ALU.mult)
                dve_steps.then(v, v.tensor_tensor(l2_qb[:, :, :, hh:HD], l2_q[:, :, :, 0:hh], other[:, :, :, hh:HD], ALU.mult))
                v.tensor_tensor(l2_q[:, :, :, :], l2_qa[:, :, :, :], l2_qb[:, :, :, :], ALU.add).then_inc(l2_qnd, 1)
                v.wait_ge(l2_qrsd, g + 1)
                dve_steps.then(v, v.tensor_scalar(l2_scale[:, :], l2_qrs[:, :], float(HD) ** -0.5, None, ALU.mult))
                v.wait_ge(l2_krsd, g + 1)
                dve_steps.then(v, v.tensor_tensor(l2_kn[:, :, :], l2_kraw[:, :, :],
                                                  l2_krs[:, :].unsqueeze(2).to_broadcast([P, KC, HD]), ALU.mult))
                kx = l2_kn[:, MC:KC, :]
                v.tensor_tensor(l2_ra[:, :, :], kx, rope_k[0][:, :, :], ALU.mult)
                v.tensor_tensor(l2_rb[:, :, 0:hh], kx[:, :, hh:HD], rope_k[1][:, :, 0:hh], ALU.mult)
                dve_steps.then(v, v.tensor_tensor(l2_rb[:, :, hh:HD], kx[:, :, 0:hh], rope_k[1][:, :, hh:HD], ALU.mult))
                v.tensor_tensor(l2_kraw[:, MC:KC, :], l2_ra[:, :, :], l2_rb[:, :, :], ALU.add).then_inc(l2_knd, 1)
                for k in range(TB):
                    v.wait_ge(l2_qTh, g * TB + (k + 1))
                    v.tensor_tensor(l2_qTlo[:, k, :], bank(3 + k), l2_qThi[:, k, :].bitcast(F32), ALU.subtract)\
                        .then_inc(l2_qTl, 1)
                for q in range(KG):
                    v.wait_ge(l2_kTh, g * KG + (q + 1))
                    a, z = q * BANK, min(q * BANK + BANK, M)
                    ins = v.scalar_tensor_tensor(l2_kTlo[:, a:z], bank(3 + q % 2, z - a), l2_kwc[:, 0:1],
                                                 l2_kThi[:, a:z].bitcast(F32), ALU.mult, ALU.subtract)
                    if q == KG - 1:
                        ins = v.tensor_tensor(l2_kTlo[:, M:MX], bank(3 + q % 2, S, M - a), l2_kThi[:, M:MX].bitcast(F32),
                                              ALU.subtract)
                    ins.then_inc(l2_kTl, 1)

                def scores(u):
                    for n, (a, z) in enumerate(l2_pieces(u // REP)):
                        v.wait_ge(l2_s, (g * U + u) * PIECES + (n + 1))
                        v.tensor_scalar(l2_p[u % 2][:, a:z], bank((u * PIECES + n) % 3, z - a, (z - a) % 2), 1.0, LOWEST, ALU.mult,
                                        ALU.max, accum_out=l2_mx4[:, u, n:n + 1]).then_inc(l2_sc, 1)
                    v.wait_ge(l2_sc, (g * U + u + 1) * PIECES)
                    dve_steps.then(v, v.tensor_reduce(l2_mx[:, u:u + 1], l2_mx4[:, u, :], AX.X, ALU.max))
                    v.tensor_scalar(l2_nb[:, u:u + 1], l2_mx[:, u:u + 1], l2_scale[:, u:u + 1], -1.0,
                                    ALU.mult, ALU.mult).then_inc(l2_nbd, 1)

                def normal(u):
                    n = l2_keys(u // REP)
                    v.wait_ge(l2_exp, g * U + (u + 1))
                    dve_steps.then(v, v.reciprocal(l2_rec[:, u:u + 1], l2_sum[:, u:u + 1]))
                    v.tensor_scalar(l2_p[u % 2][:, 0:n], l2_p[u % 2][:, 0:n], l2_rec[:, u:u + 1], None, ALU.mult)\
                        .then_inc(l2_pn, 1)

                def turned(u):
                    for q in range(KG):
                        nb = len(l2_blocks(u // REP, q))
                        at = slice((u % 2) * P, (u % 2 + 1) * P)
                        v.wait_ge(l2_Th, (g * U + u) * KG + (q + 1))
                        v.tensor_tensor(l2_pTlo[:, 4 * q:4 * q + nb, at],
                                        bank(3 + q % 2, nb * P).rearrange("p (j n) -> p j n", n=P),
                                        l2_pThi[:, 4 * q:4 * q + nb, at].bitcast(F32), ALU.subtract).then_inc(l2_Tl, 1)

                def add_out(k):
                    v.wait_ge(l2_y, g * TB + (k + 1))
                    row = x[:, bass.ds(b * TB + k, 1), :].rearrange("p o d -> p (o d)")
                    v.tensor_tensor(row, bank(6 + k, D), row, ALU.add).then_inc(x_upd, 1)

                scores(0)
                for u in range(U):
                    normal(u)
                    if u + 1 < U:
                        scores(u + 1)
                    turned(u)
                    if u == REP + 1:
                        add_out(0)
                add_out(1)
            dve_steps.leave(B * KH)

        def l2x_tensor(pe):
            norm_tensor(pe, ln_l2x)
            with pe.Fori(0, B) as b, pe.Fori(0, KH) as h:
                g = b * KH + h
                pe.wait_ge(l2_cland, b * 16 + 16)
                pe.wait_ge(l2_wland, g * 16 + 16)
                pe.wait_ge(l2_xbd, g + 1)
                pe.wait_ge(x_upd, g * TB + X_AT[4])
                for j in range(KC):
                    r = chunk_rows(j) if j < MC else P
                    if j >= 3:
                        pe.wait_ge(l2_vd, g * KC + (j - 2))
                    for c in range(DC):
                        lhs = l2_ctx[:, c, j * P:j * P + r] if j < MC else l2_xb[:, c, (j - MC) * P:(j - MC + 1) * P]
                        at = 0 if j < MC else 2 * HD
                        mm = pe.matmul(bank(j % 3, 2 * HD)[0:r, :], lhs,
                                       l2_w[:, c, at:at + 2 * HD], start=(c == 0), stop=(c == DC - 1))
                    mm.then_inc(l2_kv, 1)
                for k in range(TB):
                    for c in range(DC):
                        mm = pe.matmul(bank(3 + k), l2_xb[:, c, k * P:(k + 1) * P], l2_w[:, c, 4 * HD:],
                                       start=(c == 0), stop=(c == DC - 1))
                    mm.then_inc(l2_qp, 1)
                pe.wait_ge(l2_qnd, g + 1)
                for k in range(TB):
                    for n in range(REP):
                        mm = pe.transpose(bank(3 + k, P, n * P), l2_q[:, k, n, :], ident[:, :])
                    mm.then_inc(l2_qT, 1)
                pe.wait_ge(l2_knd, g + 1)
                for q in range(KG):
                    if q < 2:
                        pe.wait_ge(l2_qTl, g * TB + (q + 1))
                    else:
                        pe.wait_ge(l2_kTl, g * KG + (q - 1))
                    for j, a, r in l2_blocks(TB - 1, q):
                        src = l2_kn[0:r, j, :] if j < MC else l2_kraw[:, j, :]
                        mm = pe.transpose(bank(3 + q % 2, r, a - q * BANK), src, ident[0:r, 0:r])
                    mm.then_inc(l2_kT, 1)
                pe.wait_ge(l2_qTl, (g + 1) * TB)

                def scores(u):
                    k, n = u // REP, u % REP
                    rows = slice(n * P, (n + 1) * P)
                    for i, (a, z) in enumerate(l2_pieces(k)):
                        at = u * PIECES + i
                        if u == 0:
                            pe.wait_ge(l2_kTl, g * KG + (i + 1))
                        if at >= 3:
                            pe.wait_ge(l2_sc, g * (U * PIECES) + (at - 2))
                        a -= (z - a) % 2
                        diagonal = M + k * P
                        dst = bank(at % 3, z - a)
                        pe.matmul(dst, l2_qThi[:, k, rows], l2_kThi[:, a:z], start=True, stop=False)
                        if a <= diagonal < z:
                            pe.matmul(bank(at % 3, P, diagonal - a), identb[:, :], causal[:, :],
                                      start=False, stop=False, skip_group_check=True)
                        pe.matmul(dst, l2_qThi[:, k, rows], l2_kTlo[:, a:z], start=False, stop=False)
                        mm = pe.matmul(dst, l2_qTlo[:, k, rows], l2_kThi[:, a:z], start=False, stop=True)
                        mm.then_inc(l2_s, 1)

                def turn(u):
                    pe.wait_ge(l2_pn, g * U + (u + 1))
                    for q in range(KG):
                        if u > 0 or q >= 2:
                            pe.wait_ge(l2_Tl, (g * U + u) * KG + q - 1)
                        for j, a, r in l2_blocks(u // REP, q):
                            mm = pe.transpose(bank(3 + q % 2, P, (j % 4) * P)[0:r, :], l2_p[u % 2][:, a:a + r], ident[:, :])
                        mm.then_inc(l2_T, 1)

                def values(w):
                    k = w // 2
                    if w >= 1:
                        pe.wait_ge(l2_o, g * (U // 2) + w)
                    pe.wait_ge(l2_Tl, (g * U + 2 * w + 2) * KG)
                    if w == 0:
                        pe.wait_ge(l2_vd, (g + 1) * KC)
                    for j in range(MC + k + 1):
                        r = chunk_rows(j) if j < MC else P
                        mm = three(pe, bank(5, 2 * P, (w % 2) * 2 * P), (l2_vhi[0:r, j, :], l2_vlo[0:r, j, :]),
                                   (l2_pThi[0:r, j, :], l2_pTlo[0:r, j, :]), j == 0, j == MC + k)
                    mm.then_inc(l2_pv, 1)

                def output(k):
                    pe.wait_ge(l2_oland, g * 16 + 16)
                    pe.wait_ge(l2_o, g * (U // 2) + 2 * (k + 1))
                    for n in range(REP):
                        mm = pe.matmul(bank(6 + k, D), l2_oT[:, n, :], l2_wo[:, n, :], start=(n == 0), stop=(n == REP - 1))
                    mm.then_inc(l2_y, 1)

                scores(0)
                for u in range(U):
                    if u + 1 < U:
                        scores(u + 1)
                    if u % 2 == 0 and u >= 2:
                        values(u // 2 - 1)
                    turn(u)
                    if u == REP:
                        output(0)
                values(U // 2 - 1)
                output(1)

        L2_DVE_STEPS = 7 + 2 * U
        moe_prepare("L2", 2, 5)

        ln_l3x = norm_plan(True, False)
        l3 = ExitStack()
        W3 = 4 * D3
        l3_ctx = sb("l3_ctx", [P, DC, M], F32, l3)
        l3_wkv = sb("l3_wkv", [P, DC, 2 * D], F32, l3)
        l3_wq = sb("l3_wq", [P, DC, D], F32, l3)
        l3_xb = sb("l3_xb", [P, DC, S], F32, l3)
        l3_raw = [sb(f"l3_raw{n}", [P, D], F32, l3) for n in range(3)]
        l3_sq = [sb(f"l3_sq{n}", [P, D], F32, l3) for n in range(2)]
        l3_n = [sb(f"l3_n{n}", [P, D], F32, l3) for n in range(2)]
        l3_ms = [sb(f"l3_ms{n}", [P, H3], F32, l3) for n in range(2)]
        l3_rs = [sb(f"l3_rs{n}", [P, H3], F32, l3) for n in range(2)]
        l3_pairs = [sb(f"l3_pairs{n}", [P, H3, 4, D3], F16, l3) for n in range(2)]
        l3_v = sb("l3_v", [P, MC, H3, 32], F32, l3)
        l3_kT = sb("l3_kT", [P, NG, M], F16, l3)
        l3_qT = sb("l3_qT", [P, NG, HG, S], F16, l3)
        l3_p = [sb(f"l3_p{n}", [P, HG * S], F32, l3) for n in range(3)]
        l3_o = [sb(f"l3_o{n}", [P, S], F32, l3) for n in range(2)]
        l3_rec = sb("l3_rec", [P, TB, HG], F32, l3)
        l3_y = sb("l3_y", [P, TB, HG, D3], F32, l3)
        l3.close()
        (l3_cland, l3_wland, l3_init, l3_xbd, l3_kv, l3_kvd, l3_msd, l3_rsd, l3_pd, l3_T, l3_Td, l3_s, l3_e, l3_pv,
         l3_od, l3_oT) = (sem(n) for n in (
             "l3_cland l3_wland l3_init l3_xbd l3_kv l3_kvd l3_msd l3_rsd l3_pd l3_T l3_Td l3_s l3_e l3_pv "
             "l3_od l3_oT").split())
        N3 = MC + TB
        C3 = NG * MC

        def rows3(j):
            return chunk_rows(j) if j < MC else P

        def l3x_sync(sp):
            sp.wait_ge(x_upd, X_AT[6])
            sp.dma_start(l3_wkv[:, :, :], t["L3_kv"]).then_inc(l3_wland, 16)
            sp.dma_start(l3_wq[:, :, :], t["L3_q"]).then_inc(l3_wland, 16)
            with sp.Fori(0, B) as b:
                sp.wait_ge(l3_kv, b * N3)
                sp.dma_start(l3_ctx[:, :, :], t["ctx_T"][bass.ds(b, 1)].rearrange("o p c m -> p (o c) m"))\
                    .then_inc(l3_cland, 16)

        def l3x_pool(g):
            g.wait_ge(x_upd, X_AT[6])
            pool_steps.then(g, g.memset(l3_v[:, :, :, :], 0.0))
            g.memset(l3_v[:, :, :, D3:D3 + 1], 1.0).then_inc(l3_init, 1)
            g.memset(l3_qT[:, :, :, :], 0.0).then_inc(l3_init, 1)
            with g.Fori(0, B) as b:
                for j in range(N3):
                    g.wait_ge(l3_msd, b * N3 + (j + 1))
                    g.tensor_tensor(l3_rs[j % 2][:, :], l3_ms[j % 2][:, :], half_power[:, 0:H3], ALU.pow).then_inc(l3_rsd, 1)

        def l3x_scalar(act):
            norm_scalar(act, ln_l3x)
            act.preload_act_table(ACT.Exp)
            act.wait_ge(xT_cp, ln_l3x["cp_end"])
            act.wait_ge(l3_init, 2)
            with act.Fori(0, B) as b:
                act.wait_ge(l3_kv, b * N3)
                act.activation(l3_xb[:, :, :], xT[:, :, bass.ds(b * S, S)], ACT.Copy).then_inc(l3_xbd, 1)

                def project(j):
                    r = rows3(j)
                    act.wait_ge(l3_kv, b * N3 + (j + 1))
                    if j >= 3:
                        act.wait_ge(l3_pd, b * N3 + (j - 2))
                    ins = act.activation(l3_raw[j % 3][0:r, :], bank(6 + j % 2, D)[0:r, :], ACT.Copy)
                    if j < MC:
                        ins.then_inc(l3_kvd, 1)
                        ins = act.activation(l3_v[0:r, j, :, 0:D3],
                                             bank(6 + j % 2, D, D)[0:r, :].rearrange("p (h d) -> p h d", d=D3), ACT.Copy)
                        ins.then_inc(l3_kvd, 1)
                    else:
                        ins.then_inc(l3_kvd, 2)

                def turned(j):
                    r = rows3(j)
                    act.wait_ge(l3_T, b * N3 + (j + 1))
                    src = bank(4 + j % 2).bitcast(F16).rearrange("p (g m) -> p g m", g=NG)
                    if j < MC:
                        act.activation(l3_kT[:, :, j * P:j * P + r], src[:, :, 0:r], ACT.Copy).then_inc(l3_Td, 1)
                    else:
                        k = j - MC
                        for n in range(HG):
                            part = slice(n * W3, (n + 1) * W3)
                            ins = act.activation(l3_qT[part, :, n, k * P:(k + 1) * P], src[part, :, :], ACT.Copy)
                        ins.then_inc(l3_Td, 1)

                for j in range(N3 + 2):
                    if j < N3:
                        project(j)
                    if j >= 2:
                        turned(j - 2)
                for i in range(C3):
                    r = chunk_rows(i % MC)
                    act.wait_ge(l3_s, b * C3 + (i + 1))
                    if i >= 3:
                        act.wait_ge(l3_pv, b * C3 + (i - 2))
                    act.activation(l3_p[i % 3][0:r, :], psum[0:r, (i % 2) * 2 * BANK:(i % 2 + 1) * 2 * BANK], ACT.Exp,
                                   scale=float(D3) ** -0.5).then_inc(l3_e, 1)

        def l3x_vector(v):
            v.wait_ge(x_upd, X_AT[6])
            for n in range(3):
                ins = v.memset(l3_raw[n][:, :], 0.0)
            dve_steps.then(v, ins)
            norm_vector(v, ln_l3x, x)
            with v.Fori(0, B) as b:
                dve_steps.enter(b, 4 * N3 + 2 * NG)

                def squares(j):
                    v.wait_ge(l3_kvd, b * (2 * N3) + (2 * j + 1))
                    raw = l3_raw[j % 3][:, :]
                    dve_steps.then(v, v.tensor_tensor(l3_sq[j % 2][:, :], raw, raw, ALU.mult))
                    dve_steps.then(v, v.tensor_reduce(l3_ms[j % 2][:, :], l3_sq[j % 2][:, :].rearrange("p (h d) -> p h d", d=D3),
                                                      AX.X, ALU.add))
                    v.tensor_scalar(l3_ms[j % 2][:, :], l3_ms[j % 2][:, :], 1.0 / D3, RMS_EPS, ALU.mult, ALU.add)\
                        .then_inc(l3_msd, 1)

                def pair(j):
                    v.wait_ge(l3_rsd, b * N3 + (j + 1))
                    norm = l3_n[j % 2][:, :].rearrange("p (h d) -> p h d", d=D3)
                    dve_steps.then(v, v.tensor_tensor(norm, l3_raw[j % 3][:, :].rearrange("p (h d) -> p h d", d=D3),
                                                      l3_rs[j % 2][:, :].unsqueeze(2).to_broadcast([P, H3, D3]), ALU.mult))
                    if j >= 2:
                        v.wait_ge(l3_T, b * N3 + (j - 1))
                    both = norm.unsqueeze(2).to_broadcast([P, H3, 2, D3])
                    pairs = l3_pairs[j % 2]
                    hi, lo = (pairs[:, :, 0::2, :], pairs[:, :, 1::2, :]) if j < MC else (pairs[:, :, 0:2, :], pairs[:, :, 2:4, :])
                    dve_steps.then(v, v.tensor_copy(hi, both))
                    v.tensor_tensor(lo, both, hi, ALU.subtract).then_inc(l3_pd, 1)

                for j in range(N3 + 1):
                    if j < N3:
                        squares(j)
                    if j >= 1:
                        pair(j - 1)
                for n in range(NG):
                    v.wait_ge(l3_pv, b * C3 + (n + 1) * MC)
                    v.tensor_copy(l3_o[n % 2][:, :], bank(4 + n % 2, S)).then_inc(l3_od, 1)
                    v.wait_ge(l3_oT, b * NG + (n + 1))
                    got = bank(6, TB * P).rearrange("p (k h d) -> p k h d", k=TB, h=HG)
                    dve_steps.then(v, v.reciprocal(l3_rec[:, :, :], got[:, :, :, D3]))
                    dve_steps.then(v, v.tensor_tensor(l3_y[:, :, :, :], got[:, :, :, 0:D3],
                                                      l3_rec[:, :, :].unsqueeze(3).to_broadcast([P, TB, HG, D3]), ALU.mult))
                    row = x[:, bass.ds(b * TB, TB), n * HG * D3:(n + 1) * HG * D3]
                    v.tensor_tensor(row, row, l3_y[:, :, :, :].rearrange("p k h d -> p k (h d)"), ALU.add).then_inc(x_upd, 1)
            dve_steps.leave(B)

        def l3x_tensor(pe):
            norm_tensor(pe, ln_l3x)
            pe.wait_ge(l3_wland, 32)
            with pe.Fori(0, B) as b:
                pe.wait_ge(l3_cland, b * 16 + 16)
                pe.wait_ge(l3_xbd, b + 1)
                pe.wait_ge(x_upd, b * NG + X_AT[6])

                def project(j):
                    r = rows3(j)
                    if j >= 2:
                        pe.wait_ge(l3_kvd, b * (2 * N3) + 2 * (j - 1))
                    width = 2 * D if j < MC else D
                    for c in range(DC):
                        lhs = l3_ctx[:, c, j * P:j * P + r] if j < MC else l3_xb[:, c, (j - MC) * P:(j - MC + 1) * P]
                        mm = pe.matmul(bank(6 + j % 2, width)[0:r, :], lhs, (l3_wkv if j < MC else l3_wq)[:, c, :],
                                       start=(c == 0), stop=(c == DC - 1))
                    mm.then_inc(l3_kv, 1)

                def turn(j):
                    pe.wait_ge(l3_pd, b * N3 + (j + 1))
                    if j >= 2:
                        pe.wait_ge(l3_Td, b * N3 + (j - 1))
                    dst = bank(4 + j % 2).bitcast(F16)
                    src = l3_pairs[j % 2][:, :, :, :].rearrange("p h a d -> p (h a d)")
                    for n in range(NG):
                        mm = pe.transpose(dst[:, n * P:(n + 1) * P], src[:, n * P:(n + 1) * P], identh[:, :])
                    mm.then_inc(l3_T, 1)

                def scores(i):
                    n, j = i // MC, i % MC
                    r = chunk_rows(j)
                    if i >= 2:
                        pe.wait_ge(l3_e, b * C3 + (i - 1))
                    for a in range(2):
                        mm = pe.matmul(bank(i % 2 * 2 + a)[0:r, :], l3_kT[:, n, j * P:j * P + r],
                                       l3_qT[:, n, 2 * a:2 * a + 2, :].rearrange("p h s -> p (h s)"), start=True, stop=True)
                    mm.then_inc(l3_s, 1)

                def values(i):
                    n, j = i // MC, i % MC
                    r = chunk_rows(j)
                    pe.wait_ge(l3_e, b * C3 + (i + 1))
                    if j == 0 and n >= 2:
                        pe.wait_ge(l3_od, b * NG + (n - 1))
                    for a in range(HG):
                        mm = pe.matmul(bank(4 + n % 2, S)[a * 32:(a + 1) * 32, :], l3_v[0:r, j, n * HG + a, :],
                                       l3_p[i % 3][0:r, a * S:(a + 1) * S], start=(j == 0), stop=(j == MC - 1))
                    mm.then_inc(l3_pv, 1)

                def out(n):
                    pe.wait_ge(l3_od, b * NG + (n + 1))
                    if n >= 1:
                        pe.wait_ge(x_upd, b * NG + (n + X_AT[6]))
                    for k in range(TB):
                        mm = pe.transpose(bank(6, P, k * P), l3_o[n % 2][:, k * P:(k + 1) * P], ident[:, :])
                    mm.then_inc(l3_oT, 1)

                for j in range(N3 + 2):
                    if j < N3:
                        project(j)
                    if j >= 2:
                        turn(j - 2)
                pe.wait_ge(l3_Td, (b + 1) * N3)
                scores(0)
                for i in range(C3):
                    if i + 1 < C3:
                        scores(i + 1)
                    values(i)
                    if i % MC == 2 and i >= MC:
                        out(i // MC - 1)
                out(NG - 1)

        ln_l3f = norm_plan(False, False)
        MAGIC = 1.5 * 2 ** 23
        FC = FF3 // P
        f3 = ExitStack()
        f3_w = [sb(f"f3_w{n}", [P, DC * FF3], F32, f3) for n in range(3)]
        f3_wq = [sb(f"f3_wq{n}", [P, DC * FF3], BF16, f3) for n in range(3)]
        f3_wsum = sb("f3_wsum", [P, 3], F32, f3)
        f3_ws, f3_wr = sb("f3_ws", [P, 3], F32, f3), sb("f3_wr", [P, 3], F32, f3)
        f3_xmax, f3_xs, f3_xr = (sb(f"f3_x{n}", [P, NT], F32, f3) for n in ("max", "s", "r"))
        f3_sg, f3_su = sb("f3_sg", [P, NT], F32, f3), sb("f3_su", [P, NT], F32, f3)
        f3_xq = sb("f3_xq", [P, NT, D], F32, f3)
        f3_xb = sb("f3_xb", [P, NT, D], BF16, f3)
        f3_xT = sb("f3_xT", [P, DC, NTOK], BF16, f3)
        f3_g = [sb(f"f3_g{n}", [P, FF3], F32, f3) for n in range(2)]
        f3_h = [sb(f"f3_h{n}", [P, FF3], F32, f3) for n in range(2)]
        f3_hb = [sb(f"f3_hb{n}", [P, FF3], BF16, f3) for n in range(2)]
        f3_hT = [sb(f"f3_hT{n}", [P, FC, P], BF16, f3) for n in range(2)]
        f3_hmax, f3_hs, f3_hr = (sb(f"f3_h{n}", [P, TB], F32, f3) for n in ("max", "s", "r"))
        f3_hd = sb("f3_hd", [P, TB], F32, f3)
        f3_sgt, f3_sut = sb("f3_sgt", [P, TB], F32, f3), sb("f3_sut", [P, TB], F32, f3)
        f3.close()
        f3_wland = sems("f3_wland", 3)
        (f3_wsumd, f3_wtot, f3_wqd, f3_xbd, f3_xTp, f3_xTd, f3_scd, f3_gu, f3_gd, f3_hq, f3_hbd, f3_hTp, f3_hTd,
         f3_dn) = (sem(n) for n in (
             "f3_wsumd f3_wtot f3_wqd f3_xbd f3_xTp f3_xTd f3_scd f3_gu f3_gd f3_hq f3_hbd f3_hTp f3_hTd "
             "f3_dn").split())

        def l3f_sync(sp):
            sp.wait_ge(x_upd, X_AT[7])
            for n, name in enumerate(("L3_gate", "L3_up", "L3_down")):
                sp.dma_start(f3_w[n][:, :], t[name].rearrange("p c n -> p (c n)")).then_inc(f3_wland[n], 16)
            with sp.Fori(0, B) as b:
                sp.wait_ge(x_upd, b * TB + (X_AT[7] + TB))
                sp.dma_start(out[bass.ds(b, 1)].rearrange("o (k p) d -> p (o k) d", p=P), x[:, bass.ds(b * TB, TB), :])\
                    .then_inc(out_done, 16)
            sp.wait_ge(out_done, 16 * B)

        def l3f_pool(g):
            pass

        def l3f_vector(v):
            v.wait_ge(x_upd, X_AT[7])
            for n in range(3):
                v.wait_ge(f3_wland[n], 16)
                v.tensor_reduce(f3_wsum[:, n:n + 1], f3_w[n][:, :], AX.X, ALU.add, apply_absolute_value=True)\
                    .then_inc(f3_wsumd, 1)
            norm_vector(v, ln_l3f, x)
            v.wait_ge(xn_done, NT * (ln_l3f["k"] + 1))
            dve_steps.then(v, v.tensor_reduce(f3_xmax[:, :], xn[:, :, :], AX.X, ALU.max, apply_absolute_value=True))
            dve_steps.then(v, v.tensor_scalar(f3_xs[:, :], f3_xmax[:, :], 1.0 / 127, 1e-5, ALU.mult, ALU.add))
            dve_steps.then(v, v.reciprocal(f3_xr[:, :], f3_xs[:, :]))
            for n in range(NT):
                ins = v.tensor_scalar(f3_xq[:, n, :], xn[:, n, :], f3_xr[:, n:n + 1], MAGIC, ALU.mult, ALU.add)
            dve_steps.then(v, ins)
            dve_steps.then(v, v.tensor_scalar(f3_xq[:, :, :], f3_xq[:, :, :], MAGIC - 128, MAGIC + 127, ALU.max, ALU.min))
            v.tensor_scalar(f3_xb[:, :, :], f3_xq[:, :, :], MAGIC, None, ALU.subtract).then_inc(f3_xbd, 1)
            v.wait_ge(f3_wtot, 1)
            dve_steps.then(v, v.tensor_scalar(f3_ws[:, :], bank(6, 3), 1.0 / (D * FF3), 1e-5, ALU.mult, ALU.add))
            dve_steps.then(v, v.reciprocal(f3_wr[:, :], f3_ws[:, :]))
            for n in range(3):
                dve_steps.then(v, v.tensor_scalar(f3_w[n][:, :], f3_w[n][:, :], f3_wr[:, n:n + 1], MAGIC, ALU.mult, ALU.add))
                dve_steps.then(v, v.tensor_scalar(f3_w[n][:, :], f3_w[n][:, :], MAGIC - 1, MAGIC + 1, ALU.max, ALU.min))
                v.tensor_scalar(f3_wq[n][:, :], f3_w[n][:, :], MAGIC, None, ALU.subtract).then_inc(f3_wqd, 1)
            v.tensor_scalar(f3_sg[:, :], f3_xs[:, :], f3_ws[:, 0:1], None, ALU.mult)
            dve_steps.then(v, v.tensor_scalar(f3_su[:, :], f3_xs[:, :], f3_ws[:, 1:2], None, ALU.mult))
            for hf in range(2):
                for c in range(DC):
                    if c == 0:
                        v.wait_ge(f3_xTp, hf + 1)
                    v.tensor_copy(f3_xT[:, c, hf * HALF:(hf + 1) * HALF], bank(2 * c + hf).bitcast(BF16)[:, 0:HALF])\
                        .then_inc(f3_xTd, 1)
            with v.Fori(0, B) as b:
                dve_steps.enter(b, TB * 5)
                for k in range(TB):
                    n = b * TB + k
                    v.tensor_copy(f3_sgt[:, k:k + 1], f3_sg[:, bass.ds(n, 1)])
                    v.tensor_copy(f3_sut[:, k:k + 1], f3_su[:, bass.ds(n, 1)]).then_inc(f3_scd, 1)
                for k in range(TB):
                    v.wait_ge(f3_scd, (b + 1) * TB)
                    v.wait_ge(f3_gd, b * TB + (k + 1))
                    dve_steps.then(v, v.scalar_tensor_tensor(f3_h[k][:, :], psum[:, 2 * BANK:4 * BANK], f3_sut[:, k:k + 1],
                                                             f3_g[k][:, :], ALU.mult, ALU.mult))
                    dve_steps.then(v, v.tensor_reduce(f3_hmax[:, k:k + 1], f3_h[k][:, :], AX.X, ALU.max, apply_absolute_value=True))
                    dve_steps.then(v, v.tensor_scalar(f3_hs[:, k:k + 1], f3_hmax[:, k:k + 1], 1.0 / 127, 1e-5, ALU.mult, ALU.add))
                    v.tensor_scalar(f3_hd[:, k:k + 1], f3_hs[:, k:k + 1], f3_ws[:, 2:3], None, ALU.mult)
                    dve_steps.then(v, v.reciprocal(f3_hr[:, k:k + 1], f3_hs[:, k:k + 1]))
                    dve_steps.then(v, v.tensor_scalar(f3_h[k][:, :], f3_h[k][:, :], f3_hr[:, k:k + 1], MAGIC, ALU.mult, ALU.add))
                    v.tensor_scalar(f3_h[k][:, :], f3_h[k][:, :], MAGIC - 128, MAGIC + 127, ALU.max, ALU.min).then_inc(f3_hq, 1)
                for k in range(TB):
                    v.wait_ge(f3_dn, b * TB + (k + 1))
                    row = x[:, bass.ds(b * TB + k, 1), :].rearrange("p o d -> p (o d)")
                    v.scalar_tensor_tensor(row, bank(6 + k, D), f3_hd[:, k:k + 1], row, ALU.mult, ALU.add).then_inc(x_upd, 1)
            dve_steps.leave(B)

        def l3f_scalar(act):
            act.preload_act_table(ACT.Silu)
            with act.Fori(0, B) as b:
                for k in range(TB):
                    act.wait_ge(f3_scd, (b + 1) * TB)
                    act.wait_ge(f3_gu, b * TB + (k + 1))
                    act.activation(f3_g[k][:, :], psum[:, 0:2 * BANK], ACT.Silu, scale=f3_sgt[:, k:k + 1]).then_inc(f3_gd, 1)
                for k in range(TB):
                    act.wait_ge(f3_hq, b * TB + (k + 1))
                    act.activation(f3_hb[k][:, :], f3_h[k][:, :], ACT.Copy, bias=-MAGIC).then_inc(f3_hbd, 1)
                    act.wait_ge(f3_hTp, b * TB + (k + 1))
                    act.activation(f3_hT[k][:, :, :].rearrange("p c n -> p (c n)"), bank(4 + k).bitcast(BF16), ACT.Copy)\
                        .then_inc(f3_hTd, 1)

        def l3f_tensor(pe):
            pe.wait_ge(f3_wsumd, 3)
            pe.wait_ge(x_upd, X_AT[7])
            pe.matmul(bank(6, 3), ones[:, :], f3_wsum[:, :], start=True, stop=True).then_inc(f3_wtot, 1)
            pe.wait_ge(f3_xbd, 1)
            for n in range(NT):
                for c in range(DC):
                    mm = pe.transpose(bank(2 * c + n // 4).bitcast(BF16)[:, n % 4 * P:(n % 4 + 1) * P],
                                      f3_xb[:, n, c * P:(c + 1) * P], identb[:, :])
                if n % 4 == 3:
                    mm.then_inc(f3_xTp, 1)
            pe.wait_ge(f3_xTd, 2 * DC)
            pe.wait_ge(f3_wqd, 3)
            gate, up = (f3_wq[n][:, :].rearrange("p (c f) -> p c f", c=DC) for n in range(2))
            down = f3_wq[2][:, :].rearrange("p (c d) -> p c d", c=FC)
            with pe.Fori(0, B) as b:
                for k in range(TB):
                    pe.wait_ge(f3_hq, b * TB + k)
                    for w, at in ((gate, 0), (up, 2)):
                        for a in range(2):
                            for c in range(DC):
                                mm = pe.matmul(bank(at + a), f3_xT[:, c, bass.ds(b * S + k * P, P)],
                                               w[:, c, a * BANK:(a + 1) * BANK], start=(c == 0), stop=(c == DC - 1))
                    mm.then_inc(f3_gu, 1)
                for k in range(TB):
                    pe.wait_ge(f3_hbd, b * TB + (k + 1))
                    for c in range(FC):
                        mm = pe.transpose(bank(4 + k).bitcast(BF16)[:, c * P:(c + 1) * P], f3_hb[k][:, c * P:(c + 1) * P],
                                          identb[:, :])
                    mm.then_inc(f3_hTp, 1)
                    pe.wait_ge(f3_hTd, b * TB + (k + 1))
                    for c in range(FC):
                        mm = pe.matmul(bank(6 + k, D), f3_hT[k][:, c, :], down[:, c, :], start=(c == 0), stop=(c == FC - 1))
                    mm.then_inc(f3_dn, 1)

        block = stack.enter_context(nc.Block())

        @block.sync
        def _(sp):
            sp.dma_start(x[:, :, :], t["x"].rearrange("b (k p) d -> p (b k) d", p=P)).then_inc(x_land, 16)
            l0x_sync(sp)
            moe_sync(sp, "L0")
            moe_sync(sp, "L1")
            l2x_sync(sp)
            moe_sync(sp, "L2")
            l3x_sync(sp)
            l3f_sync(sp)

        @block.gpsimd
        def _(g):
            constants_pool(g)
            norm_pool(g, ln_l0x)
            norm_pool(g, moe_plan["L0"]["ln"])
            moe_pool(g, "L0")
            norm_pool(g, ln_l1z)
            norm_pool(g, ln_l1y)
            norm_pool(g, moe_plan["L1"]["ln"])
            moe_pool(g, "L1")
            norm_pool(g, ln_l2x)
            l2x_pool(g)
            norm_pool(g, moe_plan["L2"]["ln"])
            moe_pool(g, "L2")
            norm_pool(g, ln_l3x)
            l3x_pool(g)
            norm_pool(g, ln_l3f)
            l3f_pool(g)

        @block.scalar
        def _(act):
            parameters_scalar(act)
            norm_scalar(act, ln_l0x)
            l0x_scalar(act)
            moe_scalar(act, "L0")
            l1x_scalar(act)
            moe_scalar(act, "L1")
            l2x_scalar(act)
            moe_scalar(act, "L2")
            l3x_scalar(act)
            l3f_scalar(act)

        @block.vector
        def _(v):
            v.wait_ge(x_land, 16)
            norm_vector(v, ln_l0x, x)
            l0x_vector(v)
            moe_vector(v, "L0")
            l1x_vector(v)
            moe_vector(v, "L1")
            l2x_vector(v)
            moe_vector(v, "L2")
            l3x_vector(v)
            l3f_vector(v)

        @block.tensor
        def _(pe):
            pe.wait_ge(consts, NCONST)
            norm_tensor(pe, ln_l0x)
            l0x_tensor(pe)
            moe_tensor(pe, "L0")
            l1x_tensor(pe)
            moe_tensor(pe, "L1")
            l2x_tensor(pe)
            moe_tensor(pe, "L2")
            l3x_tensor(pe)
            l3f_tensor(pe)


def kernel(**inputs):
    import numpy as _np
    import ml_dtypes as _ml
    import concourse.bacc as _bacc
    from concourse import mybir as _mybir
    from concourse.bass_utils import run_bass_kernel_spmd as _run

    a = {k: _np.asarray(v) for k, v in inputs.items()}

    def width_first(w):
        return w.reshape(w.shape[0], DC, P).transpose(2, 1, 0)

    def expert_chunks(name, gate, up, down):
        n = moe_chunks(name)
        pad = _np.zeros((n * P - gate.shape[0], D), _np.float32)
        full = [_np.concatenate([w, pad]).reshape(n, P, D) for w in (gate, up, down)]
        lhs = [w.reshape(n, P, DC, P).transpose(0, 3, 2, 1).reshape(n, P, DC * P) for w in full[:2]]
        return _np.concatenate([*lhs, full[2]], axis=2)

    def expert_rows(name):
        experts, hidden, shared = MOE[name]
        rows = _np.arange(moe_chunks(name) * P)
        which = _np.where(rows < experts * hidden, rows // hidden, experts)
        one = which[None, :] == _np.arange(experts + (shared > 0))[:, None]
        return _np.concatenate([one] * 3).astype(_ml.bfloat16)

    e0, h0, _ = MOE["L0"]
    e1, h1, s1 = MOE["L1"]
    e2, h2, _ = MOE["L2"]
    ctx = a["ctx_2048"]
    data = {
        "x": a["x"],
        "ctx": ctx,
        "ctx_T": ctx.reshape(B, M, DC, P).transpose(0, 3, 2, 1),
        "mask": a["mask_BxS2_bk0"],
        "L0_w": expert_chunks("L0", a["L0_ffn_w_gate_proj"].reshape(e0 * h0, D),
                              a["L0_ffn_w_up_proj"].reshape(e0 * h0, D),
                              a["L0_ffn_w_down_proj"].transpose(0, 2, 1).reshape(e0 * h0, D)),
        "L0_router": width_first(a["L0_ffn_gate_w"]),
        "L0_rows": expert_rows("L0"),
        "decay": a["L1_xattn_decay"].reshape(1, 1),
        "L1_in": width_first(a["L1_xattn_W_in"]),
        "L1_out": width_first(a["L1_xattn_W_out"]),
        "L1_bin": a["L1_xattn_b_in"].reshape(DC, P).T,
        "L1_bout": a["L1_xattn_b_out"].reshape(DC, P).T,
        "L1_gamma": a["L1_xattn_gamma"].reshape(1, D),
        "L1_beta": a["L1_xattn_beta"].reshape(1, D),
        "L1_w": expert_chunks("L1",
                              _np.concatenate([a["L1_ffn_W1"].transpose(0, 2, 1).reshape(e1 * h1, D), a["L1_ffn_sw1"]]),
                              _np.concatenate([a["L1_ffn_W3"].transpose(0, 2, 1).reshape(e1 * h1, D), a["L1_ffn_sw3"]]),
                              _np.concatenate([a["L1_ffn_W2"].reshape(e1 * h1, D), a["L1_ffn_sw2"].T])),
        "L1_router": width_first(a["L1_ffn_gate_w"]),
        "L1_rbias": a["L1_ffn_router_bias"].reshape(1, e1),
        "L1_rows": expert_rows("L1"),
        "L2_w": expert_chunks("L2", a["L2_ffn_Wg"].transpose(0, 2, 1).reshape(e2 * h2, D),
                              a["L2_ffn_Wu"].transpose(0, 2, 1).reshape(e2 * h2, D),
                              a["L2_ffn_Wd"].reshape(e2 * h2, D)),
        "L2_router": width_first(a["L2_ffn_Wr"].T),
        "L2_rbias": a["L2_ffn_br"].reshape(1, e2),
        "L2_rows": expert_rows("L2"),
    }
    def rope(fn):
        freq = 1.0 / _np.float32(10000.0) ** (_np.arange(0, HD, 2, dtype=_np.float32) / _np.float32(HD))
        angle = _np.outer(_np.arange(S, dtype=_np.float32), freq.astype(_np.float32)).astype(_np.float32)
        return fn(angle).astype(_np.float32).reshape(TB, P, HD // 2).transpose(1, 0, 2)

    def by_head(w, heads):
        return w.reshape(DC, P, KH, heads * HD).transpose(2, 1, 0, 3)

    data.update({
        "rope_cos": rope(_np.cos), "rope_sin": rope(_np.sin),
        "L2_qw": a["L2_xattn_q_norm_w"].reshape(1, HD), "L2_kw": a["L2_xattn_k_norm_w"].reshape(1, HD),
        "L2_kwc": a["L2_xattn_k_norm_w"].reshape(HD, 1),
        "L2_w_qkv": _np.concatenate([by_head(a[f"L2_xattn_{n}"], 1) for n in ("wk_ctx", "wv_ctx", "wk", "wv")]
                                    + [by_head(a["L2_xattn_wq"], REP)], axis=3),
        "L2_wo": a["L2_xattn_wo"].reshape(KH, REP, HD, D).transpose(0, 2, 1, 3),
    })
    wkv3 = _np.concatenate([a["L3_xattn_Wk"], a["L3_xattn_Wv"]])
    data.update({
        "L3_kv": width_first(_np.concatenate([wkv3[0::2], wkv3[1::2]])),
        "L3_q": width_first(a["L3_xattn_Wq"]),
        "L3_gate": width_first(a["L3_ffn_w_gate"]),
        "L3_up": width_first(a["L3_ffn_w_up"]),
        "L3_down": a["L3_ffn_w_down"].T.reshape(FF3 // P, P, D).transpose(1, 0, 2),
    })
    nc = _bacc.Bacc("TRN2", target_bir_lowering=False, num_devices=1)
    arrays, args = {}, {}
    for name, value in data.items():
        value = _np.ascontiguousarray(value)
        arrays[f"in_{name}_dram"] = value
        kind = _mybir.dt.uint8 if value.dtype == bool else _mybir.dt.from_np(value.dtype)
        args[name] = nc.dram_tensor(f"in_{name}_dram", value.shape, kind,
                                    kind="ExternalInput").ap()
    out = nc.dram_tensor("out_0_dram", (B, S, D), _mybir.dt.float32, kind="ExternalOutput").ap()
    program(nc, args, out)
    r = _run(nc, [arrays], core_ids=[0])
    return r.results[0]["out_0_dram"]
```

```python
from contextlib import ExitStack

import numpy as np

import concourse.bass as bass
from concourse import mybir

F32 = mybir.dt.float32
F32R = mybir.dt.float32r
BF16 = mybir.dt.bfloat16
F16 = mybir.dt.float16
U8 = mybir.dt.uint8
ACT = mybir.ActivationFunctionType
ALU = mybir.AluOpType
AX = mybir.AxisListType

P = 128
B, S, D = 4, 256, 256
DC = D // P
TB = S // P
NT = B * TB
NTOK = B * S
M = 1601
MC = -(-M // P)
ML = M - (MC - 1) * P
BANK = 512
HALF = NTOK // 2
LN_EPS = 1e-5
RMS_EPS = 1e-6
BIG = 1e30
LOWEST = -3.0e38

MOE = {"L0": (32, 96, 0), "L1": (8, 176, 352), "L2": (4, 1024, 0)}

QH, KH, HD = 16, 4, 128
REP = QH // KH
H3, D3 = 32, 8
HG = 4
NG = H3 // HG
FF3 = 1024


def chunk_rows(j):
    return P if j < MC - 1 else ML


def moe_chunks(name):
    experts, hidden, shared = MOE[name]
    n = -(-(experts * hidden + shared) // P)
    return n + n % 2


class Steps:

    def __init__(self, sem):
        self.sem, self.base, self.done, self.i, self.per = sem, 0, 0, None, 0

    def then(self, engine, instruction):
        instruction.then_inc(self.sem, 1)
        self.done += 1
        value = self.base + self.done
        engine.wait_ge(self.sem, value if self.i is None else self.i * self.per + value)

    def enter(self, i, per):
        self.base, self.done, self.i, self.per = self.base + self.done, 0, i, per

    def leave(self, turns):
        assert self.done == self.per, (self.done, self.per)
        self.base, self.done, self.i = self.base + turns * self.per, 0, None



def program(nc, t, out):
    with ExitStack() as stack:

        def sem(name):
            return stack.enter_context(nc.semaphore(name))

        def sems(name, n):
            return [sem(f"{name}{i}") for i in range(n)]

        def sb(name, shape, dt=F32, scope=stack):
            return scope.enter_context(nc.sbuf_tensor(name, shape, dt))

        psum = stack.enter_context(nc.psum_tensor("psum", [P, 8 * BANK], F32))

        def bank(n, width=BANK, at=0):
            return psum[:, n * BANK + at:n * BANK + at + width]

        x = sb("x", [P, NT, D])
        xn = sb("xn", [P, NT, D])
        xT = sb("xT", [P, DC, NTOK])
        ident = sb("ident", [P, P])
        identb = sb("identb", [P, P], BF16)
        identh = sb("identh", [P, P], F16)
        half_power = sb("half_power", [P, 2 * HD])
        zerob = sb("zerob", [1, BANK], BF16)
        ones = sb("ones", [P, P])
        stats = sb("stats", [P, NT, 6])
        mv = sb("mv", [P, NT, 2])
        veps = sb("veps", [P, NT])
        rstd = sb("rstd", [P, NT])

        decay_raw = sb("decay_raw", [P, 1])
        decay_k = sb("decay_k", [P, 1])
        decay_sum = sb("decay_sum", [P, DC, B])
        decay_total = sb("decay_total", [P, 1])

        r_earlier = sb("r_earlier", [P, 8, 8])
        l1_in, l1_out = sb("l1_in", [P, DC, D]), sb("l1_out", [P, DC, D])
        l1_bin, l1_bout = sb("l1_bin", [P, DC]), sb("l1_bout", [P, DC])
        l1_gamma, l1_beta = sb("l1_gamma", [P, D]), sb("l1_beta", [P, D])
        causal = sb("causal", [P, BANK], BF16)
        causal_T = sb("causal_T", [P, REP, P], BF16)
        x_land = sem("x_land")
        consts = sem("consts")
        x_upd = sem("x_upd")
        ln_stats, ln_mv, ln_veps, ln_rstd = sem("ln_stats"), sem("ln_mv"), sem("ln_veps"), sem("ln_rstd")
        xn_done = sem("xn_done")
        xT_ps = sem("xT_ps")
        xT_cp = sem("xT_cp")
        xT_lo = sem("xT_lo")
        dve_steps = Steps(sem("dve_steps"))
        pool_steps = Steps(sem("pool_steps"))
        out_done = sem("out_done")
        NCONST = 7

        UPDATES = [NT, NT, NT, NT, 2 * B * KH * TB, NT, B * NG, NT]
        X_AT = [sum(UPDATES[:k]) for k in range(len(UPDATES) + 1)]

        norm_count = {"k": 0, "ps": 0, "cp": 0, "lo": 0}

        def norm_plan(transposed, split):
            at = dict(norm_count, transposed=transposed, split=split)
            norm_count["k"] += 1
            if transposed:
                norm_count["ps"] += 2
                norm_count["cp"] += 4
                if split:
                    norm_count["lo"] += 4
            at["cp_end"], at["lo_end"] = norm_count["cp"], norm_count["lo"]
            return at

        def norm_vector(v, at, src):
            k = at["k"]
            for n in range(NT):
                v.bn_stats(stats[:, n, :], src[:, n, :]).then_inc(ln_stats, 1)
            v.wait_ge(ln_stats, NT * (k + 1))
            for n in range(NT):
                v.bn_aggr(mv[:, n, :], stats[:, n, :]).then_inc(ln_mv, 1)
            v.wait_ge(ln_mv, NT * (k + 1))
            v.tensor_scalar(veps[:, :], mv[:, :, 1], LN_EPS, None, ALU.add).then_inc(ln_veps, 1)
            v.wait_ge(ln_rstd, k + 1)
            for n in range(NT):
                v.tensor_scalar(xn[:, n, :], src[:, n, :], mv[:, n, 0:1], rstd[:, n:n + 1],
                                ALU.subtract, ALU.mult).then_inc(xn_done, 1)
            if at["split"]:
                for q in range(4):
                    hf, c = q // 2, q % 2
                    v.wait_ge(xT_cp, at["cp"] + q + 1)
                    cols = slice(hf * HALF, (hf + 1) * HALF)
                    v.tensor_tensor(xlo[:, c, cols], bank(2 * c + hf), xhi[:, c, cols].bitcast(F32),
                                    ALU.subtract).then_inc(xT_lo, 1)

        def norm_pool(g, at):
            g.wait_ge(ln_veps, at["k"] + 1)
            g.tensor_tensor(rstd[:, :], veps[:, :], half_power[:, 0:NT], ALU.pow).then_inc(ln_rstd, 1)

        def norm_tensor(pe, at):
            for n in range(NT):
                pe.wait_ge(xn_done, NT * at["k"] + n + 1)
                for c in range(DC):
                    last_t = pe.transpose(bank(2 * c + n // 4, P, (n % 4) * P),
                                          xn[:, n, c * P:(c + 1) * P], ident[:, :])
                if n % 4 == 3:
                    last_t.then_inc(xT_ps, 1)

        def norm_scalar(act, at):
            dst = xhi if at["split"] else xT
            for q in range(4):
                hf, c = q // 2, q % 2
                act.wait_ge(xT_ps, at["ps"] + hf + 1)
                act.activation(dst[:, c, hf * HALF:(hf + 1) * HALF], bank(2 * c + hf),
                               ACT.Copy).then_inc(xT_cp, 1)

        ln_l0x = norm_plan(True, False)
        l0 = ExitStack()
        c_T = [sb(f"c_T{s}", [P, DC, M], F32, l0) for s in range(2)]
        c_N = [sb(f"c_N{s}", [P, MC, D], F32, l0) for s in range(2)]
        c_mask = [sb(f"c_mask{s}", [P, M], U8, l0) for s in range(2)]
        c_bias = [sb(f"c_bias{s}", [P, M], F32, l0) for s in range(2)]
        c_any = [sb(f"c_any{s}", [P, 1], F32, l0) for s in range(2)]
        l0_xb = [sb(f"l0_xb{s}", [P, DC, S], F32, l0) for s in range(2)]
        l0_sm = [sb(f"l0_sm{n}", [P, M], F32, l0) for n in range(TB)]
        l0_p = [sb(f"l0_p{n}", [P, M], F32, l0) for n in range(TB)]
        l0_pt = [sb(f"l0_pt{n}", [P, MC, P], F32, l0) for n in range(TB)]
        l0_mx = sb("l0_mx", [P, TB], F32, l0)
        l0_nmx = sb("l0_nmx", [P, TB], F32, l0)
        l0_sum = sb("l0_sum", [P, TB], F32, l0)
        l0_rec = sb("l0_rec", [P, TB], F32, l0)
        l0_top = sb("l0_top", [P, 1], F32, l0)
        l0_gate = sb("l0_gate", [P, TB], F32, l0)
        decay_geo = sb("decay_geo", [P, M], F32, l0)
        decay_junk = sb("decay_junk", [P, M], F32, l0)
        decay_tmp = [sb(f"decay_tmp{s}", [P, DC], F32, l0) for s in range(2)]
        l0.close()
        c_land = sems("c_land", 2)
        decay_land, decay_sig = sem("decay_land"), sem("decay_sig")
        l0_xbd, l0_s, l0_masked, l0_shift = sem("l0_xbd"), sem("l0_s"), sem("l0_masked"), sem("l0_shift")
        l0_exp, l0_T, l0_ptd = sem("l0_exp"), sem("l0_T"), sem("l0_ptd")
        l0_pv = sems("l0_pv", 2)
        l0_decayed = sems("l0_decayed", 2)
        TG = -(-MC // 4)

        def l0x_sync(sp):
            with sp.Fori(0, B // 2) as i:
                for s in range(2):
                    n = i * 2 + s
                    sp.wait_ge(l0_pv[s], i * TB)
                    sp.wait_ge(l0_decayed[s], i)
                    one = bass.ds(n, 1)
                    sp.dma_start(c_T[s][:, :, :], t["ctx_T"][one].rearrange("o p c m -> p (o c) m"))\
                        .then_inc(c_land[s], 16)
                    sp.dma_start(c_mask[s][:, :], t["mask"][one, :].to_broadcast([P, M]))\
                        .then_inc(c_land[s], 16)
                    sp.dma_start(c_N[s][:, 0:MC - 1, :],
                                 t["ctx"][one, 0:(MC - 1) * P, :].rearrange("o (j p) d -> p (o j) d", p=P))\
                        .then_inc(c_land[s], 16)
                    sp.dma_start(c_N[s][0:ML, MC - 1, :],
                                 t["ctx"][one, (MC - 1) * P:M, :].rearrange("o p d -> p (o d)"))\
                        .then_inc(c_land[s], 16)

        def l0x_scalar(act):
            act.wait_ge(decay_land, 16)
            act.activation(decay_k[:, :], decay_raw[:, :], ACT.Sigmoid).then_inc(decay_sig, 1)
            act.preload_act_table(ACT.Exp)
            act.wait_ge(xT_cp, ln_l0x["cp_end"])
            with act.Fori(0, B // 2) as i:
                for s in range(2):
                    n = i * 2 + s
                    act.activation(l0_xb[s][:, :, :], xT[:, :, bass.ds(n * S, S)], ACT.Copy)\
                        .then_inc(l0_xbd, 1)
                    for k in range(TB):
                        act.wait_ge(l0_shift, i * 4 + 2 * s + k + 1)
                        act.activation(l0_p[k][:, :], l0_sm[k][:, :], ACT.Exp, bias=l0_nmx[:, k:k + 1],
                                       accum_out=l0_sum[:, k:k + 1]).then_inc(l0_exp, 1)
                    for k in range(TB):
                        for q in range(TG):
                            act.wait_ge(l0_T, (i * 4 + 2 * s + k) * TG + q + 1)
                            if q < TG - 1:
                                ins = act.activation(l0_pt[k][:, 4 * q:4 * q + 4, :], bank(4 + q % 2), ACT.Copy)
                            else:
                                ins = act.activation(l0_pt[k][0:ML, MC - 1, :], bank(4 + q % 2, P)[0:ML, :], ACT.Copy)
                            ins.then_inc(l0_ptd, 1)

        def l0x_vector(v):
            v.wait_ge(decay_sig, 1)
            v.wait_ge(consts, NCONST)
            dve_steps.then(v, v.tensor_tensor_scan(decay_geo[:, :], decay_k[:, 0:1].to_broadcast([P, M]),
                                                   ones[:, 0:1].to_broadcast([P, M]), 0.0, ALU.mult, ALU.add))
            dve_steps.then(v, v.tensor_reduce(decay_total[:, :], decay_geo[:, :], AX.X, ALU.add))
            with v.Fori(0, B // 2) as i:
                dve_steps.enter(i, 2 * (5 + 2 * TB))
                for s in range(2):
                    n = i * 2 + s
                    v.wait_ge(c_land[s], 64 * (i + 1))
                    dve_steps.then(v, v.tensor_scalar(c_bias[s][:, :], c_mask[s][:, :], 16 * BIG, -16 * BIG,
                                                      ALU.mult, ALU.add))
                    dve_steps.then(v, v.tensor_reduce(l0_top[:, :], c_bias[s][:, :], AX.X, ALU.max))
                    dve_steps.then(v, v.tensor_scalar(c_any[s][:, :], l0_top[:, :], -1.0, None, ALU.is_ge))
                    for k in range(TB):
                        v.wait_ge(l0_s, i * 4 + 2 * s + k + 1)
                        v.memset(l0_gate[:, k:k + 1], 0.0)
                        v.tensor_tensor_reduce(l0_sm[k][:, :], psum[:, 0:M], c_bias[s][:, :], 1.0 / 16, LOWEST,
                                               ALU.add, ALU.max, l0_mx[:, k:k + 1]).then_inc(l0_masked, 1)
                        v.wait_ge(l0_masked, i * 4 + 2 * s + k + 1)
                        v.tensor_scalar(l0_nmx[:, k:k + 1], l0_mx[:, k:k + 1], -1.0, None, ALU.mult)\
                            .then_inc(l0_shift, 1)
                    for c in range(DC):
                        ins = v.tensor_tensor_reduce(decay_junk[:, :], c_T[s][:, c, :], decay_geo[:, ::-1], 1.0, 0.0,
                                                     ALU.mult, ALU.add, decay_tmp[s][:, c:c + 1])
                        dve_steps.then(v, ins)
                    v.tensor_copy(decay_sum[:, :, bass.ds(n, 1)], decay_tmp[s][:, :].rearrange("p (c o) -> p c o", o=1))\
                        .then_inc(l0_decayed[s], 1)
                    for k in range(TB):
                        v.wait_ge(l0_exp, i * 4 + 2 * s + k + 1)
                        dve_steps.then(v, v.reciprocal(l0_rec[:, k:k + 1], l0_sum[:, k:k + 1]))
                        dve_steps.then(v, v.tensor_tensor(l0_rec[:, k:k + 1], l0_rec[:, k:k + 1], c_any[s][:, :], ALU.mult))
                        v.wait_ge(l0_pv[s], i * TB + k + 1)
                        row = x[:, bass.ds(n * TB + k, 1), :].rearrange("p o d -> p (o d)")
                        v.scalar_tensor_tensor(row, bank(6 + k, D), l0_rec[:, k:k + 1], row,
                                               ALU.mult, ALU.add).then_inc(x_upd, 1)
            dve_steps.leave(B // 2)

        def l0x_tensor(pe):
            with pe.Fori(0, B // 2) as i:
                for s in range(2):
                    pe.wait_ge(c_land[s], 64 * (i + 1))
                    pe.wait_ge(l0_xbd, i * 2 + s + 1)
                    for k in range(TB):
                        pe.wait_ge(l0_masked, i * 4 + 2 * s + k)
                        for a in range(0, M, BANK):
                            z = min(a + BANK, M)
                            for c in range(DC):
                                mm = pe.matmul(psum[:, a:z], l0_xb[s][:, c, k * P:(k + 1) * P], c_T[s][:, c, a:z],
                                               start=(c == 0), stop=(c == DC - 1))
                        mm.then_inc(l0_s, 1)
                    for k in range(TB):
                        tile = i * 4 + 2 * s + k
                        pe.wait_ge(l0_exp, tile + 1)
                        for q in range(TG):
                            if q >= 2:
                                pe.wait_ge(l0_ptd, tile * TG + q - 1)
                            for j in range(4 * q, min(4 * q + 4, MC)):
                                r = chunk_rows(j)
                                mm = pe.transpose(bank(4 + q % 2, P, (j % 4) * P)[0:r, :],
                                                  l0_p[k][:, j * P:j * P + r], ident[:, :])
                            mm.then_inc(l0_T, 1)
                        for j in range(MC):
                            if j % 4 == 0:
                                pe.wait_ge(l0_ptd, tile * TG + j // 4 + 1)
                            r = chunk_rows(j)
                            mm = pe.matmul(bank(6 + k, D), l0_pt[k][0:r, j, :], c_N[s][0:r, j, :],
                                           start=(j == 0), stop=(j == MC - 1))
                        mm.then_inc(l0_pv[s], 1)

        def constants_pool(g):
            for tile in (ident, identb, identh):
                pool_steps.then(g, g.memset(tile[:, :], 0.0))
                g.affine_select(out=tile[:, :], in_=tile[:, :], compare_op=ALU.not_equal, fill=1.0,
                                base=0, pattern=[[-1, P]], channel_multiplier=1).then_inc(consts, 1)
            pool_steps.then(g, g.memset(half_power[:, :], -0.5))
            g.memset(ones[:, :], 1.0).then_inc(consts, 1)
            g.memset(zerob[:, :], 0.0).then_inc(consts, 1)
            pool_steps.then(g, g.memset(causal[:, :], 0.0))
            g.affine_select(out=causal[:, BANK - P:], in_=causal[:, BANK - P:], compare_op=ALU.is_ge, fill=-BIG,
                            base=0, pattern=[[-1, P]], channel_multiplier=1).then_inc(consts, 1)
            pool_steps.then(g, g.memset(causal_T[:, :, :], 0.0))
            g.affine_select(out=causal_T[:, :, :], in_=causal_T[:, :, :], compare_op=ALU.is_ge, fill=-BIG,
                            base=0, pattern=[[0, REP], [1, P]], channel_multiplier=-1).then_inc(consts, 1)
            pool_steps.then(g, g.memset(r_earlier[:, :, :], 1.0))
            g.affine_select(out=r_earlier[:, :, :], in_=r_earlier[:, :, :], compare_op=ALU.is_gt, fill=0.0,
                            base=0, pattern=[[1, 8], [-1, 8]], channel_multiplier=0).then_inc(early_done, 1)

        def parameters_scalar(act):
            act.dma_start(decay_raw[:, :], t["decay"].to_broadcast([P, 1])).then_inc(decay_land, 16)
            for dst, name in ((l1_in, "L1_in"), (l1_out, "L1_out"), (l1_bin, "L1_bin"), (l1_bout, "L1_bout")):
                act.dma_start(dst[...], t[name]).then_inc(l1_land, 16)
            for dst, name in ((l1_gamma, "L1_gamma"), (l1_beta, "L1_beta")):
                act.dma_start(dst[:, :], t[name].to_broadcast([P, D])).then_inc(l1_land, 16)

        EMAX = 32
        moe = ExitStack()
        xhi = sb("xhi", [P, DC, NTOK], F32R, moe)
        xlo = sb("xlo", [P, DC, NTOK], F32R, moe)
        w_stage = [sb(f"w_stage{s}", [P, 3 * D], F32, moe) for s in range(2)]
        w_hi_gu = [sb(f"w_hi_gu{s}", [P, 2 * D], F32R, moe) for s in range(2)]
        w_lo_gu = [sb(f"w_lo_gu{s}", [P, 2 * D], F32R, moe) for s in range(2)]
        w_hi_d = [sb(f"w_hi_d{s}", [P, D], F32R, moe) for s in range(2)]
        w_lo_d = [sb(f"w_lo_d{s}", [P, D], F32R, moe) for s in range(2)]
        e_silu = [sb(f"e_silu{s}", [P, HALF], F32, moe) for s in range(2)]
        e_h = [sb(f"e_h{s}", [P, HALF], F32, moe) for s in range(2)]
        e_hhi = [sb(f"e_hhi{s}", [P, HALF], F32R, moe) for s in range(2)]
        e_hlo = [sb(f"e_hlo{s}", [P, HALF], F32R, moe) for s in range(2)]
        e_out = sb("e_out", [P, DC, HALF], F32, moe)
        e_rows = sb("e_rows", [3 * EMAX, max(moe_chunks(n) for n in MOE) * P], BF16, moe)
        r_w = sb("r_w", [P, DC, EMAX], F32, moe)
        r_whi = sb("r_whi", [P, DC, EMAX], F32R, moe)
        r_wlo = sb("r_wlo", [P, DC, EMAX], F32R, moe)
        r_bias = {"L1": sb("r_bias1", [P, 8], F32, moe), "L2": sb("r_bias2", [P, 4], F32, moe)}
        r_log = sb("r_log", [P, NT, EMAX], F32, moe)
        r_a = sb("r_a", [P, NT, EMAX], F32, moe)
        r_b = sb("r_b", [P, NT, EMAX], F32, moe)
        r_top = sb("r_top", [P, NT, 8], F32, moe)
        r_sum = sb("r_sum", [P, NT], F32, moe)
        r_pair = sb("r_pair", [P, NT, 8, 8], F32, moe)
        r_tie = sb("r_tie", [P, NT, 8, 8], F32, moe)
        r_route = sb("r_route", [P, NT, EMAX], F32, moe)
        r_parts = sb("r_parts", [P, NT, 3 * EMAX], BF16, moe)
        r_T = sb("r_T", [3 * EMAX, NTOK], BF16, moe)
        moe.close()

        rows_land, rw_land, rw_split = sem("rows_land"), sem("rw_land"), sem("rw_split")
        rbias_land, early_done = sem("rbias_land"), sem("early_done")
        r_logits, r_in, r_acted, r_done, r_Tps, r_Tcp = (sem(n) for n in (
            "r_logits", "r_in", "r_acted", "r_done", "r_Tps", "r_Tcp"))
        w_land, w_gu, w_d = sems("w_land", 2), sems("w_gu", 2), sems("w_d", 2)
        e_gu, e_act, e_hd, e_down = sems("e_gu", 2), sems("e_act", 2), sems("e_hd", 2), sems("e_down", 2)
        e_acc, e_outd, e_T = sem("e_acc"), sem("e_outd"), sem("e_T")
        G_BANK, U_BANK, R_BANK = (2, 3), (4, 5), (6, 7)

        def three(pe, dst, lhs, rhs, start, stop):
            pe.matmul(dst, lhs[0], rhs[0], start=start, stop=False)
            pe.matmul(dst, lhs[0], rhs[1], start=False, stop=False)
            return pe.matmul(dst, lhs[1], rhs[0], start=False, stop=stop)

        moe_plan = {}

        def moe_prepare(name, index, layer):
            experts, hidden, shared = MOE[name]
            plan = {"ln": norm_plan(True, True), "index": index, "n": moe_chunks(name), "experts": experts,
                    "slots": experts + (shared > 0), "x_at": X_AT[layer],
                    "pairs": sum(moe_chunks(m) for m in list(MOE)[:index])}
            moe_plan[name] = plan

        def moe_sync(sp, name):
            p = moe_plan[name]
            pairs = p["n"] // 2
            sp.wait_ge(x_upd, p["x_at"])
            n3, E = 3 * p["slots"], p["experts"]
            sp.dma_start(e_rows[0:n3, 0:p["n"] * P], t[f"{name}_rows"]).then_inc(rows_land, 16)
            sp.dma_start(r_w[:, :, 0:E], t[f"{name}_router"]).then_inc(rw_land, 16)
            if name in r_bias:
                sp.dma_start(r_bias[name][:, :], t[f"{name}_rbias"].to_broadcast([P, E])).then_inc(rbias_land, 16)
            for hf in range(2):
                m0 = p["pairs"] + hf * pairs
                with sp.Fori(0, pairs) as i:
                    for s in range(2):
                        sp.wait_ge(w_d[s], i + m0)
                        sp.dma_start(w_stage[s][:, :], t[f"{name}_w"][bass.ds(i * 2 + s, 1)]
                                     .rearrange("o p n -> p (o n)")).then_inc(w_land[s], 16)

        def moe_pool(g, name):
            p = moe_plan[name]
            pairs = p["n"] // 2
            for hf in range(2):
                m0 = p["pairs"] + hf * pairs
                with g.Fori(0, pairs) as i:
                    pool_steps.enter(i, 4)
                    for s in range(2):
                        g.wait_ge(w_land[s], i * 16 + 16 * (m0 + 1))
                        g.wait_ge(e_gu[s], i + m0)
                        gu = w_stage[s][:, 0:2 * D]
                        pool_steps.then(g, g.tensor_tensor(w_hi_gu[s][:, :], gu, ones[:, 0:1].to_broadcast([P, 2 * D]), ALU.mult))
                        g.tensor_tensor(w_lo_gu[s][:, :], gu, w_hi_gu[s][:, :].bitcast(F32), ALU.subtract)\
                            .then_inc(w_gu[s], 1)
                        g.wait_ge(e_down[s], i + m0)
                        d = w_stage[s][:, 2 * D:3 * D]
                        pool_steps.then(g, g.tensor_tensor(w_hi_d[s][:, :], d, ones[:, 0:1].to_broadcast([P, D]), ALU.mult))
                        g.tensor_tensor(w_lo_d[s][:, :], d, w_hi_d[s][:, :].bitcast(F32), ALU.subtract)\
                            .then_inc(w_d[s], 1)
                pool_steps.leave(pairs)

        def moe_scalar(act, name):
            p = moe_plan[name]
            norm_scalar(act, p["ln"])
            k, E = p["index"], p["experts"]
            act.wait_ge(r_in, k + 1)
            if name == "L0":
                act.activation(r_a[:, :, 0:E], r_a[:, :, 0:E], ACT.Exp)
                act.activation(r_b[:, :, 0:E], r_b[:, :, 0:E], ACT.Exp).then_inc(r_acted, 1)
            else:
                act.activation(r_a[:, :, 0:E], r_log[:, :, 0:E], ACT.Sigmoid if name == "L1" else ACT.Exp)\
                    .then_inc(r_acted, 1)
            pairs = p["n"] // 2
            act.preload_act_table(ACT.Silu)
            for hf in range(2):
                m0 = p["pairs"] + hf * pairs
                with act.Fori(0, pairs) as i:
                    for s in range(2):
                        act.wait_ge(e_gu[s], i + (m0 + 1))
                        act.activation(e_silu[s][:, :], bank(G_BANK[s]), ACT.Silu).then_inc(e_act[s], 1)
                act.wait_ge(e_acc, 2 * k + hf + 1)
                for c in range(DC):
                    act.activation(e_out[:, c, :], bank(c), ACT.Copy).then_inc(e_outd, 1)

        def route_topk(v, E, k, scores):
            def by(ap, axis):
                return ap.unsqueeze(axis).to_broadcast([P, NT, E, E])
            pair, tie = r_pair[:, :, 0:E, 0:E], r_tie[:, :, 0:E, 0:E]
            other, own = by(scores, 2), by(scores, 3)
            dve_steps.then(v, v.tensor_tensor(tie, other, own, ALU.is_equal))
            dve_steps.then(v, v.tensor_tensor(tie, tie, r_earlier[:, 0:E, 0:E].unsqueeze(1).to_broadcast([P, NT, E, E]), ALU.mult))
            dve_steps.then(v, v.tensor_tensor(pair, other, own, ALU.is_gt))
            dve_steps.then(v, v.tensor_tensor(pair, pair, tie, ALU.add))
            dve_steps.then(v, v.tensor_reduce(r_b[:, :, 0:E], pair, AX.X, ALU.add))
            dve_steps.then(v, v.tensor_scalar(r_b[:, :, 0:E], r_b[:, :, 0:E], k - 0.5, None, ALU.is_lt))

        def moe_vector(v, name):
            p = moe_plan[name]
            k, E, n_slots = p["index"], p["experts"], p["slots"]
            v.wait_ge(x_upd, p["x_at"])
            norm_vector(v, p["ln"], x)
            v.wait_ge(rw_land, 16 * (k + 1))
            dve_steps.then(v, v.tensor_copy(r_whi[:, :, 0:E], r_w[:, :, 0:E]))
            v.tensor_tensor(r_wlo[:, :, 0:E], r_w[:, :, 0:E], r_whi[:, :, 0:E].bitcast(F32), ALU.subtract)\
                .then_inc(rw_split, 1)
            v.wait_ge(r_logits, k + 1)
            lg = bank(6, NT * E).rearrange("p (k e) -> p k e", k=NT)
            a, b, log, route = (r[:, :, 0:E] for r in (r_a, r_b, r_log, r_route))

            def wide(col):
                return col.unsqueeze(2).to_broadcast([P, NT, E])

            if name == "L0":
                dve_steps.then(v, v.tensor_copy(log, lg))
                for n in range(NT):
                    ins = v.max(r_top[:, n, :], log[:, n, :])
                dve_steps.then(v, ins)
                for n in range(NT):
                    ins = v.match_replace(b[:, n, :], r_top[:, n, :], log[:, n, :], -BIG)
                dve_steps.then(v, ins)
                dve_steps.then(v, v.tensor_tensor(a, log, wide(r_top[:, :, 0]), ALU.subtract))
                v.tensor_tensor(b, b, wide(r_top[:, :, 0]), ALU.subtract).then_inc(r_in, 1)
                v.wait_ge(r_acted, k + 1)
                dve_steps.then(v, v.tensor_tensor(route, a, b, ALU.subtract))
                dve_steps.then(v, v.tensor_reduce(r_sum[:, :], route, AX.X, ALU.add))
                dve_steps.then(v, v.reciprocal(r_sum[:, :], r_sum[:, :]))
                dve_steps.then(v, v.tensor_tensor(route, route, wide(r_sum[:, :]), ALU.mult))
            elif name == "L1":
                v.tensor_copy(log, lg).then_inc(r_in, 1)
                v.wait_ge(rbias_land, 16)
                v.wait_ge(early_done, 1)
                v.wait_ge(r_acted, k + 1)
                dve_steps.then(v, v.tensor_tensor(log, a, r_bias[name][:, :].unsqueeze(1).to_broadcast([P, NT, E]), ALU.add))
                route_topk(v, E, 2, log)
                dve_steps.then(v, v.tensor_tensor(route, a, b, ALU.mult))
                dve_steps.then(v, v.tensor_reduce(r_sum[:, :], route, AX.X, ALU.add))
                dve_steps.then(v, v.tensor_scalar(r_sum[:, :], r_sum[:, :], 1e-12, None, ALU.max))
                dve_steps.then(v, v.reciprocal(r_sum[:, :], r_sum[:, :]))
                dve_steps.then(v, v.tensor_tensor(route, route, wide(r_sum[:, :]), ALU.mult))
                dve_steps.then(v, v.memset(r_route[:, :, E:E + 1], 1.0))
            else:
                v.wait_ge(rbias_land, 32)
                dve_steps.then(v, v.tensor_tensor(log, lg, r_bias[name][:, :].unsqueeze(1).to_broadcast([P, NT, E]), ALU.add))
                dve_steps.then(v, v.tensor_reduce(r_sum[:, :], log, AX.X, ALU.max))
                v.tensor_tensor(log, log, wide(r_sum[:, :]), ALU.subtract).then_inc(r_in, 1)
                v.wait_ge(r_acted, k + 1)
                dve_steps.then(v, v.tensor_reduce(r_sum[:, :], a, AX.X, ALU.add))
                dve_steps.then(v, v.reciprocal(r_sum[:, :], r_sum[:, :]))
                dve_steps.then(v, v.tensor_tensor(a, a, wide(r_sum[:, :]), ALU.mult))
                route_topk(v, E, 1, a)
                dve_steps.then(v, v.tensor_tensor(route, a, b, ALU.mult))
            route = r_route[:, :, 0:n_slots]
            rest = r_a[:, :, 0:n_slots]
            parts = [r_parts[:, :, i * n_slots:(i + 1) * n_slots] for i in range(3)]
            dve_steps.then(v, v.tensor_copy(parts[0], route))
            dve_steps.then(v, v.tensor_tensor(rest, route, parts[0], ALU.subtract))
            dve_steps.then(v, v.tensor_copy(parts[1], rest))
            v.tensor_tensor(parts[2], rest, parts[1], ALU.subtract)\
                .then_inc(r_done, 1)
            v.wait_ge(r_Tps, k + 1)
            v.tensor_copy(r_T[0:3 * n_slots, :], bank(7).bitcast(BF16)[0:3 * n_slots, :]).then_inc(r_Tcp, 1)
            pairs = p["n"] // 2
            for hf in range(2):
                m0 = p["pairs"] + hf * pairs
                with v.Fori(0, pairs) as i:
                    dve_steps.enter(i, 6)
                    for s in range(2):
                        v.wait_ge(e_act[s], i + (m0 + 1))
                        dve_steps.then(v, v.tensor_tensor(e_silu[s][:, :], bank(U_BANK[s]), e_silu[s][:, :], ALU.mult))
                        dve_steps.then(v, v.tensor_tensor(e_h[s][:, :], bank(R_BANK[s]), e_silu[s][:, :], ALU.mult))
                        v.wait_ge(e_down[s], i + m0)
                        dve_steps.then(v, v.tensor_copy(e_hhi[s][:, :], e_h[s][:, :]))
                        v.tensor_tensor(e_hlo[s][:, :], e_h[s][:, :], e_hhi[s][:, :].bitcast(F32), ALU.subtract)\
                            .then_inc(e_hd[s], 1)
                dve_steps.leave(pairs)
                for n in range(NT // 2):
                    if n % 2 == 0:
                        v.wait_ge(e_T, 2 * k + hf + 1)
                    tile = x[:, hf * (NT // 2) + n, :]
                    v.tensor_tensor(tile, bank((3, 5)[n // 2], D, (n % 2) * D), tile, ALU.add).then_inc(x_upd, 1)

        def moe_tensor(pe, name):
            p = moe_plan[name]
            k, E, n3 = p["index"], p["experts"], 3 * p["slots"]
            norm_tensor(pe, p["ln"])
            pe.wait_ge(rw_split, k + 1)
            pe.wait_ge(xT_lo, p["ln"]["lo_end"])
            for n in range(NT):
                tok = slice(n * P, (n + 1) * P)
                for c in range(DC):
                    mm = three(pe, bank(6, E, n * E), (xhi[:, c, tok], xlo[:, c, tok]),
                               (r_whi[:, c, 0:E], r_wlo[:, c, 0:E]), c == 0, c == DC - 1)
            mm.then_inc(r_logits, 1)
            pe.wait_ge(r_done, k + 1)
            for n in range(NT):
                mm = pe.transpose(bank(7).bitcast(BF16)[0:n3, n * P:(n + 1) * P],
                                  r_parts[:, n, 0:n3], identb[:, :])
            mm.then_inc(r_Tps, 1)
            pe.wait_ge(r_Tcp, k + 1)
            pe.wait_ge(rows_land, 16 * (k + 1))
            pairs = p["n"] // 2
            for hf in range(2):
                m0 = p["pairs"] + hf * pairs
                cols = slice(hf * HALF, (hf + 1) * HALF)

                def gate_up(s, pair, chunk):
                    pe.wait_ge(w_gu[s], pair + 1)
                    pe.wait_ge(e_hd[s], pair)
                    for at, dst in ((0, G_BANK), (D, U_BANK)):
                        for c in range(DC):
                            w = slice(at + c * P, at + (c + 1) * P)
                            three(pe, bank(dst[s]), (w_hi_gu[s][:, w], w_lo_gu[s][:, w]),
                                  (xhi[:, c, cols], xlo[:, c, cols]), c == 0, c == DC - 1)
                    pe.matmul(bank(R_BANK[s]), e_rows[0:n3, chunk], r_T[0:n3, cols],
                              start=True, stop=True).then_inc(e_gu[s], 1)

                def down(s, pair):
                    pe.wait_ge(w_d[s], pair + 1)
                    pe.wait_ge(e_hd[s], pair + 1)
                    for c in range(DC):
                        w = slice(c * P, (c + 1) * P)
                        mm = pe.matmul(bank(c), w_hi_d[s][:, w], e_hhi[s][:, :], start=False, stop=False, skip_group_check=True)
                        mm = pe.matmul(bank(c), w_hi_d[s][:, w], e_hlo[s][:, :], start=False, stop=False, skip_group_check=True)
                        mm = pe.matmul(bank(c), w_lo_d[s][:, w], e_hhi[s][:, :], start=False, stop=False, skip_group_check=True)
                    mm.then_inc(e_down[s], 1)

                if hf == 1:
                    pe.wait_ge(x_upd, p["x_at"] + NT // 2)
                for c in range(DC):
                    pe.matmul(bank(c), zerob[:, 0:P], zerob[:, :], start=True, stop=False, skip_group_check=True)
                gate_up(0, m0, slice(0, P))
                with pe.Fori(0, pairs - 1) as i:
                    gate_up(1, i + m0, bass.ds(i * 2 * P + P, P))
                    down(0, i + m0)
                    gate_up(0, i + (m0 + 1), bass.ds(i * 2 * P + 2 * P, P))
                    down(1, i + m0)
                gate_up(1, m0 + pairs - 1, slice((p["n"] - 1) * P, p["n"] * P))
                down(0, m0 + pairs - 1)
                down(1, m0 + pairs - 1)
                for c in range(DC):
                    mm = pe.matmul(bank(c), zerob[:, 0:P], zerob[:, :], start=False, stop=True, skip_group_check=True)
                mm.then_inc(e_acc, 1)
                for n in range(NT // 2):
                    for c in range(DC):
                        if n == 0:
                            pe.wait_ge(e_outd, 4 * k + 2 * hf + c + 1)
                        mm = pe.transpose(bank((3, 5)[n // 2], P, (n % 2) * D + c * P),
                                          e_out[:, c, n * P:(n + 1) * P], ident[:, :])
                mm.then_inc(e_T, 1)

        moe_prepare("L0", 0, 1)

        ln_l1z = norm_plan(False, False)
        ln_l1y = norm_plan(False, False)
        l1 = ExitStack()
        l1_bsum = sb("l1_bsum", [P, DC], F32, l1)
        l1_mean = sb("l1_mean", [P, DC, B], F32, l1)
        l1_summ = sb("l1_summ", [P, DC, B], F32, l1)
        l1_wide = sb("l1_wide", [P, DC, B, P], F32, l1)
        l1_y = sb("l1_y", [P, NT, D], F32, l1)
        l1.close()
        l1_land, l1_h, l1_meand, l1_s, l1_wided, l1_b = (sem(n) for n in (
            "l1_land", "l1_h", "l1_meand", "l1_s", "l1_wided", "l1_b"))

        def l1x_scalar(act):
            pass

        def l1x_vector(v):
            v.wait_ge(x_upd, X_AT[2])
            norm_vector(v, ln_l1z, x)
            v.wait_ge(l1_land, 16 * 6)
            dve_steps.then(v, v.tensor_scalar(l1_bsum[:, :], l1_bin[:, :], decay_total[:, 0:1], None, ALU.mult))
            v.wait_ge(l1_h, 1)
            for c in range(DC):
                v.tensor_scalar(l1_mean[:, c, :], bank(0, B, c * B), l1_bsum[:, c:c + 1], 1.0 / M,
                                ALU.add, ALU.mult).then_inc(l1_meand, 1)
            v.wait_ge(l1_s, 1)
            for c in range(DC):
                ins = v.tensor_scalar(l1_summ[:, c, :], bank(1, B, c * B), l1_bout[:, c:c + 1], None, ALU.add)
            dve_steps.then(v, ins)
            v.tensor_copy(l1_wide[:, :, :, :].rearrange("p c b n -> p (c b) n"),
                          l1_summ[:, :, :].rearrange("p c b -> p (c b)").unsqueeze(2).to_broadcast([P, DC * B, P]))\
                .then_inc(l1_wided, 1)
            v.wait_ge(l1_b, 1)
            v.wait_ge(xn_done, NT * (ln_l1z["k"] + 1))
            for n in range(NT):
                b = n // TB
                ins = v.tensor_tensor(l1_y[:, n, :], xn[:, n, :], bank(2 + b // 2, D, (b % 2) * D), ALU.add)
            dve_steps.then(v, ins)
            norm_vector(v, ln_l1y, l1_y)
            v.wait_ge(xn_done, NT * (ln_l1y["k"] + 1))
            gamma = l1_gamma[:, :].unsqueeze(1).to_broadcast([P, NT, D])
            beta = l1_beta[:, :].unsqueeze(1).to_broadcast([P, NT, D])
            dve_steps.then(v, v.tensor_tensor(xn[:, :, :], xn[:, :, :], gamma, ALU.mult))
            dve_steps.then(v, v.tensor_tensor(xn[:, :, :], xn[:, :, :], beta, ALU.add))
            for n in range(NT):
                v.tensor_tensor(x[:, n, :], x[:, n, :], xn[:, n, :], ALU.add).then_inc(x_upd, 1)

        def l1x_tensor(pe):
            pe.wait_ge(l1_land, 16 * 6)
            pe.wait_ge(x_upd, X_AT[2])
            for e in range(DC):
                for c in range(DC):
                    mm = pe.matmul(bank(0, B, e * B), l1_in[:, c, e * P:(e + 1) * P], decay_sum[:, c, :],
                                   start=(c == 0), stop=(c == DC - 1))
            mm.then_inc(l1_h, 1)
            pe.wait_ge(l1_meand, DC)
            for e in range(DC):
                for c in range(DC):
                    mm = pe.matmul(bank(1, B, e * B), l1_out[:, c, e * P:(e + 1) * P], l1_mean[:, c, :],
                                   start=(c == 0), stop=(c == DC - 1))
            mm.then_inc(l1_s, 1)
            pe.wait_ge(l1_wided, 1)
            for b in range(B):
                for c in range(DC):
                    mm = pe.matmul(bank(2 + b // 2, P, (b % 2) * D + c * P), l1_wide[:, c, b, :], ident[:, :],
                                   start=True, stop=True)
            mm.then_inc(l1_b, 1)

        moe_prepare("L1", 1, 3)

        ln_l2x = norm_plan(True, False)
        l2 = ExitStack()
        KC = MC + TB
        KG = -(-KC // 4)
        MX = M + S
        U = REP * TB
        QW = REP * P
        TURNS = B * KH
        l2_ctx = sb("l2_ctx", [P, DC, M], F32, l2)
        l2_w = sb("l2_w", [P, DC, 4 * HD + REP * HD], F32, l2)
        l2_wo = sb("l2_wo", [P, QH, D], F32, l2)
        l2_xb = sb("l2_xb", [P, DC, S], F32, l2)
        l2_kraw = [sb(f"l2_kraw{n}", [P, 4, HD], F32, l2) for n in range(2)]
        l2_kn = [sb(f"l2_kn{n}", [P, 4, HD], F32, l2) for n in range(2)]
        l2_ra = sb("l2_ra", [P, TB, HD], F32, l2)
        l2_rb = sb("l2_rb", [P, TB, HD], F32, l2)
        l2_q = sb("l2_q", [P, TB, REP, HD], F32, l2)
        l2_qa = sb("l2_qa", [P, TB, REP, HD], F32, l2)
        l2_qb = sb("l2_qb", [P, TB, REP, HD], F32, l2)
        l2_vhi = [sb(f"l2_vhi{s}", [P, KC, HD], F32R, l2) for s in range(2)]
        l2_vlo = [sb(f"l2_vlo{s}", [P, KC, HD], F32R, l2) for s in range(2)]
        l2_kThi = [sb(f"l2_kThi{s}", [P, MX + 1], F32R, l2) for s in range(2)]
        l2_kTlo = [sb(f"l2_kTlo{s}", [P, MX + 1], F32R, l2) for s in range(2)]
        l2_qThi = [sb(f"l2_qThi{s}", [P, TB, QW], F32R, l2) for s in range(2)]
        l2_qTlo = [sb(f"l2_qTlo{s}", [P, TB, QW], F32R, l2) for s in range(2)]
        l2_m = [sb(f"l2_m{s}", [REP, TB, QW], F32R, l2) for s in range(2)]
        l2_p = [sb(f"l2_p{n}", [P, QW], F32, l2) for n in range(3)]
        l2_phi = [sb(f"l2_phi{n}", [P, QW], F32R, l2) for n in range(3)]
        l2_plo = [sb(f"l2_plo{n}", [P, QW], F32R, l2) for n in range(3)]
        l2_rec = [sb(f"l2_rec{k}", [P, REP], F32, l2) for k in range(TB)]
        parts = [xn[:, 2 * n:2 * n + 2, :].rearrange("p k d -> p (k d)") for n in range(2 * TB)]
        l2_acc, l2_oT = parts[:TB], parts[TB:]
        l2_cos, l2_sin = sb("l2_cos", [P, TB, HD // 2], F32, l2), sb("l2_sin", [P, TB, HD // 2], F32, l2)
        l2_qw, l2_kw = sb("l2_qw", [P, HD], F32, l2), sb("l2_kw", [P, HD], F32, l2)
        l2_kwc = sb("l2_kwc", [P, 1], F32, l2)
        rope_q = [sb(f"rope_q{n}", [P, TB, HD], F32, l2) for n in range(2)]
        rope_k = [sb(f"rope_k{n}", [P, TB, HD], F32, l2) for n in range(2)]
        l2_kms, l2_krs = sb("l2_kms", [P, KG, 4], F32, l2), sb("l2_krs", [P, KG, 4], F32, l2)
        l2_qms, l2_qrs = sb("l2_qms", [P, U], F32, l2), sb("l2_qrs", [P, U], F32, l2)
        l2_mx4, l2_mx = sb("l2_mx4", [P, U, KG], F32, l2), sb("l2_mx", [P, U], F32, l2)
        l2_ones = sb("l2_ones", [REP, P], F32R, l2)
        l2.close()
        (l2_cland, l2_wland, l2_pland, l2_proj, l2_qc, l2_kvc, l2_vl, l2_ksqd, l2_kmsd, l2_krsd, l2_qmsd, l2_qrsd,
         l2_knd, l2_qnd, l2_kT, l2_kTh, l2_kTl, l2_qT, l2_qTh, l2_qTl, l2_near, l2_far, l2_top, l2_mT, l2_md, l2_s, l2_e,
         l2_lo, l2_accd, l2_pv, l2_sum, l2_inv, l2_o, l2_y) = (sem(n) for n in (
             "l2_cland l2_wland l2_pland l2_proj l2_qc l2_kvc l2_vl l2_ksqd l2_kmsd l2_krsd l2_qmsd l2_qrsd "
             "l2_knd l2_qnd l2_kT l2_kTh l2_kTl l2_qT l2_qTh l2_qTl l2_near l2_far l2_top l2_mT l2_md l2_s l2_e "
             "l2_lo l2_accd l2_pv l2_sum l2_inv l2_o l2_y").split())

        STEPS = [(k, j) for k in range(TB) for j in range(MC + k + 1)]
        NS = len(STEPS)
        TILE_END = [max(c for c in range(NS) if STEPS[c][0] == k) for k in range(TB)]
        NPROJ = TB + KC
        Q_AT, KV_AT = 0, TB
        QT_AT = [7, 9]
        KSQ_AT = [6, 10, 14, 17]
        KN_AT = [8, 12, 16, 19]
        KT_AT = [11, 14, 18, 20]
        MAX_AT = {0: [13, 15, 19, 21], 1: [17, 23, 25, 27]}
        M_AT = 24
        M1_AT = 4
        SUM_AT = [(TILE_END[0] + 2, TILE_END[0] + 3), (1, 2)]

        def max_pieces(c):
            return [(k, 2 * (c - a) + n, q) for k, at in MAX_AT.items() for q, a in enumerate(at)
                    if 0 <= c - a < 2 for n in range(2)]

        SEARCH = [piece for c in range(NS) for piece in max_pieces(c)]
        NM = len(SEARCH)
        assert NM == U * KG
        SHARED = []
        for c in range(NS):
            if c < NPROJ:
                SHARED.append(("project", c))
            SHARED += [("search", SEARCH.index(piece)) for piece in max_pieces(c)]

        def shared_bank(slot, kind, i):
            return 5 + (slot * len(SHARED) + SHARED.index((kind, i))) % 2

        def piece_cols(k, q):
            a, z = q * BANK, min(q * BANK + BANK, M + (k + 1) * P)
            return a - (z - a) % 2, z

        def key_cols(j):
            return (j * P, chunk_rows(j)) if j < MC else (M + (j - MC) * P, P)

        def need(engine, semaphore, count):
            if not (isinstance(count, int) and count <= 0):
                engine.wait_ge(semaphore, count)

        def ahead(c, by, g, n):
            return (g, c + by) if c + by < NS else (n, c + by - NS)

        def l2_turns(engine, turn, steps=None):
            turn(None, 1, 0)
            turn(0, 0, 1)
            with engine.Fori(0, TURNS // 2 - 1) as i:
                if steps:
                    steps.enter(i, 2 * L2_DVE_STEPS)
                for s in (1, 0):
                    g = i * 2 + (2 - s)
                    turn(g, s, i * 2 + (3 - s))
            if steps:
                steps.leave(TURNS // 2 - 1)
            turn(TURNS - 1, 1, None)

        def l2x_sync(sp):
            sp.wait_ge(x_upd, X_AT[4])
            for dst, name in ((l2_cos, "rope_cos"), (l2_sin, "rope_sin"), (l2_kwc, "L2_kwc"), (l2_wo, "L2_wo")):
                sp.dma_start(dst[...], t[name]).then_inc(l2_pland, 16)
            for dst, name in ((l2_qw, "L2_qw"), (l2_kw, "L2_kw")):
                sp.dma_start(dst[:, :], t[name].to_broadcast([P, HD])).then_inc(l2_pland, 16)
            sp.wait_ge(xT_cp, ln_l2x["cp_end"])
            with sp.Fori(0, B) as b:
                sp.wait_ge(l2_proj, b * (KH * NPROJ))
                sp.dma_start(l2_ctx[:, :, :], t["ctx_T"][bass.ds(b, 1)].rearrange("o p c m -> p (o c) m"))\
                    .then_inc(l2_cland, 16)
                sp.dma_start(l2_xb[:, :, :], xT[:, :, bass.ds(b * S, S)]).then_inc(l2_cland, 16)
                with sp.Fori(0, KH) as h:
                    sp.wait_ge(l2_proj, (b * KH + h) * NPROJ)
                    sp.dma_start(l2_w[:, :, :], t["L2_w_qkv"][bass.ds(h, 1)].rearrange("o p c n -> p (o c) n"))\
                        .then_inc(l2_wland, 16)

        def l2x_pool(g_):
            def sums(g, c):
                k, j = STEPS[c]
                if j == 0:
                    return
                r = key_cols(j)[1]
                if j == 1:
                    need(g_, l2_sum, g * TB + (k - 1))
                g_.wait_ge(l2_e, g * (2 * NS) + 2 * (c + 1))
                first = l2_p[(c - 1) % 3] if j == 1 else l2_acc[k]
                if j > 1:
                    g_.wait_ge(l2_accd, g * NS + c)
                g_.tensor_tensor(l2_acc[k][0:r, :], first[0:r, :], l2_p[c % 3][0:r, :], ALU.add)\
                    .then_inc(l2_accd, 2 if j == 1 else 1)

            def turn(g, slot, n):
                for c in range(NS):
                    at, step = ahead(c, 1, g, n)
                    if at is not None:
                        sums(at, step)
                    if n is None:
                        continue
                    if c == 2:
                        g_.wait_ge(l2_qmsd, n + 1)
                        g_.tensor_tensor(l2_qrs[:, :], l2_qms[:, :], half_power[:, 0:U], ALU.pow).then_inc(l2_qrsd, 1)
                    for q in range(KG):
                        if c == KSQ_AT[q]:
                            nb = min(4, KC - 4 * q)
                            g_.wait_ge(l2_kmsd, n * KG + (q + 1))
                            g_.tensor_tensor(l2_krs[:, q, 0:nb], l2_kms[:, q, 0:nb], half_power[:, 0:nb], ALU.pow).then_inc(l2_krsd, 1)

            l2_turns(g_, turn)

        def l2x_scalar(act):
            norm_scalar(act, ln_l2x)
            act.preload_act_table(ACT.Exp)
            act.wait_ge(l2_pland, 16 * 6)

            def exp(g, c):
                k, j = STEPS[c]
                r = key_cols(j)[1]
                act.wait_ge(l2_s, g * NS + (c + 1))
                last = c - 3 if c >= 3 else NS - 2 + c if c < 2 else NS - 3
                done = (g * NS + last if c >= 3 else g * NS + (last - NS)) + 1
                need(act, l2_pv, done)
                need(act, l2_accd, done)
                src = bank(c % 3)[0:r, :]
                act.activation(l2_phi[c % 3][0:r, :], src, ACT.Exp).then_inc(l2_e, 1)
                act.activation(l2_p[c % 3][0:r, :], src, ACT.Exp).then_inc(l2_e, 1)

            def products(g, k):
                act.wait_ge(l2_pv, g * NS + (TILE_END[k] + 1))
                need(act, l2_y, (g * TB + k - TB + 1) * 2)
                act.activation(l2_oT[k][:, :], bank(3 + k), ACT.Copy).then_inc(l2_o, 1)

            def turn(g, slot, n):
                new = 1 - slot
                for c in range(NS):
                    at, step = ahead(c, 2, g, n)
                    if at is not None:
                        exp(at, step)
                    if g is not None and c == SUM_AT[0][0]:
                        products(g, 0)
                    if g is not None and c == SUM_AT[1][0] and not (isinstance(g, int) and g == 0):
                        products(g - 1, 1)
                    if n is None:
                        continue
                    if c < TB:
                        act.wait_ge(l2_proj, n * NPROJ + (c + 1))
                        need(act, l2_qT, n * TB)
                        need(act, l2_qnd, n)
                        src = bank(shared_bank(new, "project", c))
                        act.activation(l2_q[:, c, :, :], src, ACT.Copy).then_inc(l2_qc, 1)
                        act.activation(l2_qa[:, c, :, :], src, ACT.Square).then_inc(l2_qc, 1)
                    elif c < NPROJ:
                        j = c - TB
                        r = key_cols(j)[1]
                        act.wait_ge(l2_proj, n * NPROJ + (c + 1))
                        if j % 4 == 0:
                            need(act, l2_knd, n * KG + (j // 4 - 1))
                        kv = bank(shared_bank(new, "project", c), 2 * HD)
                        act.activation(l2_kraw[j // 4 % 2][0:r, j % 4, :], kv[0:r, 0:HD], ACT.Copy).then_inc(l2_kvc, 1)
                        act.activation(l2_vhi[new][0:r, j, :], kv[0:r, HD:2 * HD], ACT.Copy).then_inc(l2_kvc, 1)
                    for q in range(KG):
                        nb = min(4, KC - 4 * q)
                        if c == KSQ_AT[q]:
                            act.wait_ge(l2_kvc, n * (2 * KC) + 2 * min(KC, 4 * q + 4))
                            need(act, l2_kT, n * KG + (q - 1))
                            act.activation(l2_kn[q % 2][:, 0:nb, :], l2_kraw[q % 2][:, 0:nb, :], ACT.Square).then_inc(l2_ksqd, 1)
                        if c == KT_AT[q]:
                            act.wait_ge(l2_kT, n * KG + (q + 1))
                            a, z = q * BANK, min(q * BANK + BANK, M)
                            ins = act.activation(l2_kThi[new][:, a:z], bank(7, z - a), ACT.Copy, scale=l2_kwc[:, 0:1])
                            if q == KG - 1:
                                ins = act.activation(l2_kThi[new][:, M:MX], bank(7, S, M - a), ACT.Copy)
                            ins.then_inc(l2_kTh, 1)
                    for k in range(TB):
                        if c == QT_AT[k]:
                            act.wait_ge(l2_qT, n * TB + (k + 1))
                            act.activation(l2_qThi[new][:, k, :], bank(7), ACT.Copy).then_inc(l2_qTh, 1)

            l2_turns(act, turn)
            products(TURNS - 1, 1)

        def l2x_vector(v):
            v.wait_ge(x_upd, X_AT[4])
            dve_steps.then(v, v.memset(l2_kraw[1][:, :, :], 0.0))
            v.tensor_copy(l2_ones[:, :], ones[0:REP, :])
            v.wait_ge(l2_pland, 16 * 6)
            hh = HD // 2
            for (own, other), w in ((rope_q, l2_qw), (rope_k, l2_kw)):
                for k in range(TB):
                    v.tensor_tensor(own[:, k, 0:hh], l2_cos[:, k, :], w[:, 0:hh], ALU.mult)
                    v.tensor_tensor(own[:, k, hh:HD], l2_cos[:, k, :], w[:, hh:HD], ALU.mult)
                    v.scalar_tensor_tensor(other[:, k, 0:hh], l2_sin[:, k, :], -1.0, w[:, hh:HD], ALU.mult, ALU.mult)
                    ins = v.tensor_tensor(other[:, k, hh:HD], l2_sin[:, k, :], w[:, 0:hh], ALU.mult)
            dve_steps.then(v, ins)
            norm_vector(v, ln_l2x, x)
            own, other = (r[:, :, :].unsqueeze(2).to_broadcast([P, TB, REP, HD]) for r in rope_q)

            def rest(g, c):
                k, j = STEPS[c]
                r = key_cols(j)[1]
                v.wait_ge(l2_e, g * (2 * NS) + 2 * (c + 1))
                v.tensor_tensor(l2_plo[c % 3][0:r, :], l2_p[c % 3][0:r, :], l2_phi[c % 3][0:r, :].bitcast(F32), ALU.subtract)\
                    .then_inc(l2_lo, 1)

            def inverse(g, k):
                v.wait_ge(l2_sum, g * TB + (k + 1))
                v.reciprocal(l2_rec[k][:, :], bank(7, REP)).then_inc(l2_inv, 1)

            def add_out(g, k, half):
                if half == 0:
                    v.wait_ge(l2_inv, g * TB + (k + 1))
                v.wait_ge(l2_y, (g * TB + k) * 2 + (half + 1))
                row = x[:, bass.ds((g // KH) * TB + k, 1), :].rearrange("p o d -> p (o d)")
                for i in range(REP // 2):
                    h = half * (REP // 2) + i
                    ins = v.scalar_tensor_tensor(row, bank(7, D, i * D), l2_rec[k][:, h:h + 1], row, ALU.mult, ALU.add)
                    if i == 0:
                        dve_steps.then(v, ins)
                ins.then_inc(x_upd, 1)

            def tops(g, k):
                v.wait_ge(l2_far, g * NM + (SEARCH.index((k, REP - 1, KG - 1)) + 1))
                v.tensor_reduce(l2_mx[:, k * REP:(k + 1) * REP], l2_mx4[:, k * REP:(k + 1) * REP, :], AX.X, ALU.max)\
                    .then_inc(l2_top, 1)

            def shifts(g, slot, k):
                v.wait_ge(l2_mT, g * TB + (k + 1))
                v.scalar_tensor_tensor(l2_m[slot][:, k, :].rearrange("h (a n) -> h a n", a=REP),
                                       bank(7, P)[0:REP, :].unsqueeze(1).to_broadcast([REP, REP, P]), -1.0,
                                       ident[0:REP, 0:REP].unsqueeze(2).to_broadcast([REP, REP, P]), ALU.mult, ALU.mult)\
                    .then_inc(l2_md, 1)

            def prepare(c, slot, n):
                if TB <= c < NPROJ:
                    j = c - TB
                    r = key_cols(j)[1]
                    v.wait_ge(l2_kvc, n * (2 * KC) + 2 * (j + 1))
                    v.tensor_tensor(l2_vlo[slot][0:r, j, :], bank(shared_bank(slot, "project", c), 2 * HD)[0:r, HD:2 * HD],
                                    l2_vhi[slot][0:r, j, :].bitcast(F32), ALU.subtract).then_inc(l2_vl, 1)
                if c == 2:
                    v.wait_ge(l2_qc, (n + 1) * (2 * TB))
                    dve_steps.then(v, v.tensor_reduce(l2_qms[:, :], l2_qa[:, :, :, :].rearrange("p k r n -> p (k r) n"),
                                                      AX.X, ALU.add))
                    v.tensor_scalar(l2_qms[:, :], l2_qms[:, :], HD * RMS_EPS, None, ALU.add).then_inc(l2_qmsd, 1)
                if c == 3:
                    dve_steps.then(v, v.tensor_tensor(l2_qa[:, :, :, :], l2_q[:, :, :, :], own, ALU.mult))
                if c == 4:
                    v.tensor_tensor(l2_qb[:, :, :, 0:hh], l2_q[:, :, :, hh:HD], other[:, :, :, 0:hh], ALU.mult)
                    dve_steps.then(v, v.tensor_tensor(l2_qb[:, :, :, hh:HD], l2_q[:, :, :, 0:hh], other[:, :, :, hh:HD], ALU.mult))
                if c == 5:
                    dve_steps.then(v, v.tensor_tensor(l2_qb[:, :, :, :], l2_qa[:, :, :, :], l2_qb[:, :, :, :], ALU.add))
                if c == 6:
                    v.wait_ge(l2_qrsd, n + 1)
                    v.tensor_tensor(l2_q[:, :, :, :].rearrange("p k r n -> p (k r) n"),
                                    l2_qb[:, :, :, :].rearrange("p k r n -> p (k r) n"),
                                    l2_qrs[:, :].unsqueeze(2).to_broadcast([P, U, HD]), ALU.mult).then_inc(l2_qnd, 1)
                for k in range(TB):
                    if c == QT_AT[k]:
                        v.wait_ge(l2_qTh, n * TB + (k + 1))
                        v.tensor_tensor(l2_qTlo[slot][:, k, :], bank(7), l2_qThi[slot][:, k, :].bitcast(F32), ALU.subtract)\
                            .then_inc(l2_qTl, 1)
                for q in range(KG):
                    nb = min(4, KC - 4 * q)
                    kn = l2_kn[q % 2]
                    if c == KSQ_AT[q]:
                        v.wait_ge(l2_ksqd, n * KG + (q + 1))
                        dve_steps.then(v, v.tensor_reduce(l2_kms[:, q, 0:nb], kn[:, 0:nb, :], AX.X, ALU.add))
                        v.tensor_scalar(l2_kms[:, q, 0:nb], l2_kms[:, q, 0:nb], 1.0 / HD, RMS_EPS, ALU.mult, ALU.add)\
                            .then_inc(l2_kmsd, 1)
                    if c == KN_AT[q]:
                        v.wait_ge(l2_krsd, n * KG + (q + 1))
                        ins = v.tensor_tensor(kn[:, 0:nb, :], l2_kraw[q % 2][:, 0:nb, :],
                                              l2_krs[:, q, 0:nb].unsqueeze(2).to_broadcast([P, nb, HD]), ALU.mult)
                        if q == KG - 1:
                            dve_steps.then(v, ins)
                            kx = kn[:, nb - TB:nb, :]
                            v.tensor_tensor(l2_ra[:, :, :], kx, rope_k[0][:, :, :], ALU.mult)
                            v.tensor_tensor(l2_rb[:, :, 0:hh], kx[:, :, hh:HD], rope_k[1][:, :, 0:hh], ALU.mult)
                            dve_steps.then(v, v.tensor_tensor(l2_rb[:, :, hh:HD], kx[:, :, 0:hh], rope_k[1][:, :, hh:HD], ALU.mult))
                            ins = v.tensor_tensor(kx, l2_ra[:, :, :], l2_rb[:, :, :], ALU.add)
                        ins.then_inc(l2_knd, 1)
                    if c == KT_AT[q]:
                        v.wait_ge(l2_kTh, n * KG + (q + 1))
                        a, z = q * BANK, min(q * BANK + BANK, M)
                        ins = v.scalar_tensor_tensor(l2_kTlo[slot][:, a:z], bank(7, z - a), l2_kwc[:, 0:1],
                                                     l2_kThi[slot][:, a:z].bitcast(F32), ALU.mult, ALU.subtract)
                        if q == KG - 1:
                            ins = v.tensor_tensor(l2_kTlo[slot][:, M:MX], bank(7, S, M - a), l2_kThi[slot][:, M:MX].bitcast(F32),
                                                  ALU.subtract)
                        ins.then_inc(l2_kTl, 1)
                for k, h, q in max_pieces(c):
                    i = SEARCH.index((k, h, q))
                    a, z = piece_cols(k, q)
                    v.wait_ge(l2_near, n * NM + (i + 1))
                    u = k * REP + h
                    v.tensor_reduce(l2_mx4[:, u, q:q + 1], bank(shared_bank(slot, "search", i), z - a), AX.X, ALU.max)\
                        .then_inc(l2_far, 1)

            def turn(g, slot, n):
                for c in range(NS):
                    at, step = ahead(c, 1, g, n)
                    if at is not None:
                        rest(at, step)
                    if g is not None:
                        if c == 0:
                            tops(g, 1)
                        if c == M1_AT:
                            shifts(g, slot, 1)
                        for k, turns_ago in ((0, 0), (1, 1)):
                            if isinstance(g, int) and g < turns_ago:
                                continue
                            if c == SUM_AT[k][0]:
                                inverse(g - turns_ago, k)
                            for half in range(2):
                                if c == SUM_AT[k][1] + half:
                                    add_out(g - turns_ago, k, half)
                    if n is not None:
                        prepare(c, 1 - slot, n)
                        if c == MAX_AT[0][-1] + 1:
                            tops(n, 0)
                        if c == M_AT:
                            shifts(n, 1 - slot, 0)

            l2_turns(v, turn, dve_steps)
            inverse(TURNS - 1, 1)
            for half in range(2):
                add_out(TURNS - 1, 1, half)

        def l2x_tensor(pe):
            norm_tensor(pe, ln_l2x)

            def scores(g, slot, c):
                k, j = STEPS[c]
                a, r = key_cols(j)
                even = r + r % 2
                if j == 0:
                    pe.wait_ge(l2_md, g * TB + (k + 1))
                if k == 0:
                    pe.wait_ge(l2_kTl, g * KG + (j // 4 + 1))
                last = c - 3 if c >= 3 else NS - 2 + c if c < 2 else NS - 3
                need(pe, l2_e, (g * (2 * NS) + 2 * (last + 1)) if c >= 3 else g * (2 * NS) + 2 * (last - NS + 1))
                dst = bank(c % 3)[0:even, :]
                keys = slice(a, a + even)
                if j == MC + k:
                    pe.matmul(dst, identb[:, :], causal_T[:, :, :].rearrange("p h n -> p (h n)"), start=True, stop=False)
                pe.matmul(dst, l2_ones[:, 0:even], l2_m[slot][:, k, :], start=(j < MC + k), stop=False)
                three(pe, dst, (l2_kThi[slot][:, keys], l2_kTlo[slot][:, keys]),
                      (l2_qThi[slot][:, k, :], l2_qTlo[slot][:, k, :]), False, True).then_inc(l2_s, 1)

            def values(g, slot, c):
                k, j = STEPS[c]
                r = key_cols(j)[1]
                pe.wait_ge(l2_lo, g * NS + (c + 1))
                if j == 0:
                    need(pe, l2_o, g * TB + (k - 1))
                if k == 0:
                    pe.wait_ge(l2_vl, g * KC + (j + 1))
                three(pe, bank(3 + k), (l2_vhi[slot][0:r, j, :], l2_vlo[slot][0:r, j, :]),
                      (l2_phi[c % 3][0:r, :], l2_plo[c % 3][0:r, :]), j == 0, j == MC + k).then_inc(l2_pv, 1)

            def sums(g, k):
                pe.wait_ge(l2_accd, g * NS + (TILE_END[k] + 1))
                for h in range(REP):
                    mm = pe.matmul(bank(7, 1, h), l2_acc[k][:, h * P:(h + 1) * P], ones[:, 0:1], start=True, stop=True)
                mm.then_inc(l2_sum, 1)

            def output(g, k, half):
                if half == 0:
                    pe.wait_ge(l2_o, g * TB + (k + 1))
                    pe.wait_ge(l2_inv, g * TB + (k + 1))
                else:
                    pe.wait_ge(x_upd, (g * TB + k) * 2 + (X_AT[4] + 1))
                for i in range(REP // 2):
                    h = half * (REP // 2) + i
                    mm = pe.matmul(bank(7, D, i * D), l2_oT[k][:, h * P:(h + 1) * P],
                                   l2_wo[:, bass.ds((g % KH) * REP + h, 1), :].rearrange("p o d -> p (o d)"),
                                   start=True, stop=True)
                mm.then_inc(l2_y, 1)

            def maxima(g, k):
                pe.wait_ge(l2_top, g * TB + (k + 1))
                pe.transpose(bank(7, P)[0:REP, :], l2_mx[:, k * REP:(k + 1) * REP], ident[:, :]).then_inc(l2_mT, 1)

            def bank_free(kind, i, n):
                at = SHARED.index((kind, i)) - 2
                if at < 0:
                    need(pe, l2_far, n * NM)
                elif SHARED[at][0] == "search":
                    pe.wait_ge(l2_far, n * NM + (SHARED[at][1] + 1))
                elif SHARED[at][1] < TB:
                    pe.wait_ge(l2_qc, n * (2 * TB) + 2 * (SHARED[at][1] + 1))
                else:
                    pe.wait_ge(l2_vl, n * KC + (SHARED[at][1] - TB + 1))

            def prepare(c, slot, n):
                if c == 0:
                    pe.wait_ge(l2_wland, n * 16 + 16)
                    pe.wait_ge(l2_cland, (n // KH) * 32 + 32)
                if c < NPROJ:
                    bank_free("project", c, n)
                    dst = bank(shared_bank(slot, "project", c))
                    j = c - TB
                    for d in range(DC):
                        if c < TB:
                            lhs, cols, into = l2_xb[:, d, c * P:(c + 1) * P], slice(4 * HD, None), dst
                        elif j < MC:
                            lhs, cols = l2_ctx[:, d, j * P:j * P + chunk_rows(j)], slice(0, 2 * HD)
                            into = dst[0:chunk_rows(j), 0:2 * HD]
                        else:
                            lhs, cols, into = l2_xb[:, d, (j - MC) * P:(j - MC + 1) * P], slice(2 * HD, 4 * HD), dst[:, 0:2 * HD]
                        mm = pe.matmul(into, lhs, l2_w[:, d, cols], start=(d == 0), stop=(d == DC - 1))
                    mm.then_inc(l2_proj, 1)
                for k in range(TB):
                    if c == QT_AT[k]:
                        pe.wait_ge(l2_qnd, n + 1)
                        if k == 0:
                            need(pe, l2_md, n * TB)
                        else:
                            pe.wait_ge(l2_qTl, n * TB + k)
                        for h in range(REP):
                            mm = pe.transpose(bank(7, P, h * P), l2_q[:, k, h, :], ident[:, :])
                        mm.then_inc(l2_qT, 1)
                for q in range(KG):
                    if c == KT_AT[q]:
                        pe.wait_ge(l2_knd, n * KG + (q + 1))
                        if q == 0:
                            pe.wait_ge(l2_qTl, (n + 1) * TB)
                        else:
                            pe.wait_ge(l2_kTl, n * KG + q)
                        if q == 2:
                            need(pe, x_upd, (n - 1) * (2 * TB) + (X_AT[4] + 2) if not isinstance(n, int) or n else 0)
                        for j in range(4 * q, min(4 * q + 4, KC)):
                            a, r = key_cols(j)
                            mm = pe.transpose(bank(7, r, a - q * BANK), l2_kn[q % 2][0:r, j % 4, :], ident[0:r, 0:r])
                        mm.then_inc(l2_kT, 1)
                for k, h, q in max_pieces(c):
                    i = SEARCH.index((k, h, q))
                    a, z = piece_cols(k, q)
                    pe.wait_ge(l2_kTh, n * KG + (q + 1))
                    bank_free("search", i, n)
                    at = shared_bank(slot, "search", i)
                    masked = q == KG - 1
                    if masked:
                        pe.matmul(bank(at, z - a), identb[:, :], causal[:, BANK - (z - a):], start=True, stop=False)
                    pe.matmul(bank(at, z - a), l2_qThi[slot][:, k, h * P:(h + 1) * P], l2_kThi[slot][:, a:z],
                              start=not masked, stop=True).then_inc(l2_near, 1)
                if c == M_AT:
                    pe.wait_ge(l2_kTl, (n + 1) * KG)
                    maxima(n, 0)

            def turn(g, slot, n):
                for c in range(NS):
                    if g is not None:
                        values(g, slot, c)
                    at, step = ahead(c, 3, g, n)
                    if at is not None:
                        scores(at, slot if c + 3 < NS else 1 - slot, step)
                    if g is not None:
                        later = not isinstance(g, int) or g >= 1
                        if c == SUM_AT[1][0] and later:
                            sums(g - 1, 1)
                        for half in range(2):
                            if c == SUM_AT[1][1] + half and later:
                                output(g - 1, 1, half)
                        if c == M1_AT:
                            if later:
                                pe.wait_ge(x_upd, g * (2 * TB) + X_AT[4])
                            maxima(g, 1)
                        if c == SUM_AT[0][0]:
                            if n is not None:
                                pe.wait_ge(l2_kTl, n * KG + 2)
                            sums(g, 0)
                        for half in range(2):
                            if c == SUM_AT[0][1] + half:
                                output(g, 0, half)
                    if n is not None:
                        prepare(c, 1 - slot, n)

            l2_turns(pe, turn)
            sums(TURNS - 1, 1)
            for half in range(2):
                output(TURNS - 1, 1, half)

        L2_DVE_STEPS = 2 * TB + 4 + KG + 2
        moe_prepare("L2", 2, 5)

        ln_l3x = norm_plan(True, False)
        l3 = ExitStack()
        W3 = 4 * D3
        l3_ctx = sb("l3_ctx", [P, DC, M], F32, l3)
        l3_wkv = sb("l3_wkv", [P, DC, 2 * D], F32, l3)
        l3_wq = sb("l3_wq", [P, DC, D], F32, l3)
        l3_xb = sb("l3_xb", [P, DC, S], F32, l3)
        l3_raw = [sb(f"l3_raw{n}", [P, D], F32, l3) for n in range(3)]
        l3_sq = [sb(f"l3_sq{n}", [P, D], F32, l3) for n in range(2)]
        l3_n = [sb(f"l3_n{n}", [P, D], F32, l3) for n in range(2)]
        l3_ms = [sb(f"l3_ms{n}", [P, H3], F32, l3) for n in range(2)]
        l3_rs = [sb(f"l3_rs{n}", [P, H3], F32, l3) for n in range(2)]
        l3_pairs = [sb(f"l3_pairs{n}", [P, H3, 4, D3], F16, l3) for n in range(2)]
        l3_v = sb("l3_v", [P, MC, H3, 32], F32, l3)
        l3_kT = sb("l3_kT", [P, NG, M], F16, l3)
        l3_qT = sb("l3_qT", [P, NG, HG, S], F16, l3)
        l3_p = [sb(f"l3_p{n}", [P, HG * S], F32, l3) for n in range(3)]
        l3_o = [sb(f"l3_o{n}", [P, S], F32, l3) for n in range(2)]
        l3_rec = sb("l3_rec", [P, TB, HG], F32, l3)
        l3_y = sb("l3_y", [P, TB, HG, D3], F32, l3)
        l3.close()
        (l3_cland, l3_wland, l3_init, l3_xbd, l3_kv, l3_kvd, l3_msd, l3_rsd, l3_pd, l3_T, l3_Td, l3_s, l3_e, l3_pv,
         l3_od, l3_oT) = (sem(n) for n in (
             "l3_cland l3_wland l3_init l3_xbd l3_kv l3_kvd l3_msd l3_rsd l3_pd l3_T l3_Td l3_s l3_e l3_pv "
             "l3_od l3_oT").split())
        N3 = MC + TB
        C3 = NG * MC

        def rows3(j):
            return chunk_rows(j) if j < MC else P

        def l3x_sync(sp):
            sp.wait_ge(x_upd, X_AT[6])
            sp.dma_start(l3_wkv[:, :, :], t["L3_kv"]).then_inc(l3_wland, 16)
            sp.dma_start(l3_wq[:, :, :], t["L3_q"]).then_inc(l3_wland, 16)
            with sp.Fori(0, B) as b:
                sp.wait_ge(l3_kv, b * N3)
                sp.dma_start(l3_ctx[:, :, :], t["ctx_T"][bass.ds(b, 1)].rearrange("o p c m -> p (o c) m"))\
                    .then_inc(l3_cland, 16)

        def l3x_pool(g):
            g.wait_ge(x_upd, X_AT[6])
            pool_steps.then(g, g.memset(l3_v[:, :, :, :], 0.0))
            g.memset(l3_v[:, :, :, D3:D3 + 1], 1.0).then_inc(l3_init, 1)
            g.memset(l3_qT[:, :, :, :], 0.0).then_inc(l3_init, 1)
            with g.Fori(0, B) as b:
                for j in range(N3):
                    g.wait_ge(l3_msd, b * N3 + (j + 1))
                    g.tensor_tensor(l3_rs[j % 2][:, :], l3_ms[j % 2][:, :], half_power[:, 0:H3], ALU.pow).then_inc(l3_rsd, 1)

        def l3x_scalar(act):
            norm_scalar(act, ln_l3x)
            act.preload_act_table(ACT.Exp)
            act.wait_ge(xT_cp, ln_l3x["cp_end"])
            act.wait_ge(l3_init, 2)
            with act.Fori(0, B) as b:
                act.wait_ge(l3_kv, b * N3)
                act.activation(l3_xb[:, :, :], xT[:, :, bass.ds(b * S, S)], ACT.Copy).then_inc(l3_xbd, 1)

                def project(j):
                    r = rows3(j)
                    act.wait_ge(l3_kv, b * N3 + (j + 1))
                    if j >= 3:
                        act.wait_ge(l3_pd, b * N3 + (j - 2))
                    ins = act.activation(l3_raw[j % 3][0:r, :], bank(6 + j % 2, D)[0:r, :], ACT.Copy)
                    if j < MC:
                        ins.then_inc(l3_kvd, 1)
                        ins = act.activation(l3_v[0:r, j, :, 0:D3],
                                             bank(6 + j % 2, D, D)[0:r, :].rearrange("p (h d) -> p h d", d=D3), ACT.Copy)
                        ins.then_inc(l3_kvd, 1)
                    else:
                        ins.then_inc(l3_kvd, 2)

                def turned(j):
                    r = rows3(j)
                    act.wait_ge(l3_T, b * N3 + (j + 1))
                    src = bank(4 + j % 2).bitcast(F16).rearrange("p (g m) -> p g m", g=NG)
                    if j < MC:
                        act.activation(l3_kT[:, :, j * P:j * P + r], src[:, :, 0:r], ACT.Copy).then_inc(l3_Td, 1)
                    else:
                        k = j - MC
                        for n in range(HG):
                            part = slice(n * W3, (n + 1) * W3)
                            ins = act.activation(l3_qT[part, :, n, k * P:(k + 1) * P], src[part, :, :], ACT.Copy)
                        ins.then_inc(l3_Td, 1)

                for j in range(N3 + 2):
                    if j < N3:
                        project(j)
                    if j >= 2:
                        turned(j - 2)
                for i in range(C3):
                    r = chunk_rows(i % MC)
                    act.wait_ge(l3_s, b * C3 + (i + 1))
                    if i >= 3:
                        act.wait_ge(l3_pv, b * C3 + (i - 2))
                    act.activation(l3_p[i % 3][0:r, :], psum[0:r, (i % 2) * 2 * BANK:(i % 2 + 1) * 2 * BANK], ACT.Exp,
                                   scale=float(D3) ** -0.5).then_inc(l3_e, 1)

        def l3x_vector(v):
            v.wait_ge(x_upd, X_AT[6])
            for n in range(3):
                ins = v.memset(l3_raw[n][:, :], 0.0)
            dve_steps.then(v, ins)
            norm_vector(v, ln_l3x, x)
            with v.Fori(0, B) as b:
                dve_steps.enter(b, 4 * N3 + 2 * NG)

                def squares(j):
                    v.wait_ge(l3_kvd, b * (2 * N3) + (2 * j + 1))
                    raw = l3_raw[j % 3][:, :]
                    dve_steps.then(v, v.tensor_tensor(l3_sq[j % 2][:, :], raw, raw, ALU.mult))
                    dve_steps.then(v, v.tensor_reduce(l3_ms[j % 2][:, :], l3_sq[j % 2][:, :].rearrange("p (h d) -> p h d", d=D3),
                                                      AX.X, ALU.add))
                    v.tensor_scalar(l3_ms[j % 2][:, :], l3_ms[j % 2][:, :], 1.0 / D3, RMS_EPS, ALU.mult, ALU.add)\
                        .then_inc(l3_msd, 1)

                def pair(j):
                    v.wait_ge(l3_rsd, b * N3 + (j + 1))
                    norm = l3_n[j % 2][:, :].rearrange("p (h d) -> p h d", d=D3)
                    dve_steps.then(v, v.tensor_tensor(norm, l3_raw[j % 3][:, :].rearrange("p (h d) -> p h d", d=D3),
                                                      l3_rs[j % 2][:, :].unsqueeze(2).to_broadcast([P, H3, D3]), ALU.mult))
                    if j >= 2:
                        v.wait_ge(l3_T, b * N3 + (j - 1))
                    both = norm.unsqueeze(2).to_broadcast([P, H3, 2, D3])
                    pairs = l3_pairs[j % 2]
                    hi, lo = (pairs[:, :, 0::2, :], pairs[:, :, 1::2, :]) if j < MC else (pairs[:, :, 0:2, :], pairs[:, :, 2:4, :])
                    dve_steps.then(v, v.tensor_copy(hi, both))
                    v.tensor_tensor(lo, both, hi, ALU.subtract).then_inc(l3_pd, 1)

                for j in range(N3 + 1):
                    if j < N3:
                        squares(j)
                    if j >= 1:
                        pair(j - 1)
                for n in range(NG):
                    v.wait_ge(l3_pv, b * C3 + (n + 1) * MC)
                    v.tensor_copy(l3_o[n % 2][:, :], bank(4 + n % 2, S)).then_inc(l3_od, 1)
                    v.wait_ge(l3_oT, b * NG + (n + 1))
                    got = bank(6, TB * P).rearrange("p (k h d) -> p k h d", k=TB, h=HG)
                    dve_steps.then(v, v.reciprocal(l3_rec[:, :, :], got[:, :, :, D3]))
                    dve_steps.then(v, v.tensor_tensor(l3_y[:, :, :, :], got[:, :, :, 0:D3],
                                                      l3_rec[:, :, :].unsqueeze(3).to_broadcast([P, TB, HG, D3]), ALU.mult))
                    row = x[:, bass.ds(b * TB, TB), n * HG * D3:(n + 1) * HG * D3]
                    v.tensor_tensor(row, row, l3_y[:, :, :, :].rearrange("p k h d -> p k (h d)"), ALU.add).then_inc(x_upd, 1)
            dve_steps.leave(B)

        def l3x_tensor(pe):
            norm_tensor(pe, ln_l3x)
            pe.wait_ge(l3_wland, 32)
            with pe.Fori(0, B) as b:
                pe.wait_ge(l3_cland, b * 16 + 16)
                pe.wait_ge(l3_xbd, b + 1)
                pe.wait_ge(x_upd, b * NG + X_AT[6])

                def project(j):
                    r = rows3(j)
                    if j >= 2:
                        pe.wait_ge(l3_kvd, b * (2 * N3) + 2 * (j - 1))
                    width = 2 * D if j < MC else D
                    for c in range(DC):
                        lhs = l3_ctx[:, c, j * P:j * P + r] if j < MC else l3_xb[:, c, (j - MC) * P:(j - MC + 1) * P]
                        mm = pe.matmul(bank(6 + j % 2, width)[0:r, :], lhs, (l3_wkv if j < MC else l3_wq)[:, c, :],
                                       start=(c == 0), stop=(c == DC - 1))
                    mm.then_inc(l3_kv, 1)

                def turn(j):
                    pe.wait_ge(l3_pd, b * N3 + (j + 1))
                    if j >= 2:
                        pe.wait_ge(l3_Td, b * N3 + (j - 1))
                    dst = bank(4 + j % 2).bitcast(F16)
                    src = l3_pairs[j % 2][:, :, :, :].rearrange("p h a d -> p (h a d)")
                    for n in range(NG):
                        mm = pe.transpose(dst[:, n * P:(n + 1) * P], src[:, n * P:(n + 1) * P], identh[:, :])
                    mm.then_inc(l3_T, 1)

                def scores(i):
                    n, j = i // MC, i % MC
                    r = chunk_rows(j)
                    if i >= 2:
                        pe.wait_ge(l3_e, b * C3 + (i - 1))
                    for a in range(2):
                        mm = pe.matmul(bank(i % 2 * 2 + a)[0:r, :], l3_kT[:, n, j * P:j * P + r],
                                       l3_qT[:, n, 2 * a:2 * a + 2, :].rearrange("p h s -> p (h s)"), start=True, stop=True)
                    mm.then_inc(l3_s, 1)

                def values(i):
                    n, j = i // MC, i % MC
                    r = chunk_rows(j)
                    pe.wait_ge(l3_e, b * C3 + (i + 1))
                    if j == 0 and n >= 2:
                        pe.wait_ge(l3_od, b * NG + (n - 1))
                    for a in range(HG):
                        mm = pe.matmul(bank(4 + n % 2, S)[a * 32:(a + 1) * 32, :], l3_v[0:r, j, n * HG + a, :],
                                       l3_p[i % 3][0:r, a * S:(a + 1) * S], start=(j == 0), stop=(j == MC - 1))
                    mm.then_inc(l3_pv, 1)

                def out(n):
                    pe.wait_ge(l3_od, b * NG + (n + 1))
                    if n >= 1:
                        pe.wait_ge(x_upd, b * NG + (n + X_AT[6]))
                    for k in range(TB):
                        mm = pe.transpose(bank(6, P, k * P), l3_o[n % 2][:, k * P:(k + 1) * P], ident[:, :])
                    mm.then_inc(l3_oT, 1)

                for j in range(N3 + 2):
                    if j < N3:
                        project(j)
                    if j >= 2:
                        turn(j - 2)
                pe.wait_ge(l3_Td, (b + 1) * N3)
                scores(0)
                for i in range(C3):
                    if i + 1 < C3:
                        scores(i + 1)
                    values(i)
                    if i % MC == 2 and i >= MC:
                        out(i // MC - 1)
                out(NG - 1)

        ln_l3f = norm_plan(False, False)
        MAGIC = 1.5 * 2 ** 23
        FC = FF3 // P
        f3 = ExitStack()
        f3_w = [sb(f"f3_w{n}", [P, DC * FF3], F32, f3) for n in range(3)]
        f3_wq = [sb(f"f3_wq{n}", [P, DC * FF3], BF16, f3) for n in range(3)]
        f3_wsum = sb("f3_wsum", [P, 3], F32, f3)
        f3_ws, f3_wr = sb("f3_ws", [P, 3], F32, f3), sb("f3_wr", [P, 3], F32, f3)
        f3_xmax, f3_xs, f3_xr = (sb(f"f3_x{n}", [P, NT], F32, f3) for n in ("max", "s", "r"))
        f3_sg, f3_su = sb("f3_sg", [P, NT], F32, f3), sb("f3_su", [P, NT], F32, f3)
        f3_xq = sb("f3_xq", [P, NT, D], F32, f3)
        f3_xb = sb("f3_xb", [P, NT, D], BF16, f3)
        f3_xT = sb("f3_xT", [P, DC, NTOK], BF16, f3)
        f3_g = [sb(f"f3_g{n}", [P, FF3], F32, f3) for n in range(2)]
        f3_h = [sb(f"f3_h{n}", [P, FF3], F32, f3) for n in range(2)]
        f3_hb = [sb(f"f3_hb{n}", [P, FF3], BF16, f3) for n in range(2)]
        f3_hT = [sb(f"f3_hT{n}", [P, FC, P], BF16, f3) for n in range(2)]
        f3_hmax, f3_hs, f3_hr = (sb(f"f3_h{n}", [P, TB], F32, f3) for n in ("max", "s", "r"))
        f3_hd = sb("f3_hd", [P, TB], F32, f3)
        f3_sgt, f3_sut = sb("f3_sgt", [P, TB], F32, f3), sb("f3_sut", [P, TB], F32, f3)
        f3.close()
        f3_wland = sems("f3_wland", 3)
        (f3_wsumd, f3_wtot, f3_wqd, f3_xbd, f3_xTp, f3_xTd, f3_scd, f3_gu, f3_gd, f3_hq, f3_hbd, f3_hTp, f3_hTd,
         f3_dn) = (sem(n) for n in (
             "f3_wsumd f3_wtot f3_wqd f3_xbd f3_xTp f3_xTd f3_scd f3_gu f3_gd f3_hq f3_hbd f3_hTp f3_hTd "
             "f3_dn").split())

        def l3f_sync(sp):
            sp.wait_ge(x_upd, X_AT[7])
            for n, name in enumerate(("L3_gate", "L3_up", "L3_down")):
                sp.dma_start(f3_w[n][:, :], t[name].rearrange("p c n -> p (c n)")).then_inc(f3_wland[n], 16)
            with sp.Fori(0, B) as b:
                sp.wait_ge(x_upd, b * TB + (X_AT[7] + TB))
                sp.dma_start(out[bass.ds(b, 1)].rearrange("o (k p) d -> p (o k) d", p=P), x[:, bass.ds(b * TB, TB), :])\
                    .then_inc(out_done, 16)
            sp.wait_ge(out_done, 16 * B)

        def l3f_pool(g):
            pass

        def l3f_vector(v):
            v.wait_ge(x_upd, X_AT[7])
            for n in range(3):
                v.wait_ge(f3_wland[n], 16)
                v.tensor_reduce(f3_wsum[:, n:n + 1], f3_w[n][:, :], AX.X, ALU.add, apply_absolute_value=True)\
                    .then_inc(f3_wsumd, 1)
            norm_vector(v, ln_l3f, x)
            v.wait_ge(xn_done, NT * (ln_l3f["k"] + 1))
            dve_steps.then(v, v.tensor_reduce(f3_xmax[:, :], xn[:, :, :], AX.X, ALU.max, apply_absolute_value=True))
            dve_steps.then(v, v.tensor_scalar(f3_xs[:, :], f3_xmax[:, :], 1.0 / 127, 1e-5, ALU.mult, ALU.add))
            dve_steps.then(v, v.reciprocal(f3_xr[:, :], f3_xs[:, :]))
            for n in range(NT):
                ins = v.tensor_scalar(f3_xq[:, n, :], xn[:, n, :], f3_xr[:, n:n + 1], MAGIC, ALU.mult, ALU.add)
            dve_steps.then(v, ins)
            dve_steps.then(v, v.tensor_scalar(f3_xq[:, :, :], f3_xq[:, :, :], MAGIC - 128, MAGIC + 127, ALU.max, ALU.min))
            v.tensor_scalar(f3_xb[:, :, :], f3_xq[:, :, :], MAGIC, None, ALU.subtract).then_inc(f3_xbd, 1)
            v.wait_ge(f3_wtot, 1)
            dve_steps.then(v, v.tensor_scalar(f3_ws[:, :], bank(6, 3), 1.0 / (D * FF3), 1e-5, ALU.mult, ALU.add))
            dve_steps.then(v, v.reciprocal(f3_wr[:, :], f3_ws[:, :]))
            for n in range(3):
                dve_steps.then(v, v.tensor_scalar(f3_w[n][:, :], f3_w[n][:, :], f3_wr[:, n:n + 1], MAGIC, ALU.mult, ALU.add))
                dve_steps.then(v, v.tensor_scalar(f3_w[n][:, :], f3_w[n][:, :], MAGIC - 1, MAGIC + 1, ALU.max, ALU.min))
                v.tensor_scalar(f3_wq[n][:, :], f3_w[n][:, :], MAGIC, None, ALU.subtract).then_inc(f3_wqd, 1)
            v.tensor_scalar(f3_sg[:, :], f3_xs[:, :], f3_ws[:, 0:1], None, ALU.mult)
            dve_steps.then(v, v.tensor_scalar(f3_su[:, :], f3_xs[:, :], f3_ws[:, 1:2], None, ALU.mult))
            for hf in range(2):
                for c in range(DC):
                    if c == 0:
                        v.wait_ge(f3_xTp, hf + 1)
                    v.tensor_copy(f3_xT[:, c, hf * HALF:(hf + 1) * HALF], bank(2 * c + hf).bitcast(BF16)[:, 0:HALF])\
                        .then_inc(f3_xTd, 1)
            with v.Fori(0, B) as b:
                dve_steps.enter(b, TB * 5)
                for k in range(TB):
                    n = b * TB + k
                    v.tensor_copy(f3_sgt[:, k:k + 1], f3_sg[:, bass.ds(n, 1)])
                    v.tensor_copy(f3_sut[:, k:k + 1], f3_su[:, bass.ds(n, 1)]).then_inc(f3_scd, 1)
                for k in range(TB):
                    v.wait_ge(f3_scd, (b + 1) * TB)
                    v.wait_ge(f3_gd, b * TB + (k + 1))
                    dve_steps.then(v, v.scalar_tensor_tensor(f3_h[k][:, :], psum[:, 2 * BANK:4 * BANK], f3_sut[:, k:k + 1],
                                                             f3_g[k][:, :], ALU.mult, ALU.mult))
                    dve_steps.then(v, v.tensor_reduce(f3_hmax[:, k:k + 1], f3_h[k][:, :], AX.X, ALU.max, apply_absolute_value=True))
                    dve_steps.then(v, v.tensor_scalar(f3_hs[:, k:k + 1], f3_hmax[:, k:k + 1], 1.0 / 127, 1e-5, ALU.mult, ALU.add))
                    v.tensor_scalar(f3_hd[:, k:k + 1], f3_hs[:, k:k + 1], f3_ws[:, 2:3], None, ALU.mult)
                    dve_steps.then(v, v.reciprocal(f3_hr[:, k:k + 1], f3_hs[:, k:k + 1]))
                    dve_steps.then(v, v.tensor_scalar(f3_h[k][:, :], f3_h[k][:, :], f3_hr[:, k:k + 1], MAGIC, ALU.mult, ALU.add))
                    v.tensor_scalar(f3_h[k][:, :], f3_h[k][:, :], MAGIC - 128, MAGIC + 127, ALU.max, ALU.min).then_inc(f3_hq, 1)
                for k in range(TB):
                    v.wait_ge(f3_dn, b * TB + (k + 1))
                    row = x[:, bass.ds(b * TB + k, 1), :].rearrange("p o d -> p (o d)")
                    v.scalar_tensor_tensor(row, bank(6 + k, D), f3_hd[:, k:k + 1], row, ALU.mult, ALU.add).then_inc(x_upd, 1)
            dve_steps.leave(B)

        def l3f_scalar(act):
            act.preload_act_table(ACT.Silu)
            with act.Fori(0, B) as b:
                for k in range(TB):
                    act.wait_ge(f3_scd, (b + 1) * TB)
                    act.wait_ge(f3_gu, b * TB + (k + 1))
                    act.activation(f3_g[k][:, :], psum[:, 0:2 * BANK], ACT.Silu, scale=f3_sgt[:, k:k + 1]).then_inc(f3_gd, 1)
                for k in range(TB):
                    act.wait_ge(f3_hq, b * TB + (k + 1))
                    act.activation(f3_hb[k][:, :], f3_h[k][:, :], ACT.Copy, bias=-MAGIC).then_inc(f3_hbd, 1)
                    act.wait_ge(f3_hTp, b * TB + (k + 1))
                    act.activation(f3_hT[k][:, :, :].rearrange("p c n -> p (c n)"), bank(4 + k).bitcast(BF16), ACT.Copy)\
                        .then_inc(f3_hTd, 1)

        def l3f_tensor(pe):
            pe.wait_ge(f3_wsumd, 3)
            pe.wait_ge(x_upd, X_AT[7])
            pe.matmul(bank(6, 3), ones[:, :], f3_wsum[:, :], start=True, stop=True).then_inc(f3_wtot, 1)
            pe.wait_ge(f3_xbd, 1)
            for n in range(NT):
                for c in range(DC):
                    mm = pe.transpose(bank(2 * c + n // 4).bitcast(BF16)[:, n % 4 * P:(n % 4 + 1) * P],
                                      f3_xb[:, n, c * P:(c + 1) * P], identb[:, :])
                if n % 4 == 3:
                    mm.then_inc(f3_xTp, 1)
            pe.wait_ge(f3_xTd, 2 * DC)
            pe.wait_ge(f3_wqd, 3)
            gate, up = (f3_wq[n][:, :].rearrange("p (c f) -> p c f", c=DC) for n in range(2))
            down = f3_wq[2][:, :].rearrange("p (c d) -> p c d", c=FC)
            with pe.Fori(0, B) as b:
                for k in range(TB):
                    pe.wait_ge(f3_hq, b * TB + k)
                    for w, at in ((gate, 0), (up, 2)):
                        for a in range(2):
                            for c in range(DC):
                                mm = pe.matmul(bank(at + a), f3_xT[:, c, bass.ds(b * S + k * P, P)],
                                               w[:, c, a * BANK:(a + 1) * BANK], start=(c == 0), stop=(c == DC - 1))
                    mm.then_inc(f3_gu, 1)
                for k in range(TB):
                    pe.wait_ge(f3_hbd, b * TB + (k + 1))
                    for c in range(FC):
                        mm = pe.transpose(bank(4 + k).bitcast(BF16)[:, c * P:(c + 1) * P], f3_hb[k][:, c * P:(c + 1) * P],
                                          identb[:, :])
                    mm.then_inc(f3_hTp, 1)
                    pe.wait_ge(f3_hTd, b * TB + (k + 1))
                    for c in range(FC):
                        mm = pe.matmul(bank(6 + k, D), f3_hT[k][:, c, :], down[:, c, :], start=(c == 0), stop=(c == FC - 1))
                    mm.then_inc(f3_dn, 1)

        block = stack.enter_context(nc.Block())

        @block.sync
        def _(sp):
            sp.dma_start(x[:, :, :], t["x"].rearrange("b (k p) d -> p (b k) d", p=P)).then_inc(x_land, 16)
            l0x_sync(sp)
            moe_sync(sp, "L0")
            moe_sync(sp, "L1")
            l2x_sync(sp)
            moe_sync(sp, "L2")
            l3x_sync(sp)
            l3f_sync(sp)

        @block.gpsimd
        def _(g):
            constants_pool(g)
            norm_pool(g, ln_l0x)
            norm_pool(g, moe_plan["L0"]["ln"])
            moe_pool(g, "L0")
            norm_pool(g, ln_l1z)
            norm_pool(g, ln_l1y)
            norm_pool(g, moe_plan["L1"]["ln"])
            moe_pool(g, "L1")
            norm_pool(g, ln_l2x)
            l2x_pool(g)
            norm_pool(g, moe_plan["L2"]["ln"])
            moe_pool(g, "L2")
            norm_pool(g, ln_l3x)
            l3x_pool(g)
            norm_pool(g, ln_l3f)
            l3f_pool(g)

        @block.scalar
        def _(act):
            parameters_scalar(act)
            norm_scalar(act, ln_l0x)
            l0x_scalar(act)
            moe_scalar(act, "L0")
            l1x_scalar(act)
            moe_scalar(act, "L1")
            l2x_scalar(act)
            moe_scalar(act, "L2")
            l3x_scalar(act)
            l3f_scalar(act)

        @block.vector
        def _(v):
            v.wait_ge(x_land, 16)
            norm_vector(v, ln_l0x, x)
            l0x_vector(v)
            moe_vector(v, "L0")
            l1x_vector(v)
            moe_vector(v, "L1")
            l2x_vector(v)
            moe_vector(v, "L2")
            l3x_vector(v)
            l3f_vector(v)

        @block.tensor
        def _(pe):
            pe.wait_ge(consts, NCONST)
            norm_tensor(pe, ln_l0x)
            l0x_tensor(pe)
            moe_tensor(pe, "L0")
            l1x_tensor(pe)
            moe_tensor(pe, "L1")
            l2x_tensor(pe)
            moe_tensor(pe, "L2")
            l3x_tensor(pe)
            l3f_tensor(pe)


def kernel(**inputs):
    import numpy as _np
    import ml_dtypes as _ml
    import concourse.bacc as _bacc
    from concourse import mybir as _mybir
    from concourse.bass_utils import run_bass_kernel_spmd as _run

    a = {k: _np.asarray(v) for k, v in inputs.items()}

    def width_first(w):
        return w.reshape(w.shape[0], DC, P).transpose(2, 1, 0)

    def expert_chunks(name, gate, up, down):
        n = moe_chunks(name)
        pad = _np.zeros((n * P - gate.shape[0], D), _np.float32)
        full = [_np.concatenate([w, pad]).reshape(n, P, D) for w in (gate, up, down)]
        lhs = [w.reshape(n, P, DC, P).transpose(0, 3, 2, 1).reshape(n, P, DC * P) for w in full[:2]]
        return _np.concatenate([*lhs, full[2]], axis=2)

    def expert_rows(name):
        experts, hidden, shared = MOE[name]
        rows = _np.arange(moe_chunks(name) * P)
        which = _np.where(rows < experts * hidden, rows // hidden, experts)
        one = which[None, :] == _np.arange(experts + (shared > 0))[:, None]
        return _np.concatenate([one] * 3).astype(_ml.bfloat16)

    e0, h0, _ = MOE["L0"]
    e1, h1, s1 = MOE["L1"]
    e2, h2, _ = MOE["L2"]
    ctx = a["ctx_2048"]
    data = {
        "x": a["x"],
        "ctx": ctx,
        "ctx_T": ctx.reshape(B, M, DC, P).transpose(0, 3, 2, 1),
        "mask": a["mask_BxS2_bk0"],
        "L0_w": expert_chunks("L0", a["L0_ffn_w_gate_proj"].reshape(e0 * h0, D),
                              a["L0_ffn_w_up_proj"].reshape(e0 * h0, D),
                              a["L0_ffn_w_down_proj"].transpose(0, 2, 1).reshape(e0 * h0, D)),
        "L0_router": width_first(a["L0_ffn_gate_w"]),
        "L0_rows": expert_rows("L0"),
        "decay": a["L1_xattn_decay"].reshape(1, 1),
        "L1_in": width_first(a["L1_xattn_W_in"]),
        "L1_out": width_first(a["L1_xattn_W_out"]),
        "L1_bin": a["L1_xattn_b_in"].reshape(DC, P).T,
        "L1_bout": a["L1_xattn_b_out"].reshape(DC, P).T,
        "L1_gamma": a["L1_xattn_gamma"].reshape(1, D),
        "L1_beta": a["L1_xattn_beta"].reshape(1, D),
        "L1_w": expert_chunks("L1",
                              _np.concatenate([a["L1_ffn_W1"].transpose(0, 2, 1).reshape(e1 * h1, D), a["L1_ffn_sw1"]]),
                              _np.concatenate([a["L1_ffn_W3"].transpose(0, 2, 1).reshape(e1 * h1, D), a["L1_ffn_sw3"]]),
                              _np.concatenate([a["L1_ffn_W2"].reshape(e1 * h1, D), a["L1_ffn_sw2"].T])),
        "L1_router": width_first(a["L1_ffn_gate_w"]),
        "L1_rbias": a["L1_ffn_router_bias"].reshape(1, e1),
        "L1_rows": expert_rows("L1"),
        "L2_w": expert_chunks("L2", a["L2_ffn_Wg"].transpose(0, 2, 1).reshape(e2 * h2, D),
                              a["L2_ffn_Wu"].transpose(0, 2, 1).reshape(e2 * h2, D),
                              a["L2_ffn_Wd"].reshape(e2 * h2, D)),
        "L2_router": width_first(a["L2_ffn_Wr"].T),
        "L2_rbias": a["L2_ffn_br"].reshape(1, e2),
        "L2_rows": expert_rows("L2"),
    }
    def rope(fn):
        freq = 1.0 / _np.float32(10000.0) ** (_np.arange(0, HD, 2, dtype=_np.float32) / _np.float32(HD))
        angle = _np.outer(_np.arange(S, dtype=_np.float32), freq.astype(_np.float32)).astype(_np.float32)
        return fn(angle).astype(_np.float32).reshape(TB, P, HD // 2).transpose(1, 0, 2)

    def by_head(w, heads):
        return w.reshape(DC, P, KH, heads * HD).transpose(2, 1, 0, 3)

    data.update({
        "rope_cos": rope(_np.cos), "rope_sin": rope(_np.sin),
        "L2_qw": a["L2_xattn_q_norm_w"].reshape(1, HD), "L2_kw": a["L2_xattn_k_norm_w"].reshape(1, HD),
        "L2_kwc": a["L2_xattn_k_norm_w"].reshape(HD, 1),
        "L2_w_qkv": _np.concatenate([by_head(a[f"L2_xattn_{n}"], 1) for n in ("wk_ctx", "wv_ctx", "wk", "wv")]
                                    + [by_head(a["L2_xattn_wq"], REP)], axis=3),
        "L2_wo": a["L2_xattn_wo"].reshape(QH, HD, D).transpose(1, 0, 2),
    })
    wkv3 = _np.concatenate([a["L3_xattn_Wk"], a["L3_xattn_Wv"]])
    data.update({
        "L3_kv": width_first(_np.concatenate([wkv3[0::2], wkv3[1::2]])),
        "L3_q": width_first(a["L3_xattn_Wq"]),
        "L3_gate": width_first(a["L3_ffn_w_gate"]),
        "L3_up": width_first(a["L3_ffn_w_up"]),
        "L3_down": a["L3_ffn_w_down"].T.reshape(FF3 // P, P, D).transpose(1, 0, 2),
    })
    nc = _bacc.Bacc("TRN2", target_bir_lowering=False, num_devices=1)
    arrays, args = {}, {}
    for name, value in data.items():
        value = _np.ascontiguousarray(value)
        arrays[f"in_{name}_dram"] = value
        kind = _mybir.dt.uint8 if value.dtype == bool else _mybir.dt.from_np(value.dtype)
        args[name] = nc.dram_tensor(f"in_{name}_dram", value.shape, kind,
                                    kind="ExternalInput").ap()
    out = nc.dram_tensor("out_0_dram", (B, S, D), _mybir.dt.float32, kind="ExternalOutput").ap()
    program(nc, args, out)
    r = _run(nc, [arrays], core_ids=[0])
    return r.results[0]["out_0_dram"]
```

```python
from contextlib import ExitStack

import numpy as np

import concourse.bass as bass
from concourse import mybir

F32 = mybir.dt.float32
F32R = mybir.dt.float32r
BF16 = mybir.dt.bfloat16
F16 = mybir.dt.float16
U8 = mybir.dt.uint8
ACT = mybir.ActivationFunctionType
ALU = mybir.AluOpType
AX = mybir.AxisListType

P = 128
B, S, D = 4, 256, 256
DC = D // P
TB = S // P
NT = B * TB
NTOK = B * S
M = 1601
MC = -(-M // P)
ML = M - (MC - 1) * P
BANK = 512
HALF = NTOK // 2
LN_EPS = 1e-5
RMS_EPS = 1e-6
BIG = 1e30
LOWEST = -3.0e38

MOE = {"L0": (32, 96, 0), "L1": (8, 176, 352), "L2": (4, 1024, 0)}

QH, KH, HD = 16, 4, 128
REP = QH // KH
H3, D3 = 32, 8
HG = 4
NG = H3 // HG
FF3 = 1024


def chunk_rows(j):
    return P if j < MC - 1 else ML


def moe_chunks(name):
    experts, hidden, shared = MOE[name]
    n = -(-(experts * hidden + shared) // P)
    return n + n % 2


class Steps:

    def __init__(self, sem):
        self.sem, self.base, self.done, self.i, self.per = sem, 0, 0, None, 0

    def then(self, engine, instruction):
        instruction.then_inc(self.sem, 1)
        self.done += 1
        value = self.base + self.done
        engine.wait_ge(self.sem, value if self.i is None else self.i * self.per + value)

    def enter(self, i, per):
        self.base, self.done, self.i, self.per = self.base + self.done, 0, i, per

    def leave(self, turns):
        assert self.done == self.per, (self.done, self.per)
        self.base, self.done, self.i = self.base + turns * self.per, 0, None



def program(nc, t, out):
    with ExitStack() as stack:

        def sem(name):
            return stack.enter_context(nc.semaphore(name))

        def sems(name, n):
            return [sem(f"{name}{i}") for i in range(n)]

        def sb(name, shape, dt=F32, scope=stack):
            return scope.enter_context(nc.sbuf_tensor(name, shape, dt))

        psum = stack.enter_context(nc.psum_tensor("psum", [P, 8 * BANK], F32))

        def bank(n, width=BANK, at=0):
            return psum[:, n * BANK + at:n * BANK + at + width]

        x = sb("x", [P, NT, D])
        xn = sb("xn", [P, NT, D])
        xT = sb("xT", [P, DC, NTOK])
        ident = sb("ident", [P, P])
        identb = sb("identb", [P, P], BF16)
        identh = sb("identh", [P, P], F16)
        half_power = sb("half_power", [P, 2 * HD])
        zerob = sb("zerob", [1, BANK], BF16)
        ones = sb("ones", [P, P])
        stats = sb("stats", [P, NT, 6])
        mv = sb("mv", [P, NT, 2])
        veps = sb("veps", [P, NT])
        rstd = sb("rstd", [P, NT])

        decay_raw = sb("decay_raw", [P, 1])
        decay_k = sb("decay_k", [P, 1])
        decay_sum = sb("decay_sum", [P, DC, B])
        decay_total = sb("decay_total", [P, 1])

        r_earlier = sb("r_earlier", [P, 8, 8])
        l1_in, l1_out = sb("l1_in", [P, DC, D]), sb("l1_out", [P, DC, D])
        l1_bin, l1_bout = sb("l1_bin", [P, DC]), sb("l1_bout", [P, DC])
        l1_gamma, l1_beta = sb("l1_gamma", [P, D]), sb("l1_beta", [P, D])
        causal = sb("causal", [P, BANK], BF16)
        causal_T = sb("causal_T", [P, REP, P], BF16)
        x_land = sem("x_land")
        consts = sem("consts")
        x_upd = sem("x_upd")
        ln_stats, ln_mv, ln_veps, ln_rstd = sem("ln_stats"), sem("ln_mv"), sem("ln_veps"), sem("ln_rstd")
        xn_done = sem("xn_done")
        xT_ps = sem("xT_ps")
        xT_cp = sem("xT_cp")
        xT_lo = sem("xT_lo")
        dve_steps = Steps(sem("dve_steps"))
        pool_steps = Steps(sem("pool_steps"))
        out_done = sem("out_done")
        NCONST = 7

        UPDATES = [NT, NT, NT, NT, 2 * B * KH * TB, NT, B * NG, NT]
        X_AT = [sum(UPDATES[:k]) for k in range(len(UPDATES) + 1)]

        norm_count = {"k": 0, "ps": 0, "cp": 0, "lo": 0}

        def norm_plan(transposed, split):
            at = dict(norm_count, transposed=transposed, split=split)
            norm_count["k"] += 1
            if transposed:
                norm_count["ps"] += 2
                norm_count["cp"] += 4
                if split:
                    norm_count["lo"] += 4
            at["cp_end"], at["lo_end"] = norm_count["cp"], norm_count["lo"]
            return at

        def norm_vector(v, at, src):
            k = at["k"]
            for n in range(NT):
                v.bn_stats(stats[:, n, :], src[:, n, :]).then_inc(ln_stats, 1)
            v.wait_ge(ln_stats, NT * (k + 1))
            for n in range(NT):
                v.bn_aggr(mv[:, n, :], stats[:, n, :]).then_inc(ln_mv, 1)
            v.wait_ge(ln_mv, NT * (k + 1))
            v.tensor_scalar(veps[:, :], mv[:, :, 1], LN_EPS, None, ALU.add).then_inc(ln_veps, 1)
            v.wait_ge(ln_rstd, k + 1)
            for n in range(NT):
                v.tensor_scalar(xn[:, n, :], src[:, n, :], mv[:, n, 0:1], rstd[:, n:n + 1],
                                ALU.subtract, ALU.mult).then_inc(xn_done, 1)
            if at["split"]:
                for q in range(4):
                    hf, c = q // 2, q % 2
                    v.wait_ge(xT_cp, at["cp"] + q + 1)
                    cols = slice(hf * HALF, (hf + 1) * HALF)
                    v.tensor_tensor(xlo[:, c, cols], bank(2 * c + hf), xhi[:, c, cols].bitcast(F32),
                                    ALU.subtract).then_inc(xT_lo, 1)

        def norm_pool(g, at):
            g.wait_ge(ln_veps, at["k"] + 1)
            g.tensor_tensor(rstd[:, :], veps[:, :], half_power[:, 0:NT], ALU.pow).then_inc(ln_rstd, 1)

        def norm_tensor(pe, at):
            for n in range(NT):
                pe.wait_ge(xn_done, NT * at["k"] + n + 1)
                for c in range(DC):
                    last_t = pe.transpose(bank(2 * c + n // 4, P, (n % 4) * P),
                                          xn[:, n, c * P:(c + 1) * P], ident[:, :])
                if n % 4 == 3:
                    last_t.then_inc(xT_ps, 1)

        def norm_scalar(act, at):
            dst = xhi if at["split"] else xT
            for q in range(4):
                hf, c = q // 2, q % 2
                act.wait_ge(xT_ps, at["ps"] + hf + 1)
                act.activation(dst[:, c, hf * HALF:(hf + 1) * HALF], bank(2 * c + hf),
                               ACT.Copy).then_inc(xT_cp, 1)

        ln_l0x = norm_plan(True, False)
        l0 = ExitStack()
        c_T = [sb(f"c_T{s}", [P, DC, M], F32, l0) for s in range(2)]
        c_N = [sb(f"c_N{s}", [P, MC, D], F32, l0) for s in range(2)]
        c_mask = [sb(f"c_mask{s}", [P, M], U8, l0) for s in range(2)]
        c_bias = [sb(f"c_bias{s}", [P, M], F32, l0) for s in range(2)]
        c_any = [sb(f"c_any{s}", [P, 1], F32, l0) for s in range(2)]
        l0_xb = [sb(f"l0_xb{s}", [P, DC, S], F32, l0) for s in range(2)]
        l0_sm = [sb(f"l0_sm{n}", [P, M], F32, l0) for n in range(TB)]
        l0_p = [sb(f"l0_p{n}", [P, M], F32, l0) for n in range(TB)]
        l0_pt = [sb(f"l0_pt{n}", [P, MC, P], F32, l0) for n in range(TB)]
        l0_mx = sb("l0_mx", [P, TB], F32, l0)
        l0_nmx = sb("l0_nmx", [P, TB], F32, l0)
        l0_sum = sb("l0_sum", [P, TB], F32, l0)
        l0_rec = sb("l0_rec", [P, TB], F32, l0)
        l0_top = sb("l0_top", [P, 1], F32, l0)
        l0_gate = sb("l0_gate", [P, TB], F32, l0)
        decay_geo = sb("decay_geo", [P, M], F32, l0)
        decay_junk = sb("decay_junk", [P, M], F32, l0)
        decay_tmp = [sb(f"decay_tmp{s}", [P, DC], F32, l0) for s in range(2)]
        l0.close()
        c_land = sems("c_land", 2)
        decay_land, decay_sig = sem("decay_land"), sem("decay_sig")
        l0_xbd, l0_s, l0_masked, l0_shift = sem("l0_xbd"), sem("l0_s"), sem("l0_masked"), sem("l0_shift")
        l0_exp, l0_T, l0_ptd = sem("l0_exp"), sem("l0_T"), sem("l0_ptd")
        l0_pv = sems("l0_pv", 2)
        l0_decayed = sems("l0_decayed", 2)
        TG = -(-MC // 4)

        def l0x_sync(sp):
            with sp.Fori(0, B // 2) as i:
                for s in range(2):
                    n = i * 2 + s
                    sp.wait_ge(l0_pv[s], i * TB)
                    sp.wait_ge(l0_decayed[s], i)
                    one = bass.ds(n, 1)
                    sp.dma_start(c_T[s][:, :, :], t["ctx_T"][one].rearrange("o p c m -> p (o c) m"))\
                        .then_inc(c_land[s], 16)
                    sp.dma_start(c_mask[s][:, :], t["mask"][one, :].to_broadcast([P, M]))\
                        .then_inc(c_land[s], 16)
                    sp.dma_start(c_N[s][:, 0:MC - 1, :],
                                 t["ctx"][one, 0:(MC - 1) * P, :].rearrange("o (j p) d -> p (o j) d", p=P))\
                        .then_inc(c_land[s], 16)
                    sp.dma_start(c_N[s][0:ML, MC - 1, :],
                                 t["ctx"][one, (MC - 1) * P:M, :].rearrange("o p d -> p (o d)"))\
                        .then_inc(c_land[s], 16)

        def l0x_scalar(act):
            act.wait_ge(decay_land, 16)
            act.activation(decay_k[:, :], decay_raw[:, :], ACT.Sigmoid).then_inc(decay_sig, 1)
            act.preload_act_table(ACT.Exp)
            act.wait_ge(xT_cp, ln_l0x["cp_end"])
            with act.Fori(0, B // 2) as i:
                for s in range(2):
                    n = i * 2 + s
                    act.activation(l0_xb[s][:, :, :], xT[:, :, bass.ds(n * S, S)], ACT.Copy)\
                        .then_inc(l0_xbd, 1)
                    for k in range(TB):
                        act.wait_ge(l0_shift, i * 4 + 2 * s + k + 1)
                        act.activation(l0_p[k][:, :], l0_sm[k][:, :], ACT.Exp, bias=l0_nmx[:, k:k + 1],
                                       accum_out=l0_sum[:, k:k + 1]).then_inc(l0_exp, 1)
                    for k in range(TB):
                        for q in range(TG):
                            act.wait_ge(l0_T, (i * 4 + 2 * s + k) * TG + q + 1)
                            if q < TG - 1:
                                ins = act.activation(l0_pt[k][:, 4 * q:4 * q + 4, :], bank(4 + q % 2), ACT.Copy)
                            else:
                                ins = act.activation(l0_pt[k][0:ML, MC - 1, :], bank(4 + q % 2, P)[0:ML, :], ACT.Copy)
                            ins.then_inc(l0_ptd, 1)

        def l0x_vector(v):
            v.wait_ge(decay_sig, 1)
            v.wait_ge(consts, NCONST)
            dve_steps.then(v, v.tensor_tensor_scan(decay_geo[:, :], decay_k[:, 0:1].to_broadcast([P, M]),
                                                   ones[:, 0:1].to_broadcast([P, M]), 0.0, ALU.mult, ALU.add))
            dve_steps.then(v, v.tensor_reduce(decay_total[:, :], decay_geo[:, :], AX.X, ALU.add))
            with v.Fori(0, B // 2) as i:
                dve_steps.enter(i, 2 * (5 + 2 * TB))
                for s in range(2):
                    n = i * 2 + s
                    v.wait_ge(c_land[s], 64 * (i + 1))
                    dve_steps.then(v, v.tensor_scalar(c_bias[s][:, :], c_mask[s][:, :], 16 * BIG, -16 * BIG,
                                                      ALU.mult, ALU.add))
                    dve_steps.then(v, v.tensor_reduce(l0_top[:, :], c_bias[s][:, :], AX.X, ALU.max))
                    dve_steps.then(v, v.tensor_scalar(c_any[s][:, :], l0_top[:, :], -1.0, None, ALU.is_ge))
                    for k in range(TB):
                        v.wait_ge(l0_s, i * 4 + 2 * s + k + 1)
                        v.memset(l0_gate[:, k:k + 1], 0.0)
                        v.tensor_tensor_reduce(l0_sm[k][:, :], psum[:, 0:M], c_bias[s][:, :], 1.0 / 16, LOWEST,
                                               ALU.add, ALU.max, l0_mx[:, k:k + 1]).then_inc(l0_masked, 1)
                        v.wait_ge(l0_masked, i * 4 + 2 * s + k + 1)
                        v.tensor_scalar(l0_nmx[:, k:k + 1], l0_mx[:, k:k + 1], -1.0, None, ALU.mult)\
                            .then_inc(l0_shift, 1)
                    for c in range(DC):
                        ins = v.tensor_tensor_reduce(decay_junk[:, :], c_T[s][:, c, :], decay_geo[:, ::-1], 1.0, 0.0,
                                                     ALU.mult, ALU.add, decay_tmp[s][:, c:c + 1])
                        dve_steps.then(v, ins)
                    v.tensor_copy(decay_sum[:, :, bass.ds(n, 1)], decay_tmp[s][:, :].rearrange("p (c o) -> p c o", o=1))\
                        .then_inc(l0_decayed[s], 1)
                    for k in range(TB):
                        v.wait_ge(l0_exp, i * 4 + 2 * s + k + 1)
                        dve_steps.then(v, v.reciprocal(l0_rec[:, k:k + 1], l0_sum[:, k:k + 1]))
                        dve_steps.then(v, v.tensor_tensor(l0_rec[:, k:k + 1], l0_rec[:, k:k + 1], c_any[s][:, :], ALU.mult))
                        v.wait_ge(l0_pv[s], i * TB + k + 1)
                        row = x[:, bass.ds(n * TB + k, 1), :].rearrange("p o d -> p (o d)")
                        v.scalar_tensor_tensor(row, bank(6 + k, D), l0_rec[:, k:k + 1], row,
                                               ALU.mult, ALU.add).then_inc(x_upd, 1)
            dve_steps.leave(B // 2)

        def l0x_tensor(pe):
            with pe.Fori(0, B // 2) as i:
                for s in range(2):
                    pe.wait_ge(c_land[s], 64 * (i + 1))
                    pe.wait_ge(l0_xbd, i * 2 + s + 1)
                    for k in range(TB):
                        pe.wait_ge(l0_masked, i * 4 + 2 * s + k)
                        for a in range(0, M, BANK):
                            z = min(a + BANK, M)
                            for c in range(DC):
                                mm = pe.matmul(psum[:, a:z], l0_xb[s][:, c, k * P:(k + 1) * P], c_T[s][:, c, a:z],
                                               start=(c == 0), stop=(c == DC - 1))
                        mm.then_inc(l0_s, 1)
                    for k in range(TB):
                        tile = i * 4 + 2 * s + k
                        pe.wait_ge(l0_exp, tile + 1)
                        for q in range(TG):
                            if q >= 2:
                                pe.wait_ge(l0_ptd, tile * TG + q - 1)
                            for j in range(4 * q, min(4 * q + 4, MC)):
                                r = chunk_rows(j)
                                mm = pe.transpose(bank(4 + q % 2, P, (j % 4) * P)[0:r, :],
                                                  l0_p[k][:, j * P:j * P + r], ident[:, :])
                            mm.then_inc(l0_T, 1)
                        for j in range(MC):
                            if j % 4 == 0:
                                pe.wait_ge(l0_ptd, tile * TG + j // 4 + 1)
                            r = chunk_rows(j)
                            mm = pe.matmul(bank(6 + k, D), l0_pt[k][0:r, j, :], c_N[s][0:r, j, :],
                                           start=(j == 0), stop=(j == MC - 1))
                        mm.then_inc(l0_pv[s], 1)

        def constants_pool(g):
            for tile in (ident, identb, identh):
                pool_steps.then(g, g.memset(tile[:, :], 0.0))
                g.affine_select(out=tile[:, :], in_=tile[:, :], compare_op=ALU.not_equal, fill=1.0,
                                base=0, pattern=[[-1, P]], channel_multiplier=1).then_inc(consts, 1)
            pool_steps.then(g, g.memset(half_power[:, :], -0.5))
            g.memset(ones[:, :], 1.0).then_inc(consts, 1)
            g.memset(zerob[:, :], 0.0).then_inc(consts, 1)
            pool_steps.then(g, g.memset(causal[:, :], 0.0))
            g.affine_select(out=causal[:, BANK - P:], in_=causal[:, BANK - P:], compare_op=ALU.is_ge, fill=-BIG,
                            base=0, pattern=[[-1, P]], channel_multiplier=1).then_inc(consts, 1)
            pool_steps.then(g, g.memset(causal_T[:, :, :], 0.0))
            g.affine_select(out=causal_T[:, :, :], in_=causal_T[:, :, :], compare_op=ALU.is_ge, fill=-BIG,
                            base=0, pattern=[[0, REP], [1, P]], channel_multiplier=-1).then_inc(consts, 1)
            pool_steps.then(g, g.memset(r_earlier[:, :, :], 1.0))
            g.affine_select(out=r_earlier[:, :, :], in_=r_earlier[:, :, :], compare_op=ALU.is_gt, fill=0.0,
                            base=0, pattern=[[1, 8], [-1, 8]], channel_multiplier=0).then_inc(early_done, 1)

        def parameters_scalar(act):
            act.dma_start(decay_raw[:, :], t["decay"].to_broadcast([P, 1])).then_inc(decay_land, 16)
            for dst, name in ((l1_in, "L1_in"), (l1_out, "L1_out"), (l1_bin, "L1_bin"), (l1_bout, "L1_bout")):
                act.dma_start(dst[...], t[name]).then_inc(l1_land, 16)
            for dst, name in ((l1_gamma, "L1_gamma"), (l1_beta, "L1_beta")):
                act.dma_start(dst[:, :], t[name].to_broadcast([P, D])).then_inc(l1_land, 16)

        EMAX = 32
        moe = ExitStack()
        xhi = sb("xhi", [P, DC, NTOK], F32R, moe)
        xlo = sb("xlo", [P, DC, NTOK], F32R, moe)
        w_stage = [sb(f"w_stage{s}", [P, 3 * D], F32, moe) for s in range(2)]
        w_hi_gu = [sb(f"w_hi_gu{s}", [P, 2 * D], F32R, moe) for s in range(2)]
        w_lo_gu = [sb(f"w_lo_gu{s}", [P, 2 * D], F32R, moe) for s in range(2)]
        w_hi_d = [sb(f"w_hi_d{s}", [P, D], F32R, moe) for s in range(2)]
        w_lo_d = [sb(f"w_lo_d{s}", [P, D], F32R, moe) for s in range(2)]
        e_silu = [sb(f"e_silu{s}", [P, HALF], F32, moe) for s in range(2)]
        e_h = [sb(f"e_h{s}", [P, HALF], F32, moe) for s in range(2)]
        e_hhi = [sb(f"e_hhi{s}", [P, HALF], F32R, moe) for s in range(2)]
        e_hlo = [sb(f"e_hlo{s}", [P, HALF], F32R, moe) for s in range(2)]
        e_out = sb("e_out", [P, DC, HALF], F32, moe)
        e_rows = sb("e_rows", [3 * EMAX, max(moe_chunks(n) for n in MOE) * P], BF16, moe)
        r_w = sb("r_w", [P, DC, EMAX], F32, moe)
        r_whi = sb("r_whi", [P, DC, EMAX], F32R, moe)
        r_wlo = sb("r_wlo", [P, DC, EMAX], F32R, moe)
        r_bias = {"L1": sb("r_bias1", [P, 8], F32, moe), "L2": sb("r_bias2", [P, 4], F32, moe)}
        r_log = sb("r_log", [P, NT, EMAX], F32, moe)
        r_logsT = sb("r_logsT", [EMAX, NTOK], F32, moe)
        r_a = sb("r_a", [P, NT, EMAX], F32, moe)
        r_b = sb("r_b", [P, NT, EMAX], F32, moe)
        r_top = sb("r_top", [P, NT, 8], F32, moe)
        r_sum = sb("r_sum", [P, NT], F32, moe)
        r_pair = sb("r_pair", [P, NT, 8, 8], F32, moe)
        r_tie = sb("r_tie", [P, NT, 8, 8], F32, moe)
        r_route = sb("r_route", [P, NT, EMAX], F32, moe)
        r_parts = sb("r_parts", [P, NT, 3 * EMAX], BF16, moe)
        r_T = sb("r_T", [3 * EMAX, NTOK], BF16, moe)
        moe.close()

        rows_land, rw_land, rw_split = sem("rows_land"), sem("rw_land"), sem("rw_split")
        rbias_land, early_done = sem("rbias_land"), sem("early_done")
        r_logT, r_logTd = sem("r_logT"), sem("r_logTd")
        r_logits, r_in, r_acted, r_done, r_Tps, r_Tcp = (sem(n) for n in (
            "r_logits", "r_in", "r_acted", "r_done", "r_Tps", "r_Tcp"))
        w_land, w_gu, w_d = sems("w_land", 2), sems("w_gu", 2), sems("w_d", 2)
        e_gu, e_act, e_hd, e_down = sems("e_gu", 2), sems("e_act", 2), sems("e_hd", 2), sems("e_down", 2)
        e_acc, e_outd, e_T = sem("e_acc"), sem("e_outd"), sem("e_T")
        G_BANK, U_BANK, R_BANK = (2, 3), (4, 5), (6, 7)

        def three(pe, dst, lhs, rhs, start, stop):
            pe.matmul(dst, lhs[0], rhs[0], start=start, stop=False)
            pe.matmul(dst, lhs[0], rhs[1], start=False, stop=False)
            return pe.matmul(dst, lhs[1], rhs[0], start=False, stop=stop)

        moe_plan = {}

        def moe_prepare(name, index, layer):
            experts, hidden, shared = MOE[name]
            plan = {"ln": norm_plan(True, True), "index": index, "n": moe_chunks(name), "experts": experts,
                    "slots": experts + (shared > 0), "x_at": X_AT[layer],
                    "pairs": sum(moe_chunks(m) for m in list(MOE)[:index])}
            moe_plan[name] = plan

        def moe_sync(sp, name):
            p = moe_plan[name]
            pairs = p["n"] // 2
            sp.wait_ge(x_upd, p["x_at"])
            n3, E = 3 * p["slots"], p["experts"]
            sp.dma_start(e_rows[0:n3, 0:p["n"] * P], t[f"{name}_rows"]).then_inc(rows_land, 16)
            sp.dma_start(r_w[:, :, 0:E], t[f"{name}_router"]).then_inc(rw_land, 16)
            if name in r_bias:
                sp.dma_start(r_bias[name][:, :], t[f"{name}_rbias"].to_broadcast([P, E])).then_inc(rbias_land, 16)
            for hf in range(2):
                m0 = p["pairs"] + hf * pairs
                with sp.Fori(0, pairs) as i:
                    for s in range(2):
                        sp.wait_ge(w_d[s], i + m0)
                        sp.dma_start(w_stage[s][:, :], t[f"{name}_w"][bass.ds(i * 2 + s, 1)]
                                     .rearrange("o p n -> p (o n)")).then_inc(w_land[s], 16)

        def moe_pool(g, name):
            p = moe_plan[name]
            pairs = p["n"] // 2
            for hf in range(2):
                m0 = p["pairs"] + hf * pairs
                with g.Fori(0, pairs) as i:
                    pool_steps.enter(i, 4)
                    for s in range(2):
                        g.wait_ge(w_land[s], i * 16 + 16 * (m0 + 1))
                        g.wait_ge(e_gu[s], i + m0)
                        gu = w_stage[s][:, 0:2 * D]
                        pool_steps.then(g, g.tensor_tensor(w_hi_gu[s][:, :], gu, ones[:, 0:1].to_broadcast([P, 2 * D]), ALU.mult))
                        g.tensor_tensor(w_lo_gu[s][:, :], gu, w_hi_gu[s][:, :].bitcast(F32), ALU.subtract)\
                            .then_inc(w_gu[s], 1)
                        g.wait_ge(e_down[s], i + m0)
                        d = w_stage[s][:, 2 * D:3 * D]
                        pool_steps.then(g, g.tensor_tensor(w_hi_d[s][:, :], d, ones[:, 0:1].to_broadcast([P, D]), ALU.mult))
                        g.tensor_tensor(w_lo_d[s][:, :], d, w_hi_d[s][:, :].bitcast(F32), ALU.subtract)\
                            .then_inc(w_d[s], 1)
                pool_steps.leave(pairs)

        def moe_scalar(act, name):
            p = moe_plan[name]
            norm_scalar(act, p["ln"])
            k, E = p["index"], p["experts"]
            for hf in range(2):
                act.wait_ge(r_logT, 2 * k + hf + 1)
                act.activation(r_logsT[0:E, hf * HALF:(hf + 1) * HALF], bank(6 + hf)[0:E, :], ACT.Copy).then_inc(r_logTd, 1)
            act.wait_ge(r_in, k + 1)
            if name == "L0":
                act.activation(r_a[:, :, 0:E], r_a[:, :, 0:E], ACT.Exp)
                act.activation(r_b[:, :, 0:E], r_b[:, :, 0:E], ACT.Exp).then_inc(r_acted, 1)
            else:
                act.activation(r_a[:, :, 0:E], r_log[:, :, 0:E], ACT.Sigmoid if name == "L1" else ACT.Exp)\
                    .then_inc(r_acted, 1)
            pairs = p["n"] // 2
            act.preload_act_table(ACT.Silu)
            for hf in range(2):
                m0 = p["pairs"] + hf * pairs
                with act.Fori(0, pairs) as i:
                    for s in range(2):
                        act.wait_ge(e_gu[s], i + (m0 + 1))
                        act.activation(e_silu[s][:, :], bank(G_BANK[s]), ACT.Silu).then_inc(e_act[s], 1)
                act.wait_ge(e_acc, 2 * k + hf + 1)
                for c in range(DC):
                    act.activation(e_out[:, c, :], bank(c), ACT.Copy).then_inc(e_outd, 1)

        def route_topk(v, E, k, scores):
            def by(ap, axis):
                return ap.unsqueeze(axis).to_broadcast([P, NT, E, E])
            pair, tie = r_pair[:, :, 0:E, 0:E], r_tie[:, :, 0:E, 0:E]
            other, own = by(scores, 2), by(scores, 3)
            dve_steps.then(v, v.tensor_tensor(tie, other, own, ALU.is_equal))
            dve_steps.then(v, v.tensor_tensor(tie, tie, r_earlier[:, 0:E, 0:E].unsqueeze(1).to_broadcast([P, NT, E, E]), ALU.mult))
            dve_steps.then(v, v.tensor_tensor(pair, other, own, ALU.is_gt))
            dve_steps.then(v, v.tensor_tensor(pair, pair, tie, ALU.add))
            dve_steps.then(v, v.tensor_reduce(r_b[:, :, 0:E], pair, AX.X, ALU.add))
            dve_steps.then(v, v.tensor_scalar(r_b[:, :, 0:E], r_b[:, :, 0:E], k - 0.5, None, ALU.is_lt))

        def moe_vector(v, name):
            p = moe_plan[name]
            k, E, n_slots = p["index"], p["experts"], p["slots"]
            v.wait_ge(x_upd, p["x_at"])
            norm_vector(v, p["ln"], x)
            v.wait_ge(rw_land, 16 * (k + 1))
            dve_steps.then(v, v.tensor_copy(r_whi[:, :, 0:E], r_w[:, :, 0:E]))
            v.tensor_tensor(r_wlo[:, :, 0:E], r_w[:, :, 0:E], r_whi[:, :, 0:E].bitcast(F32), ALU.subtract)\
                .then_inc(rw_split, 1)
            v.wait_ge(r_logits, k + 1)
            lg = bank(5, NT * E).rearrange("p (k e) -> p k e", k=NT)
            a, b, log, route = (r[:, :, 0:E] for r in (r_a, r_b, r_log, r_route))

            def wide(col):
                return col.unsqueeze(2).to_broadcast([P, NT, E])

            if name == "L0":
                dve_steps.then(v, v.tensor_copy(log, lg))
                for n in range(NT):
                    ins = v.max(r_top[:, n, :], log[:, n, :])
                dve_steps.then(v, ins)
                for n in range(NT):
                    ins = v.match_replace(b[:, n, :], r_top[:, n, :], log[:, n, :], -BIG)
                dve_steps.then(v, ins)
                dve_steps.then(v, v.tensor_tensor(a, log, wide(r_top[:, :, 0]), ALU.subtract))
                v.tensor_tensor(b, b, wide(r_top[:, :, 0]), ALU.subtract).then_inc(r_in, 1)
                v.wait_ge(r_acted, k + 1)
                dve_steps.then(v, v.tensor_tensor(route, a, b, ALU.subtract))
                dve_steps.then(v, v.tensor_reduce(r_sum[:, :], route, AX.X, ALU.add))
                dve_steps.then(v, v.reciprocal(r_sum[:, :], r_sum[:, :]))
                dve_steps.then(v, v.tensor_tensor(route, route, wide(r_sum[:, :]), ALU.mult))
            elif name == "L1":
                v.tensor_copy(log, lg).then_inc(r_in, 1)
                v.wait_ge(rbias_land, 16)
                v.wait_ge(early_done, 1)
                v.wait_ge(r_acted, k + 1)
                dve_steps.then(v, v.tensor_tensor(log, a, r_bias[name][:, :].unsqueeze(1).to_broadcast([P, NT, E]), ALU.add))
                route_topk(v, E, 2, log)
                dve_steps.then(v, v.tensor_tensor(route, a, b, ALU.mult))
                dve_steps.then(v, v.tensor_reduce(r_sum[:, :], route, AX.X, ALU.add))
                dve_steps.then(v, v.tensor_scalar(r_sum[:, :], r_sum[:, :], 1e-12, None, ALU.max))
                dve_steps.then(v, v.reciprocal(r_sum[:, :], r_sum[:, :]))
                dve_steps.then(v, v.tensor_tensor(route, route, wide(r_sum[:, :]), ALU.mult))
                dve_steps.then(v, v.memset(r_route[:, :, E:E + 1], 1.0))
            else:
                v.wait_ge(rbias_land, 32)
                dve_steps.then(v, v.tensor_tensor(log, lg, r_bias[name][:, :].unsqueeze(1).to_broadcast([P, NT, E]), ALU.add))
                dve_steps.then(v, v.tensor_reduce(r_sum[:, :], log, AX.X, ALU.max))
                v.tensor_tensor(log, log, wide(r_sum[:, :]), ALU.subtract).then_inc(r_in, 1)
                v.wait_ge(r_acted, k + 1)
                dve_steps.then(v, v.tensor_reduce(r_sum[:, :], a, AX.X, ALU.add))
                dve_steps.then(v, v.reciprocal(r_sum[:, :], r_sum[:, :]))
                dve_steps.then(v, v.tensor_tensor(a, a, wide(r_sum[:, :]), ALU.mult))
                route_topk(v, E, 1, a)
                dve_steps.then(v, v.tensor_tensor(route, a, b, ALU.mult))
            route = r_route[:, :, 0:n_slots]
            rest = r_a[:, :, 0:n_slots]
            parts = [r_parts[:, :, i * n_slots:(i + 1) * n_slots] for i in range(3)]
            dve_steps.then(v, v.tensor_copy(parts[0], route))
            dve_steps.then(v, v.tensor_tensor(rest, route, parts[0], ALU.subtract))
            dve_steps.then(v, v.tensor_copy(parts[1], rest))
            v.tensor_tensor(parts[2], rest, parts[1], ALU.subtract)\
                .then_inc(r_done, 1)
            v.wait_ge(r_Tps, k + 1)
            v.tensor_copy(r_T[0:3 * n_slots, :], bank(7).bitcast(BF16)[0:3 * n_slots, :]).then_inc(r_Tcp, 1)
            pairs = p["n"] // 2
            for hf in range(2):
                m0 = p["pairs"] + hf * pairs
                with v.Fori(0, pairs) as i:
                    dve_steps.enter(i, 6)
                    for s in range(2):
                        v.wait_ge(e_act[s], i + (m0 + 1))
                        dve_steps.then(v, v.tensor_tensor(e_silu[s][:, :], bank(U_BANK[s]), e_silu[s][:, :], ALU.mult))
                        dve_steps.then(v, v.tensor_tensor(e_h[s][:, :], bank(R_BANK[s]), e_silu[s][:, :], ALU.mult))
                        v.wait_ge(e_down[s], i + m0)
                        dve_steps.then(v, v.tensor_copy(e_hhi[s][:, :], e_h[s][:, :]))
                        v.tensor_tensor(e_hlo[s][:, :], e_h[s][:, :], e_hhi[s][:, :].bitcast(F32), ALU.subtract)\
                            .then_inc(e_hd[s], 1)
                dve_steps.leave(pairs)
                for n in range(NT // 2):
                    if n % 2 == 0:
                        v.wait_ge(e_T, 2 * k + hf + 1)
                    tile = x[:, hf * (NT // 2) + n, :]
                    v.tensor_tensor(tile, bank((3, 5)[n // 2], D, (n % 2) * D), tile, ALU.add).then_inc(x_upd, 1)

        def moe_tensor(pe, name):
            p = moe_plan[name]
            k, E, n3 = p["index"], p["experts"], 3 * p["slots"]
            norm_tensor(pe, p["ln"])

            def gate_up(s, pair, cols):
                pe.wait_ge(w_gu[s], pair + 1)
                pe.wait_ge(e_hd[s], pair)
                for at, dst in ((0, G_BANK), (D, U_BANK)):
                    for c in range(DC):
                        w = slice(at + c * P, at + (c + 1) * P)
                        three(pe, bank(dst[s]), (w_hi_gu[s][:, w], w_lo_gu[s][:, w]),
                              (xhi[:, c, cols], xlo[:, c, cols]), c == 0, c == DC - 1)

            def weigh(s, chunk, cols):
                pe.matmul(bank(R_BANK[s]), e_rows[0:n3, chunk], r_T[0:n3, cols], start=True, stop=True).then_inc(e_gu[s], 1)

            def down(s, pair):
                pe.wait_ge(w_d[s], pair + 1)
                pe.wait_ge(e_hd[s], pair + 1)
                for c in range(DC):
                    w = slice(c * P, (c + 1) * P)
                    mm = pe.matmul(bank(c), w_hi_d[s][:, w], e_hhi[s][:, :], start=False, stop=False, skip_group_check=True)
                    mm = pe.matmul(bank(c), w_hi_d[s][:, w], e_hlo[s][:, :], start=False, stop=False, skip_group_check=True)
                    mm = pe.matmul(bank(c), w_lo_d[s][:, w], e_hhi[s][:, :], start=False, stop=False, skip_group_check=True)
                mm.then_inc(e_down[s], 1)

            pe.wait_ge(rw_split, k + 1)
            pe.wait_ge(xT_lo, p["ln"]["lo_end"])
            for hf in range(2):
                tok = slice(hf * HALF, (hf + 1) * HALF)
                for c in range(DC):
                    mm = three(pe, bank(6 + hf)[0:E, :], (r_whi[:, c, 0:E], r_wlo[:, c, 0:E]),
                               (xhi[:, c, tok], xlo[:, c, tok]), c == 0, c == DC - 1)
                mm.then_inc(r_logT, 1)
            pe.wait_ge(r_logTd, 2 * (k + 1))
            for n in range(NT):
                mm = pe.transpose(bank(5, E, n * E), r_logsT[0:E, n * P:(n + 1) * P], ident[0:E, 0:E])
            mm.then_inc(r_logits, 1)
            gate_up(0, p["pairs"], slice(0, HALF))
            pe.wait_ge(r_done, k + 1)
            for n in range(NT):
                mm = pe.transpose(bank(7).bitcast(BF16)[0:n3, n * P:(n + 1) * P],
                                  r_parts[:, n, 0:n3], identb[:, :])
            mm.then_inc(r_Tps, 1)
            pe.wait_ge(r_Tcp, k + 1)
            pe.wait_ge(rows_land, 16 * (k + 1))
            pairs = p["n"] // 2
            for hf in range(2):
                m0 = p["pairs"] + hf * pairs
                cols = slice(hf * HALF, (hf + 1) * HALF)
                if hf == 1:
                    pe.wait_ge(x_upd, p["x_at"] + NT // 2)
                for c in range(DC):
                    pe.matmul(bank(c), zerob[:, 0:P], zerob[:, :], start=True, stop=False, skip_group_check=True)
                if hf == 0:
                    weigh(0, slice(0, P), cols)
                with pe.Fori(0, pairs - 1) as i:
                    gate_up(1, i + m0, cols)
                    weigh(1, bass.ds(i * 2 * P + P, P), cols)
                    down(0, i + m0)
                    gate_up(0, i + (m0 + 1), cols)
                    weigh(0, bass.ds(i * 2 * P + 2 * P, P), cols)
                    down(1, i + m0)
                gate_up(1, m0 + pairs - 1, cols)
                weigh(1, slice((p["n"] - 1) * P, p["n"] * P), cols)
                down(0, m0 + pairs - 1)
                down(1, m0 + pairs - 1)
                for c in range(DC):
                    mm = pe.matmul(bank(c), zerob[:, 0:P], zerob[:, :], start=False, stop=True, skip_group_check=True)
                mm.then_inc(e_acc, 1)
                if hf == 0:
                    second = slice(HALF, 2 * HALF)
                    gate_up(0, m0 + pairs, second)
                    weigh(0, slice(0, P), second)
                for n in range(NT // 2):
                    for c in range(DC):
                        if n == 0:
                            pe.wait_ge(e_outd, 4 * k + 2 * hf + c + 1)
                        mm = pe.transpose(bank((3, 5)[n // 2], P, (n % 2) * D + c * P),
                                          e_out[:, c, n * P:(n + 1) * P], ident[:, :])
                mm.then_inc(e_T, 1)

        moe_prepare("L0", 0, 1)

        ln_l1z = norm_plan(False, False)
        ln_l1y = norm_plan(False, False)
        l1 = ExitStack()
        l1_bsum = sb("l1_bsum", [P, DC], F32, l1)
        l1_mean = sb("l1_mean", [P, DC, B], F32, l1)
        l1_summ = sb("l1_summ", [P, DC, B], F32, l1)
        l1_wide = sb("l1_wide", [P, DC, B, P], F32, l1)
        l1_y = sb("l1_y", [P, NT, D], F32, l1)
        l1.close()
        l1_land, l1_h, l1_meand, l1_s, l1_wided, l1_b = (sem(n) for n in (
            "l1_land", "l1_h", "l1_meand", "l1_s", "l1_wided", "l1_b"))

        def l1x_scalar(act):
            pass

        def l1x_vector(v):
            v.wait_ge(x_upd, X_AT[2])
            norm_vector(v, ln_l1z, x)
            v.wait_ge(l1_land, 16 * 6)
            dve_steps.then(v, v.tensor_scalar(l1_bsum[:, :], l1_bin[:, :], decay_total[:, 0:1], None, ALU.mult))
            v.wait_ge(l1_h, 1)
            for c in range(DC):
                v.tensor_scalar(l1_mean[:, c, :], bank(0, B, c * B), l1_bsum[:, c:c + 1], 1.0 / M,
                                ALU.add, ALU.mult).then_inc(l1_meand, 1)
            v.wait_ge(l1_s, 1)
            for c in range(DC):
                ins = v.tensor_scalar(l1_summ[:, c, :], bank(1, B, c * B), l1_bout[:, c:c + 1], None, ALU.add)
            dve_steps.then(v, ins)
            v.tensor_copy(l1_wide[:, :, :, :].rearrange("p c b n -> p (c b) n"),
                          l1_summ[:, :, :].rearrange("p c b -> p (c b)").unsqueeze(2).to_broadcast([P, DC * B, P]))\
                .then_inc(l1_wided, 1)
            v.wait_ge(l1_b, 1)
            v.wait_ge(xn_done, NT * (ln_l1z["k"] + 1))
            for n in range(NT):
                b = n // TB
                ins = v.tensor_tensor(l1_y[:, n, :], xn[:, n, :], bank(2 + b // 2, D, (b % 2) * D), ALU.add)
            dve_steps.then(v, ins)
            norm_vector(v, ln_l1y, l1_y)
            v.wait_ge(xn_done, NT * (ln_l1y["k"] + 1))
            gamma = l1_gamma[:, :].unsqueeze(1).to_broadcast([P, NT, D])
            beta = l1_beta[:, :].unsqueeze(1).to_broadcast([P, NT, D])
            dve_steps.then(v, v.tensor_tensor(xn[:, :, :], xn[:, :, :], gamma, ALU.mult))
            dve_steps.then(v, v.tensor_tensor(xn[:, :, :], xn[:, :, :], beta, ALU.add))
            for n in range(NT):
                v.tensor_tensor(x[:, n, :], x[:, n, :], xn[:, n, :], ALU.add).then_inc(x_upd, 1)

        def l1x_tensor(pe):
            pe.wait_ge(l1_land, 16 * 6)
            pe.wait_ge(x_upd, X_AT[2])
            for e in range(DC):
                for c in range(DC):
                    mm = pe.matmul(bank(0, B, e * B), l1_in[:, c, e * P:(e + 1) * P], decay_sum[:, c, :],
                                   start=(c == 0), stop=(c == DC - 1))
            mm.then_inc(l1_h, 1)
            pe.wait_ge(l1_meand, DC)
            for e in range(DC):
                for c in range(DC):
                    mm = pe.matmul(bank(1, B, e * B), l1_out[:, c, e * P:(e + 1) * P], l1_mean[:, c, :],
                                   start=(c == 0), stop=(c == DC - 1))
            mm.then_inc(l1_s, 1)
            pe.wait_ge(l1_wided, 1)
            for b in range(B):
                for c in range(DC):
                    mm = pe.matmul(bank(2 + b // 2, P, (b % 2) * D + c * P), l1_wide[:, c, b, :], ident[:, :],
                                   start=True, stop=True)
            mm.then_inc(l1_b, 1)

        moe_prepare("L1", 1, 3)

        ln_l2x = norm_plan(True, False)
        l2 = ExitStack()
        KC = MC + TB
        KG = -(-KC // 4)
        MX = M + S
        U = REP * TB
        QW = REP * P
        TURNS = B * KH
        l2_ctx = sb("l2_ctx", [P, DC, M], F32, l2)
        l2_w = sb("l2_w", [P, DC, 4 * HD + REP * HD], F32, l2)
        l2_wo = sb("l2_wo", [P, QH, D], F32, l2)
        l2_xb = sb("l2_xb", [P, DC, S], F32, l2)
        l2_kraw = [sb(f"l2_kraw{n}", [P, 4, HD], F32, l2) for n in range(2)]
        l2_kn = [sb(f"l2_kn{n}", [P, 4, HD], F32, l2) for n in range(2)]
        l2_ra = sb("l2_ra", [P, TB, HD], F32, l2)
        l2_rb = sb("l2_rb", [P, TB, HD], F32, l2)
        l2_q = sb("l2_q", [P, TB, REP, HD], F32, l2)
        l2_qa = sb("l2_qa", [P, TB, REP, HD], F32, l2)
        l2_qb = sb("l2_qb", [P, TB, REP, HD], F32, l2)
        l2_vhi = [sb(f"l2_vhi{s}", [P, KC, HD], F32R, l2) for s in range(2)]
        l2_vlo = [sb(f"l2_vlo{s}", [P, KC, HD], F32R, l2) for s in range(2)]
        l2_kThi = [sb(f"l2_kThi{s}", [P, MX + 1], F32R, l2) for s in range(2)]
        l2_kTlo = [sb(f"l2_kTlo{s}", [P, MX + 1], F32R, l2) for s in range(2)]
        l2_qThi = [sb(f"l2_qThi{s}", [P, TB, QW], F32R, l2) for s in range(2)]
        l2_qTlo = [sb(f"l2_qTlo{s}", [P, TB, QW], F32R, l2) for s in range(2)]
        l2_m = [sb(f"l2_m{s}", [REP, TB, QW], F32R, l2) for s in range(2)]
        l2_p = [sb(f"l2_p{n}", [P, QW], F32, l2) for n in range(3)]
        l2_phi = [sb(f"l2_phi{n}", [P, QW], F32R, l2) for n in range(3)]
        l2_plo = [sb(f"l2_plo{n}", [P, QW], F32R, l2) for n in range(3)]
        l2_rec = [sb(f"l2_rec{k}", [P, REP], F32, l2) for k in range(TB)]
        parts = [xn[:, 2 * n:2 * n + 2, :].rearrange("p k d -> p (k d)") for n in range(2 * TB)]
        l2_acc, l2_oT = parts[:TB], parts[TB:]
        l2_cos, l2_sin = sb("l2_cos", [P, TB, HD // 2], F32, l2), sb("l2_sin", [P, TB, HD // 2], F32, l2)
        l2_qw, l2_kw = sb("l2_qw", [P, HD], F32, l2), sb("l2_kw", [P, HD], F32, l2)
        l2_kwc = sb("l2_kwc", [P, 1], F32, l2)
        rope_q = [sb(f"rope_q{n}", [P, TB, HD], F32, l2) for n in range(2)]
        rope_k = [sb(f"rope_k{n}", [P, TB, HD], F32, l2) for n in range(2)]
        l2_kms, l2_krs = sb("l2_kms", [P, KG, 4], F32, l2), sb("l2_krs", [P, KG, 4], F32, l2)
        l2_qms, l2_qrs = sb("l2_qms", [P, U], F32, l2), sb("l2_qrs", [P, U], F32, l2)
        l2_qsq, l2_ksq = sb("l2_qsq", [P, U], F32, l2), sb("l2_ksq", [P, KG, 4], F32, l2)
        l2_mx4, l2_mx = sb("l2_mx4", [P, U, KG], F32, l2), sb("l2_mx", [P, U], F32, l2)
        l2_ones = sb("l2_ones", [REP, P], F32R, l2)
        l2.close()
        (l2_cland, l2_wland, l2_pland, l2_proj, l2_qc, l2_kvc, l2_vl, l2_ksqd, l2_kmsd, l2_krsd, l2_qmsd, l2_qrsd,
         l2_knd, l2_kxd, l2_qnd, l2_kT, l2_kTh, l2_kTl, l2_qT, l2_qTh, l2_qTl, l2_near, l2_far, l2_top, l2_mT, l2_md, l2_s, l2_e,
         l2_lo, l2_accd, l2_pv, l2_sum, l2_inv, l2_o, l2_y) = (sem(n) for n in (
             "l2_cland l2_wland l2_pland l2_proj l2_qc l2_kvc l2_vl l2_ksqd l2_kmsd l2_krsd l2_qmsd l2_qrsd "
             "l2_knd l2_kxd l2_qnd l2_kT l2_kTh l2_kTl l2_qT l2_qTh l2_qTl l2_near l2_far l2_top l2_mT l2_md l2_s l2_e "
             "l2_lo l2_accd l2_pv l2_sum l2_inv l2_o l2_y").split())

        STEPS = [(k, j) for k in range(TB) for j in range(MC + k + 1)]
        NS = len(STEPS)
        TILE_END = [max(c for c in range(NS) if STEPS[c][0] == k) for k in range(TB)]
        NPROJ = TB + KC
        NQC = 1 + REP
        Q_AT, KV_AT = 0, TB
        QT_AT = [8, 10]
        KSQ_AT = [6, 10, 14, 17]
        KN_AT = [8, 12, 16, 19]
        KT_AT = [12, 14, 18, 20]
        SEARCH_AT = {13: [(0, 0, 0, 2)], 14: [(0, 0, 2, 2)], 15: [(0, 1, 0, 2)], 16: [(0, 1, 2, 2)], 17: [(1, 0, 0, 2)],
                     18: [(1, 0, 2, 2)], 19: [(0, 2, 0, 2)], 20: [(0, 2, 2, 2)], 21: [(0, 3, 0, 2)], 22: [(0, 3, 2, 2)],
                     23: [(1, 1, 0, 2)], 24: [(1, 1, 2, 2)], 25: [(1, 2, 0, 2)], 26: [(1, 2, 2, 2)], 27: [(1, 3, 0, 2)],
                     28: [(1, 3, 2, 2)]}
        TOP_AT = 22
        M_AT = 24
        M1_AT = 6
        PV_AT = [TILE_END[0] + 2, 1]
        SUM_AT = [21, 1]
        Y_AT = [(26, 28), (3, 5)]

        def max_pieces(c):
            return [(k, h, q) for k, q, first, n in SEARCH_AT.get(c, []) for h in range(first, first + n)]

        SEARCH = [piece for c in range(NS) for piece in max_pieces(c)]
        NM = len(SEARCH)
        assert NM == U * KG
        SHARED = []
        for c in range(NS):
            if c < NPROJ:
                SHARED.append(("project", c))
            SHARED += [("search", SEARCH.index(piece)) for piece in max_pieces(c)]

        def shared_bank(slot, kind, i):
            return 5 + (slot * len(SHARED) + SHARED.index((kind, i))) % 2

        def piece_cols(k, q):
            a, z = q * BANK, min(q * BANK + BANK, M + (k + 1) * P)
            return a - (z - a) % 2, z

        def key_cols(j):
            return (j * P, chunk_rows(j)) if j < MC else (M + (j - MC) * P, P)

        def need(engine, semaphore, count):
            if not (isinstance(count, int) and count <= 0):
                engine.wait_ge(semaphore, count)

        def ahead(c, by, g, n):
            return (g, c + by) if c + by < NS else (n, c + by - NS)

        def l2_turns(engine, turn, steps=None):
            turn(None, 1, 0)
            turn(0, 0, 1)
            with engine.Fori(0, TURNS // 2 - 1) as i:
                if steps:
                    steps.enter(i, 2 * L2_DVE_STEPS)
                for s in (1, 0):
                    g = i * 2 + (2 - s)
                    turn(g, s, i * 2 + (3 - s))
            if steps:
                steps.leave(TURNS // 2 - 1)
            turn(TURNS - 1, 1, None)

        def l2x_sync(sp):
            sp.wait_ge(x_upd, X_AT[4])
            for dst, name in ((l2_cos, "rope_cos"), (l2_sin, "rope_sin"), (l2_kwc, "L2_kwc"), (l2_wo, "L2_wo")):
                sp.dma_start(dst[...], t[name]).then_inc(l2_pland, 16)
            for dst, name in ((l2_qw, "L2_qw"), (l2_kw, "L2_kw")):
                sp.dma_start(dst[:, :], t[name].to_broadcast([P, HD])).then_inc(l2_pland, 16)
            sp.wait_ge(xT_cp, ln_l2x["cp_end"])
            with sp.Fori(0, B) as b:
                sp.wait_ge(l2_proj, b * (KH * NPROJ))
                sp.dma_start(l2_ctx[:, :, :], t["ctx_T"][bass.ds(b, 1)].rearrange("o p c m -> p (o c) m"))\
                    .then_inc(l2_cland, 16)
                sp.dma_start(l2_xb[:, :, :], xT[:, :, bass.ds(b * S, S)]).then_inc(l2_cland, 16)
                with sp.Fori(0, KH) as h:
                    sp.wait_ge(l2_proj, (b * KH + h) * NPROJ)
                    sp.dma_start(l2_w[:, :, :], t["L2_w_qkv"][bass.ds(h, 1)].rearrange("o p c n -> p (o c) n"))\
                        .then_inc(l2_wland, 16)

        def l2x_pool(g_):
            def sums(g, c):
                k, j = STEPS[c]
                if j == 0:
                    return
                r = key_cols(j)[1]
                if j == 1:
                    need(g_, l2_sum, g * TB + (k - 1))
                g_.wait_ge(l2_e, g * (2 * NS) + 2 * (c + 1))
                first = l2_p[(c - 1) % 3] if j == 1 else l2_acc[k]
                if j > 1:
                    g_.wait_ge(l2_accd, g * NS + c)
                g_.tensor_tensor(l2_acc[k][0:r, :], first[0:r, :], l2_p[c % 3][0:r, :], ALU.add)\
                    .then_inc(l2_accd, 2 if j == 1 else 1)

            def turn(g, slot, n):
                for c in range(NS):
                    at, step = ahead(c, 1, g, n)
                    if at is not None:
                        sums(at, step)
                    if n is None:
                        continue
                    if c == 2:
                        g_.wait_ge(l2_qmsd, n + 1)
                        g_.tensor_tensor(l2_qrs[:, :], l2_qms[:, :], half_power[:, 0:U], ALU.pow).then_inc(l2_qrsd, 1)
                    for q in range(KG):
                        if c == KSQ_AT[q]:
                            nb = min(4, KC - 4 * q)
                            g_.wait_ge(l2_kmsd, n * KG + (q + 1))
                            g_.tensor_tensor(l2_krs[:, q, 0:nb], l2_kms[:, q, 0:nb], half_power[:, 0:nb], ALU.pow).then_inc(l2_krsd, 1)
                            g_.wait_ge(l2_krsd, n * KG + (q + 1))
                            g_.tensor_tensor(l2_kn[q % 2][:, 0:nb, :], l2_kraw[q % 2][:, 0:nb, :],
                                             l2_krs[:, q, 0:nb].unsqueeze(2).to_broadcast([P, nb, HD]), ALU.mult)\
                                .then_inc(l2_knd, 1)

            l2_turns(g_, turn)

        def l2x_scalar(act):
            norm_scalar(act, ln_l2x)
            act.preload_act_table(ACT.Exp)
            act.wait_ge(l2_pland, 16 * 6)

            def exp(g, c):
                k, j = STEPS[c]
                r = key_cols(j)[1]
                act.wait_ge(l2_s, g * NS + (c + 1))
                last = c - 3 if c >= 3 else NS - 2 + c if c < 2 else NS - 3
                done = (g * NS + last if c >= 3 else g * NS + (last - NS)) + 1
                need(act, l2_pv, done)
                need(act, l2_accd, done)
                src = bank(c % 3)[0:r, :]
                act.activation(l2_phi[c % 3][0:r, :], src, ACT.Exp).then_inc(l2_e, 1)
                act.activation(l2_p[c % 3][0:r, :], src, ACT.Exp).then_inc(l2_e, 1)

            def products(g, k):
                act.wait_ge(l2_pv, g * NS + (TILE_END[k] + 1))
                need(act, l2_y, (g * TB + k - TB + 1) * 2)
                act.activation(l2_oT[k][:, :], bank(3 + k), ACT.Copy).then_inc(l2_o, 1)

            def turn(g, slot, n):
                new = 1 - slot
                for c in range(NS):
                    if n is not None and c < TB:
                        act.wait_ge(l2_proj, n * NPROJ + (c + 1))
                        need(act, l2_qT, n * TB)
                        need(act, l2_qnd, n)
                        src = bank(shared_bank(new, "project", c))
                        act.activation(l2_q[:, c, :, :], src, ACT.Copy).then_inc(l2_qc, 1)
                        for h in range(REP):
                            act.activation(l2_qa[:, c, h, :], src[:, h * HD:(h + 1) * HD], ACT.Square,
                                           accum_out=l2_qsq[:, c * REP + h:c * REP + h + 1]).then_inc(l2_qc, 1)
                    elif n is not None and c < NPROJ:
                        j = c - TB
                        r = key_cols(j)[1]
                        act.wait_ge(l2_proj, n * NPROJ + (c + 1))
                        if j % 4 == 0:
                            need(act, l2_knd, n * KG + (j // 4 - 1))
                        kv = bank(shared_bank(new, "project", c), 2 * HD)
                        act.activation(l2_kraw[j // 4 % 2][0:r, j % 4, :], kv[0:r, 0:HD], ACT.Copy).then_inc(l2_kvc, 1)
                        act.activation(l2_vhi[new][0:r, j, :], kv[0:r, HD:2 * HD], ACT.Copy).then_inc(l2_kvc, 1)
                    at, step = ahead(c, 2, g, n)
                    if at is not None:
                        exp(at, step)
                    if g is not None and c == PV_AT[0]:
                        products(g, 0)
                    if g is not None and c == PV_AT[1] and not (isinstance(g, int) and g == 0):
                        products(g - 1, 1)
                    if n is None:
                        continue
                    for q in range(KG):
                        nb = min(4, KC - 4 * q)
                        if c == KSQ_AT[q]:
                            act.wait_ge(l2_kvc, n * (2 * KC) + 2 * min(KC, 4 * q + 4))
                            need(act, l2_kT, n * KG + (q - 1))
                            for j in range(nb):
                                act.activation(l2_kn[q % 2][:, j, :], l2_kraw[q % 2][:, j, :], ACT.Square,
                                               accum_out=l2_ksq[:, q, j:j + 1]).then_inc(l2_ksqd, 1)
                    for q in range(KG):
                        if c == KT_AT[q]:
                            act.wait_ge(l2_kT, n * KG + (q + 1))
                            a, z = q * BANK, min(q * BANK + BANK, M)
                            ins = act.activation(l2_kThi[new][:, a:z], bank(7, z - a), ACT.Copy, scale=l2_kwc[:, 0:1])
                            if q == KG - 1:
                                ins = act.activation(l2_kThi[new][:, M:MX], bank(7, S, M - a), ACT.Copy)
                            ins.then_inc(l2_kTh, 1)
                    for k in range(TB):
                        if c == QT_AT[k]:
                            act.wait_ge(l2_qT, n * TB + (k + 1))
                            act.activation(l2_qThi[new][:, k, :], bank(7), ACT.Copy).then_inc(l2_qTh, 1)

            l2_turns(act, turn)
            products(TURNS - 1, 1)

        def l2x_vector(v):
            v.wait_ge(x_upd, X_AT[4])
            dve_steps.then(v, v.memset(l2_kraw[1][:, :, :], 0.0))
            v.tensor_copy(l2_ones[:, :], ones[0:REP, :])
            v.wait_ge(l2_pland, 16 * 6)
            hh = HD // 2
            for (own, other), w in ((rope_q, l2_qw), (rope_k, l2_kw)):
                for k in range(TB):
                    v.tensor_tensor(own[:, k, 0:hh], l2_cos[:, k, :], w[:, 0:hh], ALU.mult)
                    v.tensor_tensor(own[:, k, hh:HD], l2_cos[:, k, :], w[:, hh:HD], ALU.mult)
                    v.scalar_tensor_tensor(other[:, k, 0:hh], l2_sin[:, k, :], -1.0, w[:, hh:HD], ALU.mult, ALU.mult)
                    ins = v.tensor_tensor(other[:, k, hh:HD], l2_sin[:, k, :], w[:, 0:hh], ALU.mult)
            dve_steps.then(v, ins)
            norm_vector(v, ln_l2x, x)
            own, other = (r[:, :, :].unsqueeze(2).to_broadcast([P, TB, REP, HD]) for r in rope_q)

            def rest(g, c):
                k, j = STEPS[c]
                r = key_cols(j)[1]
                v.wait_ge(l2_e, g * (2 * NS) + 2 * (c + 1))
                v.tensor_tensor(l2_plo[c % 3][0:r, :], l2_p[c % 3][0:r, :], l2_phi[c % 3][0:r, :].bitcast(F32), ALU.subtract)\
                    .then_inc(l2_lo, 1)

            def inverse(g, k):
                v.wait_ge(l2_sum, g * TB + (k + 1))
                v.reciprocal(l2_rec[k][:, :], bank(7, REP)).then_inc(l2_inv, 1)

            def add_out(g, k, half):
                if half == 0:
                    v.wait_ge(l2_inv, g * TB + (k + 1))
                v.wait_ge(l2_y, (g * TB + k) * 2 + (half + 1))
                row = x[:, bass.ds((g // KH) * TB + k, 1), :].rearrange("p o d -> p (o d)")
                for i in range(REP // 2):
                    h = half * (REP // 2) + i
                    ins = v.scalar_tensor_tensor(row, bank(7, D, i * D), l2_rec[k][:, h:h + 1], row, ALU.mult, ALU.add)
                    if i == 0:
                        dve_steps.then(v, ins)
                ins.then_inc(x_upd, 1)

            def tops(g, k):
                v.wait_ge(l2_far, g * NM + (SEARCH.index((k, REP - 1, KG - 1)) + 1))
                v.tensor_reduce(l2_mx[:, k * REP:(k + 1) * REP], l2_mx4[:, k * REP:(k + 1) * REP, :], AX.X, ALU.max)\
                    .then_inc(l2_top, 1)

            def shifts(g, slot, k):
                v.wait_ge(l2_mT, g * TB + (k + 1))
                v.scalar_tensor_tensor(l2_m[slot][:, k, :].rearrange("h (a n) -> h a n", a=REP),
                                       bank(7, P)[0:REP, :].unsqueeze(1).to_broadcast([REP, REP, P]), -1.0,
                                       ident[0:REP, 0:REP].unsqueeze(2).to_broadcast([REP, REP, P]), ALU.mult, ALU.mult)\
                    .then_inc(l2_md, 1)

            def prepare(c, slot, n):
                if TB <= c < NPROJ:
                    j = c - TB
                    r = key_cols(j)[1]
                    v.wait_ge(l2_kvc, n * (2 * KC) + 2 * (j + 1))
                    v.tensor_tensor(l2_vlo[slot][0:r, j, :], bank(shared_bank(slot, "project", c), 2 * HD)[0:r, HD:2 * HD],
                                    l2_vhi[slot][0:r, j, :].bitcast(F32), ALU.subtract).then_inc(l2_vl, 1)
                for k, h, q in max_pieces(c):
                    i = SEARCH.index((k, h, q))
                    a, z = piece_cols(k, q)
                    v.wait_ge(l2_near, n * NM + (i + 1))
                    u = k * REP + h
                    v.tensor_reduce(l2_mx4[:, u, q:q + 1], bank(shared_bank(slot, "search", i), z - a), AX.X, ALU.max)\
                        .then_inc(l2_far, 1)
                if c == 2:
                    v.wait_ge(l2_qc, (n + 1) * (NQC * TB))
                    v.tensor_scalar(l2_qms[:, :], l2_qsq[:, :], HD * RMS_EPS, None, ALU.add).then_inc(l2_qmsd, 1)
                if c == 3:
                    dve_steps.then(v, v.tensor_tensor(l2_qa[:, :, :, :], l2_q[:, :, :, :], own, ALU.mult))
                if c == 4:
                    v.tensor_tensor(l2_qb[:, :, :, 0:hh], l2_q[:, :, :, hh:HD], other[:, :, :, 0:hh], ALU.mult)
                    dve_steps.then(v, v.tensor_tensor(l2_qb[:, :, :, hh:HD], l2_q[:, :, :, 0:hh], other[:, :, :, hh:HD], ALU.mult))
                if c == 5:
                    dve_steps.then(v, v.tensor_tensor(l2_qb[:, :, :, :], l2_qa[:, :, :, :], l2_qb[:, :, :, :], ALU.add))
                if c == 6:
                    v.wait_ge(l2_qrsd, n + 1)
                    v.tensor_tensor(l2_q[:, :, :, :].rearrange("p k r n -> p (k r) n"),
                                    l2_qb[:, :, :, :].rearrange("p k r n -> p (k r) n"),
                                    l2_qrs[:, :].unsqueeze(2).to_broadcast([P, U, HD]), ALU.mult).then_inc(l2_qnd, 1)
                for k in range(TB):
                    if c == QT_AT[k]:
                        v.wait_ge(l2_qTh, n * TB + (k + 1))
                        v.tensor_tensor(l2_qTlo[slot][:, k, :], bank(7), l2_qThi[slot][:, k, :].bitcast(F32), ALU.subtract)\
                            .then_inc(l2_qTl, 1)
                for q in range(KG):
                    nb = min(4, KC - 4 * q)
                    kn = l2_kn[q % 2]
                    if c == KSQ_AT[q]:
                        v.wait_ge(l2_ksqd, n * KC + min(KC, 4 * q + 4))
                        v.tensor_scalar(l2_kms[:, q, 0:nb], l2_ksq[:, q, 0:nb], 1.0 / HD, RMS_EPS, ALU.mult, ALU.add)\
                            .then_inc(l2_kmsd, 1)
                for q in range(KG):
                    nb = min(4, KC - 4 * q)
                    kn = l2_kn[q % 2]
                    if c == KN_AT[q] and q == KG - 1:
                        v.wait_ge(l2_knd, (n + 1) * KG)
                        kx = kn[:, nb - TB:nb, :]
                        v.tensor_tensor(l2_ra[:, :, :], kx, rope_k[0][:, :, :], ALU.mult)
                        v.tensor_tensor(l2_rb[:, :, 0:hh], kx[:, :, hh:HD], rope_k[1][:, :, 0:hh], ALU.mult)
                        dve_steps.then(v, v.tensor_tensor(l2_rb[:, :, hh:HD], kx[:, :, 0:hh], rope_k[1][:, :, hh:HD], ALU.mult))
                        v.tensor_tensor(kx, l2_ra[:, :, :], l2_rb[:, :, :], ALU.add).then_inc(l2_kxd, 1)
                    if c == KT_AT[q]:
                        v.wait_ge(l2_kTh, n * KG + (q + 1))
                        a, z = q * BANK, min(q * BANK + BANK, M)
                        ins = v.scalar_tensor_tensor(l2_kTlo[slot][:, a:z], bank(7, z - a), l2_kwc[:, 0:1],
                                                     l2_kThi[slot][:, a:z].bitcast(F32), ALU.mult, ALU.subtract)
                        if q == KG - 1:
                            ins = v.tensor_tensor(l2_kTlo[slot][:, M:MX], bank(7, S, M - a), l2_kThi[slot][:, M:MX].bitcast(F32),
                                                  ALU.subtract)
                        ins.then_inc(l2_kTl, 1)

            def turn(g, slot, n):
                for c in range(NS):
                    at, step = ahead(c, 1, g, n)
                    if at is not None:
                        rest(at, step)
                    if n is not None:
                        prepare(c, 1 - slot, n)
                        if c == TOP_AT:
                            tops(n, 0)
                        if c == M_AT:
                            shifts(n, 1 - slot, 0)
                    if g is not None:
                        if c == 0:
                            tops(g, 1)
                        if c == M1_AT:
                            shifts(g, slot, 1)
                        for k, turns_ago in ((0, 0), (1, 1)):
                            if isinstance(g, int) and g < turns_ago:
                                continue
                            if c == SUM_AT[k]:
                                inverse(g - turns_ago, k)
                            for half in range(2):
                                if c == Y_AT[k][half]:
                                    add_out(g - turns_ago, k, half)

            l2_turns(v, turn, dve_steps)
            inverse(TURNS - 1, 1)
            for half in range(2):
                add_out(TURNS - 1, 1, half)

        def l2x_tensor(pe):
            norm_tensor(pe, ln_l2x)

            def scores(g, slot, c):
                k, j = STEPS[c]
                a, r = key_cols(j)
                even = r + r % 2
                if j == 0:
                    pe.wait_ge(l2_md, g * TB + (k + 1))
                if k == 0:
                    pe.wait_ge(l2_kTl, g * KG + (j // 4 + 1))
                last = c - 3 if c >= 3 else NS - 2 + c if c < 2 else NS - 3
                need(pe, l2_e, (g * (2 * NS) + 2 * (last + 1)) if c >= 3 else g * (2 * NS) + 2 * (last - NS + 1))
                dst = bank(c % 3)[0:even, :]
                keys = slice(a, a + even)
                if j == MC + k:
                    pe.matmul(dst, identb[:, :], causal_T[:, :, :].rearrange("p h n -> p (h n)"), start=True, stop=False)
                pe.matmul(dst, l2_ones[:, 0:even], l2_m[slot][:, k, :], start=(j < MC + k), stop=False)
                three(pe, dst, (l2_kThi[slot][:, keys], l2_kTlo[slot][:, keys]),
                      (l2_qThi[slot][:, k, :], l2_qTlo[slot][:, k, :]), False, True).then_inc(l2_s, 1)

            def values(g, slot, c):
                k, j = STEPS[c]
                r = key_cols(j)[1]
                pe.wait_ge(l2_lo, g * NS + (c + 1))
                if j == 0:
                    need(pe, l2_o, g * TB + (k - 1))
                if k == 0:
                    pe.wait_ge(l2_vl, g * KC + (j + 1))
                three(pe, bank(3 + k), (l2_vhi[slot][0:r, j, :], l2_vlo[slot][0:r, j, :]),
                      (l2_phi[c % 3][0:r, :], l2_plo[c % 3][0:r, :]), j == 0, j == MC + k).then_inc(l2_pv, 1)

            def sums(g, k):
                pe.wait_ge(l2_accd, g * NS + (TILE_END[k] + 1))
                if k == 1:
                    pe.wait_ge(x_upd, g * (2 * TB) + (X_AT[4] + 2))
                for h in range(REP):
                    mm = pe.matmul(bank(7, 1, h), l2_acc[k][:, h * P:(h + 1) * P], ones[:, 0:1], start=True, stop=True)
                mm.then_inc(l2_sum, 1)

            def output(g, k, half):
                if half == 0:
                    pe.wait_ge(l2_o, g * TB + (k + 1))
                    pe.wait_ge(l2_inv, g * TB + (k + 1))
                else:
                    pe.wait_ge(x_upd, (g * TB + k) * 2 + (X_AT[4] + 1))
                for i in range(REP // 2):
                    h = half * (REP // 2) + i
                    mm = pe.matmul(bank(7, D, i * D), l2_oT[k][:, h * P:(h + 1) * P],
                                   l2_wo[:, bass.ds((g % KH) * REP + h, 1), :].rearrange("p o d -> p (o d)"),
                                   start=True, stop=True)
                mm.then_inc(l2_y, 1)

            def maxima(g, k):
                pe.wait_ge(l2_top, g * TB + (k + 1))
                pe.transpose(bank(7, P)[0:REP, :], l2_mx[:, k * REP:(k + 1) * REP], ident[:, :]).then_inc(l2_mT, 1)

            def bank_free(kind, i, n):
                at = SHARED.index((kind, i)) - 2
                if at < 0:
                    need(pe, l2_far, n * NM)
                elif SHARED[at][0] == "search":
                    pe.wait_ge(l2_far, n * NM + (SHARED[at][1] + 1))
                elif SHARED[at][1] < TB:
                    pe.wait_ge(l2_qc, n * (NQC * TB) + NQC * (SHARED[at][1] + 1))
                else:
                    pe.wait_ge(l2_vl, n * KC + (SHARED[at][1] - TB + 1))

            def search(slot, n, k, h, q):
                i = SEARCH.index((k, h, q))
                a, z = piece_cols(k, q)
                pe.wait_ge(l2_kTh, n * KG + (q + 1))
                bank_free("search", i, n)
                at = shared_bank(slot, "search", i)
                masked = q == KG - 1
                if masked:
                    pe.matmul(bank(at, z - a), identb[:, :], causal[:, BANK - (z - a):], start=True, stop=False)
                pe.matmul(bank(at, z - a), l2_qThi[slot][:, k, h * P:(h + 1) * P], l2_kThi[slot][:, a:z],
                          start=not masked, stop=True).then_inc(l2_near, 1)

            def project(c, slot, n):
                if c == 0:
                    pe.wait_ge(l2_wland, n * 16 + 16)
                    pe.wait_ge(l2_cland, (n // KH) * 32 + 32)
                if c < NPROJ:
                    bank_free("project", c, n)
                    dst = bank(shared_bank(slot, "project", c))
                    j = c - TB
                    for d in range(DC):
                        if c < TB:
                            lhs, cols, into = l2_xb[:, d, c * P:(c + 1) * P], slice(4 * HD, None), dst
                        elif j < MC:
                            lhs, cols = l2_ctx[:, d, j * P:j * P + chunk_rows(j)], slice(0, 2 * HD)
                            into = dst[0:chunk_rows(j), 0:2 * HD]
                        else:
                            lhs, cols, into = l2_xb[:, d, (j - MC) * P:(j - MC + 1) * P], slice(2 * HD, 4 * HD), dst[:, 0:2 * HD]
                        mm = pe.matmul(into, lhs, l2_w[:, d, cols], start=(d == 0), stop=(d == DC - 1))
                    mm.then_inc(l2_proj, 1)

            def prepare(c, slot, n):
                for k in range(TB):
                    if c == QT_AT[k]:
                        pe.wait_ge(l2_qnd, n + 1)
                        if k == 0:
                            need(pe, l2_md, n * TB)
                        else:
                            pe.wait_ge(l2_qTl, n * TB + k)
                        for h in range(REP):
                            mm = pe.transpose(bank(7, P, h * P), l2_q[:, k, h, :], ident[:, :])
                        mm.then_inc(l2_qT, 1)
                for q in range(KG):
                    if c == KT_AT[q]:
                        pe.wait_ge(l2_knd, n * KG + (q + 1))
                        if q == KG - 1:
                            pe.wait_ge(l2_kxd, n + 1)
                        if q == 0:
                            pe.wait_ge(l2_qTl, (n + 1) * TB)
                        else:
                            pe.wait_ge(l2_kTl, n * KG + q)
                        for j in range(4 * q, min(4 * q + 4, KC)):
                            a, r = key_cols(j)
                            mm = pe.transpose(bank(7, r, a - q * BANK), l2_kn[q % 2][0:r, j % 4, :], ident[0:r, 0:r])
                        mm.then_inc(l2_kT, 1)

            def turn(g, slot, n):
                for c in range(NS):
                    pieces = max_pieces(c) if n is not None else []
                    if n is not None:
                        project(c, 1 - slot, n)
                    for piece in pieces[0:1]:
                        search(1 - slot, n, *piece)
                    if g is not None:
                        values(g, slot, c)
                    for piece in pieces[2:3]:
                        search(1 - slot, n, *pieces[1])
                    at, step = ahead(c, 3, g, n)
                    if at is not None:
                        scores(at, slot if c + 3 < NS else 1 - slot, step)
                    for piece in pieces[-1:] if len(pieces) > 1 else []:
                        search(1 - slot, n, *piece)
                    if g is not None:
                        later = not isinstance(g, int) or g >= 1
                        if c == SUM_AT[1] and later:
                            sums(g - 1, 1)
                        for half in range(2):
                            if c == Y_AT[1][half] and later:
                                output(g - 1, 1, half)
                        if c == M1_AT:
                            if later:
                                pe.wait_ge(x_upd, g * (2 * TB) + X_AT[4])
                            maxima(g, 1)
                        if c == SUM_AT[0]:
                            if n is not None:
                                pe.wait_ge(l2_kTl, (n + 1) * KG)
                            sums(g, 0)
                    if c == M_AT and n is not None:
                        if g is not None:
                            pe.wait_ge(l2_inv, g * TB + 1)
                        else:
                            pe.wait_ge(l2_kTl, (n + 1) * KG)
                        maxima(n, 0)
                    if g is not None:
                        for half in range(2):
                            if c == Y_AT[0][half]:
                                if n is not None and half == 0:
                                    pe.wait_ge(l2_md, n * TB + 1)
                                output(g, 0, half)
                    if n is not None:
                        prepare(c, 1 - slot, n)

            l2_turns(pe, turn)
            sums(TURNS - 1, 1)
            for half in range(2):
                output(TURNS - 1, 1, half)

        L2_DVE_STEPS = 2 * TB + 3 + 1
        moe_prepare("L2", 2, 5)

        ln_l3x = norm_plan(True, False)
        l3 = ExitStack()
        W3 = 4 * D3
        N3 = MC + TB
        NP = NG // 2
        C3 = 2 * MC
        PT = 4
        EARLY = [0, 1, 2, 3], [4, 6, 8, 10], [5, 7, 9, 11]
        BESIDE = [0, 4, 9, 13], [7, 12, 17, 22], [8, 13, 18, 23]
        OUT_AT = MC + 3
        assert PT * (NP - 1) == MC - 1 and N3 - PT * (NP - 1) <= PT
        ring = [0, 1, 2, 3] * (C3 % 3) + [0, 1, 2] * ((C3 - 4 * (C3 % 3)) // 3)
        assert len(ring) == C3
        l3_ct = [sb(f"l3_ct{m}", [P, DC, P], F32, l3) for m in range(PT)]
        l3_wkv = sb("l3_wkv", [P, DC, 2 * D], F32, l3)
        l3_wq = sb("l3_wq", [P, DC, D], F32, l3)
        l3_xb = sb("l3_xb", [P, DC, S], F32, l3)
        l3_raw = [sb(f"l3_raw{n}", [P, D], F32, l3) for n in range(PT)]
        l3_sq = sb("l3_sq", [P, D], F32, l3)
        l3_n = sb("l3_n", [P, D], F32, l3)
        l3_ms = [sb(f"l3_ms{n}", [P, H3], F32, l3) for n in range(PT)]
        l3_rs = [sb(f"l3_rs{n}", [P, H3], F32, l3) for n in range(PT)]
        l3_pairs = [sb(f"l3_pairs{n}", [P, H3, 4, D3], F16, l3) for n in range(2)]
        l3_v = [sb(f"l3_v{s}", [P, MC, H3, D3], F32, l3) for s in range(2)]
        l3_kT = [sb(f"l3_kT{s}", [P, NG, MC * P], F16, l3) for s in range(2)]
        l3_qT = [sb(f"l3_qT{s}", [P, NG, HG, S], F16, l3) for s in range(2)]
        l3_vs = [sb(f"l3_vs{n}", [P, MC, HG, 32], F32, l3) for n in range(2)]
        l3_p = [sb(f"l3_p{n}", [P, HG * S], F32, l3) for n in range(4)]
        l3_o = [sb(f"l3_o{n}", [P, S], F32, l3) for n in range(2)]
        l3_rec = sb("l3_rec", [P, TB, HG], F32, l3)
        l3_y = sb("l3_y", [P, TB, HG, D3], F32, l3)
        l3_none, l3_none2 = sb("l3_none", [P, 1], F32, l3), sb("l3_none2", [P, 1], F32, l3)
        l3.close()
        l3_cland = sems("l3_cland", PT)
        (l3_xland, l3_wland, l3_init, l3_kv, l3_kvd, l3_msd, l3_rsd, l3_pd, l3_T, l3_Td, l3_vsd, l3_s, l3_e, l3_pv,
         l3_od, l3_oT) = (sem(n) for n in (
             "l3_xland l3_wland l3_init l3_kv l3_kvd l3_msd l3_rsd l3_pd l3_T l3_Td l3_vsd l3_s l3_e l3_pv "
             "l3_od l3_oT").split())

        def l3_tiles(last):
            return [(m, m < 1 if last else True) for m in range(N3 - PT * (NP - 1) if last else PT)]

        def l3_batches(engine, pair, norm, per=None):
            for b in (None, *range(B)):
                new = 0 if b is None else b + 1 if b + 1 < B else None
                with engine.Fori(0, NP - 1) as i:
                    if per:
                        dve_steps.enter(i, (b is not None) * per[0] + (new is not None) * per[1])
                    pair(b, i, new, False)
                if per:
                    dve_steps.leave(NP - 1)
                if b is None:
                    norm()
                pair(b, NP - 1, new, True)

        def l3x_sync(sp):
            sp.wait_ge(x_upd, X_AT[6])
            sp.dma_start(l3_wkv[:, :, :], t["L3_kv"]).then_inc(l3_wland, 16)
            sp.dma_start(l3_wq[:, :, :], t["L3_q"]).then_inc(l3_wland, 16)

            def tile(b, j, m):
                sp.dma_start(l3_ct[m][:, :, :], t["ctx_tiles"][b, bass.ds(j, 1)].rearrange("o p c m -> p (o c) m"))\
                    .then_inc(l3_cland[m], 16)

            for b in range(B):
                if b:
                    sp.wait_ge(l3_kv, b * N3)
                for m in range(PT):
                    tile(b, m, m)
                with sp.Fori(0, NP - 2) as i:
                    for m in range(PT):
                        sp.wait_ge(l3_kv, i * PT + (b * N3 + m + 1))
                        tile(b, i * PT + (PT + m), m)
                sp.wait_ge(l3_kv, b * N3 + (MC - PT))
                tile(b, MC - 1, 0)
                if b == 0:
                    sp.wait_ge(xT_cp, ln_l3x["cp_end"])
                sp.dma_start(l3_xb[:, :, :], xT[:, :, b * S:(b + 1) * S]).then_inc(l3_xland, 16)

        def l3x_pool(g):
            g.wait_ge(x_upd, X_AT[6])
            def stage(b, n, parity, before):
                need(g, l3_vsd, n + b * NG)
                g.wait_ge(l3_pv, before)
                g.tensor_tensor(l3_none2[:, :], half_power[:, 0:1], half_power[:, 0:1], ALU.mult)
                g.tensor_copy(l3_vs[parity][:, :, :, 0:D3], l3_v[b % 2][:, :, bass.ds(n * HG, HG), :]).then_inc(l3_vsd, 1)

            def power(new, i, m):
                g.wait_ge(l3_msd, i * PT + (new * N3 + m + 1))
                g.tensor_tensor(l3_rs[m][:, :], l3_ms[m][:, :], half_power[:, 0:H3], ALU.pow).then_inc(l3_rsd, 1)

            def pair(b, i, new, last):
                places = [m for m, _ in l3_tiles(last)] if new is not None else []
                if b is not None:
                    stage(b, i * 2 + 1, 1, i * C3 + b * (NP * C3))
                for m in places[:2]:
                    power(new, i, m)
                if b is not None and not last:
                    stage(b, i * 2 + 2, 0, i * C3 + (b * (NP * C3) + MC))
                for m in places[2:]:
                    power(new, i, m)
                if last and new is not None:
                    g.wait_ge(l3_kvd, 2 * (new * N3 + MC))
                    g.wait_ge(l3_init, 6)
                    if new:
                        stage(new, 0, 0, new * (NP * C3) - MC)
                    else:
                        g.tensor_copy(l3_vs[0][:, :, :, 0:D3], l3_v[0][:, :, 0:HG, :]).then_inc(l3_vsd, 1)

            l3_batches(g, pair, lambda: norm_pool(g, ln_l3x))

        def l3x_scalar(act):
            norm_scalar(act, ln_l3x)
            act.preload_act_table(ACT.Exp)

            def pair(b, i, new, last):
                if b is None:
                    return
                for c in range(C3):
                    act.wait_ge(l3_s, i * C3 + (b * (NP * C3) + c + 1))
                    act.activation(l3_p[ring[c]][:, :], psum[:, (c % 2) * 2 * BANK:(c % 2 + 1) * 2 * BANK], ACT.Exp,
                                   scale=float(D3) ** -0.5).then_inc(l3_e, 1)

            for b in range(B):
                with act.Fori(0, NP) as i:
                    pair(b, i, None, False)

        def l3x_vector(v):
            v.wait_ge(x_upd, X_AT[6])
            for n in range(2):
                dve_steps.then(v, v.memset(l3_vs[n][:, :, :, :], 0.0))
                v.memset(l3_vs[n][:, 0:MC - 1, :, D3:D3 + 1], 1.0).then_inc(l3_init, 1)
                for a in range(0, ML, 64):
                    z = min(a + 64, ML)
                    v.memset(l3_vs[n][a:z, MC - 1, :, D3:D3 + 1], 1.0).then_inc(l3_init, 1)
                dve_steps.then(v, v.memset(l3_qT[n][:, :, :, :], 0.0))

            def heads(ap):
                return ap.rearrange("p (h d) -> p h d", d=D3)

            def squares(new, i, m, context, last):
                k = i * PT + (new * N3 + m)
                raw, at = l3_raw[m][:, :], new % 2
                v.wait_ge(l3_kv, k + 1)
                if context:
                    v.tensor_copy(raw, bank(6, D)).then_inc(l3_kvd, 1)
                    dst = l3_v[at][:, MC - 1:MC, :, :] if last else l3_v[at][:, bass.ds(i * PT + m, 1), :, :]
                    v.tensor_copy(dst.rearrange("p o h d -> p (o h) d"), heads(bank(6, D, D))).then_inc(l3_kvd, 1)
                else:
                    v.tensor_copy(raw, bank(6, D)).then_inc(l3_kvd, 2)
                v.wait_ge(l3_kvd, k * 2 + 2)
                dve_steps.then(v, v.tensor_tensor(l3_sq[:, :], raw, raw, ALU.mult))
                dve_steps.then(v, v.tensor_reduce(l3_ms[m][:, :], heads(l3_sq[:, :]), AX.X, ALU.add))
                v.tensor_scalar(l3_ms[m][:, :], l3_ms[m][:, :], 1.0 / D3, RMS_EPS, ALU.mult, ALU.add)\
                    .then_inc(l3_msd, 1)

            def pairs(new, i, m, context):
                v.wait_ge(l3_rsd, i * PT + (new * N3 + m + 1))
                norm = heads(l3_n[:, :])
                dve_steps.then(v, v.tensor_tensor(norm, heads(l3_raw[m][:, :]),
                                                  l3_rs[m][:, :].unsqueeze(2).to_broadcast([P, H3, D3]), ALU.mult))
                both = norm.unsqueeze(2).to_broadcast([P, H3, 2, D3])
                dst = l3_pairs[m % 2]
                hi, lo = (dst[:, :, 0::2, :], dst[:, :, 1::2, :]) if context else (dst[:, :, 0:2, :], dst[:, :, 2:4, :])
                dve_steps.then(v, v.tensor_copy(hi, both))
                v.tensor_tensor(lo, both, hi, ALU.subtract).then_inc(l3_pd, 1)

            def turned(new, i, m, context, last):
                v.wait_ge(l3_T, i * PT + (new * N3 + m + 1))
                v.memset(l3_none[:, :], 0.0)
                src = bank(7).bitcast(F16).rearrange("p (g m) -> p g m", g=NG)
                if context:
                    j = MC - 1 if last else i * PT + m
                    ins = v.tensor_copy(l3_kT[new % 2][:, :, bass.ds(j * P, P)], src)
                else:
                    k = m - 1
                    for n in range(HG):
                        part = slice(n * W3, (n + 1) * W3)
                        ins = v.tensor_copy(l3_qT[new % 2][part, :, n, k * P:(k + 1) * P], src[part, :, :])
                ins.then_inc(l3_Td, 1)

            def add_out(b, i, a):
                v.wait_ge(l3_pv, i * C3 + (b * (NP * C3) + (a + 1) * MC))
                v.tensor_copy(l3_o[a][:, :], bank(4 + a, S)).then_inc(l3_od, 1)
                v.wait_ge(l3_oT, i * 2 + (b * NG + a + 1))
                got = bank(7, TB * P).rearrange("p (k h d) -> p k h d", k=TB, h=HG)
                dve_steps.then(v, v.reciprocal(l3_rec[:, :, :], got[:, :, :, D3]))
                dve_steps.then(v, v.tensor_tensor(l3_y[:, :, :, :], got[:, :, :, 0:D3],
                                                  l3_rec[:, :, :].unsqueeze(3).to_broadcast([P, TB, HG, D3]), ALU.mult))
                row = x[:, b * TB:(b + 1) * TB, bass.ds((i * 2 + a) * (HG * D3), HG * D3)]
                v.tensor_tensor(row, row, l3_y[:, :, :, :].rearrange("p k h d -> p k (h d)"), ALU.add).then_inc(x_upd, 1)

            def pair(b, i, new, last):
                proj_at, pair_at, turn_at = EARLY if b is None else BESIDE
                for c in range(C3):
                    if b is not None and c == OUT_AT:
                        add_out(b, i, 0)
                    for m, context in l3_tiles(last) if new is not None else []:
                        if c == proj_at[m]:
                            squares(new, i, m, context, last)
                        if c == pair_at[m]:
                            pairs(new, i, m, context)
                        if c == turn_at[m]:
                            turned(new, i, m, context, last)
                if b is not None:
                    add_out(b, i, 1)

            l3_batches(v, pair, lambda: norm_vector(v, ln_l3x, x), (2 * 2, PT * 4))

        def l3x_tensor(pe):
            pe.wait_ge(l3_wland, 32)

            def project(new, i, m, context, last):
                k = i * PT + (new * N3 + m)
                if context:
                    loads = NP if m == 0 else NP - 1
                    pe.wait_ge(l3_cland[m], i * 16 + (new * loads + 1) * 16)
                else:
                    pe.wait_ge(l3_xland, (new + 1) * 16)
                need(pe, l3_kvd, k * 2)
                for c in range(DC):
                    lhs = l3_ct[m][:, c, :] if context else l3_xb[:, c, (m - 1) * P:m * P]
                    mm = pe.matmul(bank(6, 2 * D if context else D), lhs, (l3_wkv if context else l3_wq)[:, c, :],
                                   start=(c == 0), stop=(c == DC - 1))
                mm.then_inc(l3_kv, 1)

            def turn(b, new, i, m):
                k = i * PT + (new * N3 + m)
                pe.wait_ge(l3_pd, k + 1)
                if b is not None and m in (0, 2):
                    pe.wait_ge(x_upd, i * 2 + (b * NG + m // 2 + X_AT[6]))
                else:
                    need(pe, l3_Td, k)
                src = l3_pairs[m % 2][:, :, :, :].rearrange("p h a d -> p (h a d)")
                for n in range(NG):
                    mm = pe.transpose(bank(7).bitcast(F16)[:, n * P:(n + 1) * P], src[:, n * P:(n + 1) * P], identh[:, :])
                mm.then_inc(l3_T, 1)

            def scores(b, i, c):
                n, j = i * 2 + c // MC, c % MC
                pe.wait_ge(l3_Td, (b + 1) * N3)
                if c >= 2 or b > 0 or not isinstance(i, int):
                    pe.wait_ge(l3_e, i * C3 + (b * (NP * C3) + c - 1))
                for a in range(2):
                    mm = pe.matmul(bank(c % 2 * 2 + a),
                                   l3_kT[b % 2][:, bass.ds(n, 1), j * P:(j + 1) * P].rearrange("p o m -> p (o m)"),
                                   l3_qT[b % 2][:, bass.ds(n, 1), 2 * a:2 * a + 2, :].rearrange("p o h s -> p (o h s)"),
                                   start=True, stop=True)
                mm.then_inc(l3_s, 1)

            def values(b, i, c):
                a, j = c // MC, c % MC
                if j == 0:
                    pe.wait_ge(l3_vsd, i * 2 + (b * NG + a + 1))
                pe.wait_ge(l3_e, i * C3 + (b * (NP * C3) + c + 1))
                for h in range(HG):
                    mm = pe.matmul(bank(4 + a, S)[h * 32:(h + 1) * 32, :], l3_vs[a][:, j, h, :],
                                   l3_p[ring[c]][:, h * S:(h + 1) * S], start=(j == 0), stop=(j == MC - 1))
                mm.then_inc(l3_pv, 1)

            def out(b, i, a, new, last):
                pe.wait_ge(l3_od, i * 2 + (b * NG + a + 1))
                if new is not None:
                    pe.wait_ge(l3_Td, i * PT + (new * N3 + min(2 * a + 2, len(l3_tiles(last)))))
                elif a == 1:
                    pe.wait_ge(x_upd, i * 2 + (b * NG + a + X_AT[6]))
                else:
                    pe.wait_ge(x_upd, i * 2 + (b * NG + X_AT[6]))
                for k in range(TB):
                    mm = pe.transpose(bank(7, P, k * P), l3_o[a][:, k * P:(k + 1) * P], ident[:, :])
                mm.then_inc(l3_oT, 1)

            def pair(b, i, new, last):
                proj_at, pair_at, turn_at = EARLY if b is None else BESIDE
                for c in range(C3):
                    if c + 2 < C3:
                        if b is not None:
                            scores(b, i, c + 2)
                    elif not last:
                        if b is not None:
                            scores(b, i + 1, c + 2 - C3)
                    if b is not None:
                        values(b, i, c)
                        if c == OUT_AT:
                            out(b, i, 0, new, last)
                    for m, context in l3_tiles(last) if new is not None else []:
                        if c == proj_at[m]:
                            project(new, i, m, context, last)
                        if c == turn_at[m]:
                            turn(b, new, i, m)
                    if last and new is not None and c + 2 >= C3:
                        scores(new, 0, c + 2 - C3)
                if b is not None:
                    out(b, i, 1, new, last)

            l3_batches(pe, pair, lambda: norm_tensor(pe, ln_l3x))

        ln_l3f = norm_plan(False, False)
        MAGIC = 1.5 * 2 ** 23
        FC = FF3 // P
        f3 = ExitStack()
        f3_w = [sb(f"f3_w{n}", [P, DC * FF3], F32, f3) for n in range(3)]
        f3_wq = [sb(f"f3_wq{n}", [P, DC * FF3], BF16, f3) for n in range(3)]
        f3_wsum = sb("f3_wsum", [P, 3], F32, f3)
        f3_ws, f3_wr = sb("f3_ws", [P, 3], F32, f3), sb("f3_wr", [P, 3], F32, f3)
        f3_xmax, f3_xs, f3_xr = (sb(f"f3_x{n}", [P, NT], F32, f3) for n in ("max", "s", "r"))
        f3_sg, f3_su = sb("f3_sg", [P, NT], F32, f3), sb("f3_su", [P, NT], F32, f3)
        f3_xq = sb("f3_xq", [P, NT, D], F32, f3)
        f3_xb = sb("f3_xb", [P, NT, D], BF16, f3)
        f3_xT = sb("f3_xT", [P, DC, NTOK], BF16, f3)
        f3_g = [sb(f"f3_g{n}", [P, FF3], F32, f3) for n in range(2)]
        f3_h = [sb(f"f3_h{n}", [P, FF3], F32, f3) for n in range(2)]
        f3_hb = [sb(f"f3_hb{n}", [P, FF3], BF16, f3) for n in range(2)]
        f3_hT = [sb(f"f3_hT{n}", [P, FC, P], BF16, f3) for n in range(2)]
        f3_hmax, f3_hs, f3_hr = (sb(f"f3_h{n}", [P, TB], F32, f3) for n in ("max", "s", "r"))
        f3_hd = sb("f3_hd", [P, TB], F32, f3)
        f3_sgt, f3_sut = sb("f3_sgt", [P, TB], F32, f3), sb("f3_sut", [P, TB], F32, f3)
        f3.close()
        f3_wland, f3_hread = sems("f3_wland", 3), sem("f3_hread")
        (f3_wsumd, f3_wtot, f3_wqd, f3_xbd, f3_xTp, f3_xTd, f3_scd, f3_gu, f3_gd, f3_hq, f3_hbd, f3_hTp, f3_hTd,
         f3_dn) = (sem(n) for n in (
             "f3_wsumd f3_wtot f3_wqd f3_xbd f3_xTp f3_xTd f3_scd f3_gu f3_gd f3_hq f3_hbd f3_hTp f3_hTd "
             "f3_dn").split())

        def l3f_sync(sp):
            sp.wait_ge(x_upd, X_AT[7])
            for n, name in enumerate(("L3_gate", "L3_up", "L3_down")):
                sp.dma_start(f3_w[n][:, :], t[name].rearrange("p c n -> p (c n)")).then_inc(f3_wland[n], 16)
            with sp.Fori(0, B) as b:
                sp.wait_ge(x_upd, b * TB + (X_AT[7] + TB))
                sp.dma_start(out[bass.ds(b, 1)].rearrange("o (k p) d -> p (o k) d", p=P), x[:, bass.ds(b * TB, TB), :])\
                    .then_inc(out_done, 16)
            sp.wait_ge(out_done, 16 * B)

        def l3f_pool(g):
            pass

        def l3f_vector(v):
            v.wait_ge(x_upd, X_AT[7])
            for n in range(3):
                v.wait_ge(f3_wland[n], 16)
                v.tensor_reduce(f3_wsum[:, n:n + 1], f3_w[n][:, :], AX.X, ALU.add, apply_absolute_value=True)\
                    .then_inc(f3_wsumd, 1)
            norm_vector(v, ln_l3f, x)
            v.wait_ge(xn_done, NT * (ln_l3f["k"] + 1))
            dve_steps.then(v, v.tensor_reduce(f3_xmax[:, :], xn[:, :, :], AX.X, ALU.max, apply_absolute_value=True))
            dve_steps.then(v, v.tensor_scalar(f3_xs[:, :], f3_xmax[:, :], 1.0 / 127, 1e-5, ALU.mult, ALU.add))
            dve_steps.then(v, v.reciprocal(f3_xr[:, :], f3_xs[:, :]))
            for n in range(NT):
                ins = v.tensor_scalar(f3_xq[:, n, :], xn[:, n, :], f3_xr[:, n:n + 1], MAGIC, ALU.mult, ALU.add)
            dve_steps.then(v, ins)
            dve_steps.then(v, v.tensor_scalar(f3_xq[:, :, :], f3_xq[:, :, :], MAGIC - 128, MAGIC + 127, ALU.max, ALU.min))
            v.tensor_scalar(f3_xb[:, :, :], f3_xq[:, :, :], MAGIC, None, ALU.subtract).then_inc(f3_xbd, 1)
            v.wait_ge(f3_wtot, 1)
            dve_steps.then(v, v.tensor_scalar(f3_ws[:, :], bank(6, 3), 1.0 / (D * FF3), 1e-5, ALU.mult, ALU.add))
            dve_steps.then(v, v.reciprocal(f3_wr[:, :], f3_ws[:, :]))
            def ternary(n):
                dve_steps.then(v, v.tensor_scalar(f3_w[n][:, :], f3_w[n][:, :], f3_wr[:, n:n + 1], MAGIC, ALU.mult, ALU.add))
                dve_steps.then(v, v.tensor_scalar(f3_w[n][:, :], f3_w[n][:, :], MAGIC - 1, MAGIC + 1, ALU.max, ALU.min))
                v.tensor_scalar(f3_wq[n][:, :], f3_w[n][:, :], MAGIC, None, ALU.subtract).then_inc(f3_wqd, 1)

            ternary(0)
            ternary(1)
            v.tensor_scalar(f3_sg[:, :], f3_xs[:, :], f3_ws[:, 0:1], None, ALU.mult)
            dve_steps.then(v, v.tensor_scalar(f3_su[:, :], f3_xs[:, :], f3_ws[:, 1:2], None, ALU.mult))
            for hf in range(2):
                for c in range(DC):
                    if c == 0:
                        v.wait_ge(f3_xTp, hf + 1)
                    v.tensor_copy(f3_xT[:, c, hf * HALF:(hf + 1) * HALF], bank(2 * c + hf).bitcast(BF16)[:, 0:HALF])\
                        .then_inc(f3_xTd, 1)
            ternary(2)
            with v.Fori(0, B) as b:
                dve_steps.enter(b, TB * 4)
                for k in range(TB):
                    n = b * TB + k
                    v.tensor_copy(f3_sgt[:, k:k + 1], f3_sg[:, bass.ds(n, 1)])
                    v.tensor_copy(f3_sut[:, k:k + 1], f3_su[:, bass.ds(n, 1)]).then_inc(f3_scd, 1)
                for k in range(TB):
                    v.wait_ge(f3_scd, (b + 1) * TB)
                    v.wait_ge(f3_gd, b * TB + (k + 1))
                    v.scalar_tensor_tensor(f3_h[k][:, :], psum[:, 2 * BANK:4 * BANK], f3_sut[:, k:k + 1], f3_g[k][:, :],
                                           ALU.mult, ALU.mult).then_inc(f3_hread, 1)
                    v.wait_ge(f3_hread, b * TB + (k + 1))
                    dve_steps.then(v, v.tensor_reduce(f3_hmax[:, k:k + 1], f3_h[k][:, :], AX.X, ALU.max, apply_absolute_value=True))
                    dve_steps.then(v, v.tensor_scalar(f3_hs[:, k:k + 1], f3_hmax[:, k:k + 1], 1.0 / 127, 1e-5, ALU.mult, ALU.add))
                    v.tensor_scalar(f3_hd[:, k:k + 1], f3_hs[:, k:k + 1], f3_ws[:, 2:3], None, ALU.mult)
                    dve_steps.then(v, v.reciprocal(f3_hr[:, k:k + 1], f3_hs[:, k:k + 1]))
                    dve_steps.then(v, v.tensor_scalar(f3_h[k][:, :], f3_h[k][:, :], f3_hr[:, k:k + 1], MAGIC, ALU.mult, ALU.add))
                    v.tensor_scalar(f3_h[k][:, :], f3_h[k][:, :], MAGIC - 128, MAGIC + 127, ALU.max, ALU.min).then_inc(f3_hq, 1)
                for k in range(TB):
                    v.wait_ge(f3_dn, b * TB + (k + 1))
                    row = x[:, bass.ds(b * TB + k, 1), :].rearrange("p o d -> p (o d)")
                    v.scalar_tensor_tensor(row, bank(6 + k, D), f3_hd[:, k:k + 1], row, ALU.mult, ALU.add).then_inc(x_upd, 1)
            dve_steps.leave(B)

        def l3f_scalar(act):
            act.preload_act_table(ACT.Silu)
            with act.Fori(0, B) as b:
                for k in range(TB):
                    act.wait_ge(f3_scd, (b + 1) * TB)
                    act.wait_ge(f3_gu, b * TB + (k + 1))
                    act.activation(f3_g[k][:, :], psum[:, 0:2 * BANK], ACT.Silu, scale=f3_sgt[:, k:k + 1]).then_inc(f3_gd, 1)
                for k in range(TB):
                    act.wait_ge(f3_hq, b * TB + (k + 1))
                    act.activation(f3_hb[k][:, :], f3_h[k][:, :], ACT.Copy, bias=-MAGIC).then_inc(f3_hbd, 1)
                    act.wait_ge(f3_hTp, b * TB + (k + 1))
                    act.activation(f3_hT[k][:, :, :].rearrange("p c n -> p (c n)"), bank(4 + k).bitcast(BF16), ACT.Copy)\
                        .then_inc(f3_hTd, 1)

        def l3f_tensor(pe):
            pe.wait_ge(f3_wsumd, 3)
            pe.wait_ge(x_upd, X_AT[7])
            pe.matmul(bank(6, 3), ones[:, :], f3_wsum[:, :], start=True, stop=True).then_inc(f3_wtot, 1)
            pe.wait_ge(f3_xbd, 1)
            for n in range(NT):
                for c in range(DC):
                    mm = pe.transpose(bank(2 * c + n // 4).bitcast(BF16)[:, n % 4 * P:(n % 4 + 1) * P],
                                      f3_xb[:, n, c * P:(c + 1) * P], identb[:, :])
                if n % 4 == 3:
                    mm.then_inc(f3_xTp, 1)
            pe.wait_ge(f3_xTd, 2 * DC)
            pe.wait_ge(f3_wqd, 2)
            gate, up = (f3_wq[n][:, :].rearrange("p (c f) -> p c f", c=DC) for n in range(2))
            down = f3_wq[2][:, :].rearrange("p (c d) -> p c d", c=FC)
            with pe.Fori(0, B) as b:
                for k in range(TB):
                    pe.wait_ge(f3_hread, b * TB + k)
                    for w, at in ((gate, 0), (up, 2)):
                        for a in range(2):
                            for c in range(DC):
                                mm = pe.matmul(bank(at + a), f3_xT[:, c, bass.ds(b * S + k * P, P)],
                                               w[:, c, a * BANK:(a + 1) * BANK], start=(c == 0), stop=(c == DC - 1))
                    mm.then_inc(f3_gu, 1)
                for k in range(TB):
                    pe.wait_ge(f3_hbd, b * TB + (k + 1))
                    for c in range(FC):
                        mm = pe.transpose(bank(4 + k).bitcast(BF16)[:, c * P:(c + 1) * P], f3_hb[k][:, c * P:(c + 1) * P],
                                          identb[:, :])
                    mm.then_inc(f3_hTp, 1)
                    pe.wait_ge(f3_hTd, b * TB + (k + 1))
                    pe.wait_ge(f3_wqd, 3)
                    for c in range(FC):
                        mm = pe.matmul(bank(6 + k, D), f3_hT[k][:, c, :], down[:, c, :], start=(c == 0), stop=(c == FC - 1))
                    mm.then_inc(f3_dn, 1)

        block = stack.enter_context(nc.Block())

        @block.sync
        def _(sp):
            sp.dma_start(x[:, :, :], t["x"].rearrange("b (k p) d -> p (b k) d", p=P)).then_inc(x_land, 16)
            l0x_sync(sp)
            moe_sync(sp, "L0")
            moe_sync(sp, "L1")
            l2x_sync(sp)
            moe_sync(sp, "L2")
            l3x_sync(sp)
            l3f_sync(sp)

        @block.gpsimd
        def _(g):
            constants_pool(g)
            norm_pool(g, ln_l0x)
            norm_pool(g, moe_plan["L0"]["ln"])
            moe_pool(g, "L0")
            norm_pool(g, ln_l1z)
            norm_pool(g, ln_l1y)
            norm_pool(g, moe_plan["L1"]["ln"])
            moe_pool(g, "L1")
            norm_pool(g, ln_l2x)
            l2x_pool(g)
            norm_pool(g, moe_plan["L2"]["ln"])
            moe_pool(g, "L2")
            l3x_pool(g)
            norm_pool(g, ln_l3f)
            l3f_pool(g)

        @block.scalar
        def _(act):
            parameters_scalar(act)
            norm_scalar(act, ln_l0x)
            l0x_scalar(act)
            moe_scalar(act, "L0")
            l1x_scalar(act)
            moe_scalar(act, "L1")
            l2x_scalar(act)
            moe_scalar(act, "L2")
            l3x_scalar(act)
            l3f_scalar(act)

        @block.vector
        def _(v):
            v.wait_ge(x_land, 16)
            norm_vector(v, ln_l0x, x)
            l0x_vector(v)
            moe_vector(v, "L0")
            l1x_vector(v)
            moe_vector(v, "L1")
            l2x_vector(v)
            moe_vector(v, "L2")
            l3x_vector(v)
            l3f_vector(v)

        @block.tensor
        def _(pe):
            pe.wait_ge(consts, NCONST)
            norm_tensor(pe, ln_l0x)
            l0x_tensor(pe)
            moe_tensor(pe, "L0")
            l1x_tensor(pe)
            moe_tensor(pe, "L1")
            l2x_tensor(pe)
            moe_tensor(pe, "L2")
            l3x_tensor(pe)
            l3f_tensor(pe)


def kernel(**inputs):
    import numpy as _np
    import ml_dtypes as _ml
    import concourse.bacc as _bacc
    from concourse import mybir as _mybir
    from concourse.bass_utils import run_bass_kernel_spmd as _run

    a = {k: _np.asarray(v) for k, v in inputs.items()}

    def width_first(w):
        return w.reshape(w.shape[0], DC, P).transpose(2, 1, 0)

    def expert_chunks(name, gate, up, down):
        n = moe_chunks(name)
        pad = _np.zeros((n * P - gate.shape[0], D), _np.float32)
        full = [_np.concatenate([w, pad]).reshape(n, P, D) for w in (gate, up, down)]
        lhs = [w.reshape(n, P, DC, P).transpose(0, 3, 2, 1).reshape(n, P, DC * P) for w in full[:2]]
        return _np.concatenate([*lhs, full[2]], axis=2)

    def expert_rows(name):
        experts, hidden, shared = MOE[name]
        rows = _np.arange(moe_chunks(name) * P)
        which = _np.where(rows < experts * hidden, rows // hidden, experts)
        one = which[None, :] == _np.arange(experts + (shared > 0))[:, None]
        return _np.concatenate([one] * 3).astype(_ml.bfloat16)

    e0, h0, _ = MOE["L0"]
    e1, h1, s1 = MOE["L1"]
    e2, h2, _ = MOE["L2"]
    ctx = a["ctx_2048"]
    data = {
        "x": a["x"],
        "ctx": ctx,
        "ctx_T": ctx.reshape(B, M, DC, P).transpose(0, 3, 2, 1),
        "mask": a["mask_BxS2_bk0"],
        "L0_w": expert_chunks("L0", a["L0_ffn_w_gate_proj"].reshape(e0 * h0, D),
                              a["L0_ffn_w_up_proj"].reshape(e0 * h0, D),
                              a["L0_ffn_w_down_proj"].transpose(0, 2, 1).reshape(e0 * h0, D)),
        "L0_router": width_first(a["L0_ffn_gate_w"]),
        "L0_rows": expert_rows("L0"),
        "decay": a["L1_xattn_decay"].reshape(1, 1),
        "L1_in": width_first(a["L1_xattn_W_in"]),
        "L1_out": width_first(a["L1_xattn_W_out"]),
        "L1_bin": a["L1_xattn_b_in"].reshape(DC, P).T,
        "L1_bout": a["L1_xattn_b_out"].reshape(DC, P).T,
        "L1_gamma": a["L1_xattn_gamma"].reshape(1, D),
        "L1_beta": a["L1_xattn_beta"].reshape(1, D),
        "L1_w": expert_chunks("L1",
                              _np.concatenate([a["L1_ffn_W1"].transpose(0, 2, 1).reshape(e1 * h1, D), a["L1_ffn_sw1"]]),
                              _np.concatenate([a["L1_ffn_W3"].transpose(0, 2, 1).reshape(e1 * h1, D), a["L1_ffn_sw3"]]),
                              _np.concatenate([a["L1_ffn_W2"].reshape(e1 * h1, D), a["L1_ffn_sw2"].T])),
        "L1_router": width_first(a["L1_ffn_gate_w"]),
        "L1_rbias": a["L1_ffn_router_bias"].reshape(1, e1),
        "L1_rows": expert_rows("L1"),
        "L2_w": expert_chunks("L2", a["L2_ffn_Wg"].transpose(0, 2, 1).reshape(e2 * h2, D),
                              a["L2_ffn_Wu"].transpose(0, 2, 1).reshape(e2 * h2, D),
                              a["L2_ffn_Wd"].reshape(e2 * h2, D)),
        "L2_router": width_first(a["L2_ffn_Wr"].T),
        "L2_rbias": a["L2_ffn_br"].reshape(1, e2),
        "L2_rows": expert_rows("L2"),
    }
    def rope(fn):
        freq = 1.0 / _np.float32(10000.0) ** (_np.arange(0, HD, 2, dtype=_np.float32) / _np.float32(HD))
        angle = _np.outer(_np.arange(S, dtype=_np.float32), freq.astype(_np.float32)).astype(_np.float32)
        return fn(angle).astype(_np.float32).reshape(TB, P, HD // 2).transpose(1, 0, 2)

    def by_head(w, heads):
        return w.reshape(DC, P, KH, heads * HD).transpose(2, 1, 0, 3)

    data.update({
        "rope_cos": rope(_np.cos), "rope_sin": rope(_np.sin),
        "L2_qw": a["L2_xattn_q_norm_w"].reshape(1, HD), "L2_kw": a["L2_xattn_k_norm_w"].reshape(1, HD),
        "L2_kwc": a["L2_xattn_k_norm_w"].reshape(HD, 1),
        "L2_w_qkv": _np.concatenate([by_head(a[f"L2_xattn_{n}"], 1) for n in ("wk_ctx", "wv_ctx", "wk", "wv")]
                                    + [by_head(a["L2_xattn_wq"], REP)], axis=3),
        "L2_wo": a["L2_xattn_wo"].reshape(QH, HD, D).transpose(1, 0, 2),
    })
    wkv3 = _np.concatenate([a["L3_xattn_Wk"], a["L3_xattn_Wv"]])
    data.update({
        "L3_kv": width_first(_np.concatenate([wkv3[0::2], wkv3[1::2]])),
        "L3_q": width_first(a["L3_xattn_Wq"]),
        "ctx_tiles": _np.concatenate([ctx, _np.zeros((B, MC * P - M, D), _np.float32)], axis=1)
        .reshape(B, MC, P, DC, P).transpose(0, 1, 4, 3, 2),
        "L3_gate": width_first(a["L3_ffn_w_gate"]),
        "L3_up": width_first(a["L3_ffn_w_up"]),
        "L3_down": a["L3_ffn_w_down"].T.reshape(FF3 // P, P, D).transpose(1, 0, 2),
    })
    nc = _bacc.Bacc("TRN2", target_bir_lowering=False, num_devices=1)
    arrays, args = {}, {}
    for name, value in data.items():
        value = _np.ascontiguousarray(value)
        arrays[f"in_{name}_dram"] = value
        kind = _mybir.dt.uint8 if value.dtype == bool else _mybir.dt.from_np(value.dtype)
        args[name] = nc.dram_tensor(f"in_{name}_dram", value.shape, kind,
                                    kind="ExternalInput").ap()
    out = nc.dram_tensor("out_0_dram", (B, S, D), _mybir.dt.float32, kind="ExternalOutput").ap()
    program(nc, args, out)
    r = _run(nc, [arrays], core_ids=[0])
    return r.results[0]["out_0_dram"]
```
